# Optimizing a Trainium2 kernel written in Bass

```python
import numpy as np
import jax
import jax.numpy as jnp

def _softmax(x, axis=-1):
    return jax.nn.softmax(x, axis=axis)

def _gelu(x):
    return jax.nn.gelu(x, approximate=True)

def _silu(x):
    return jax.nn.silu(x)

def _sigmoid(x):
    return jax.nn.sigmoid(x)

def _layernorm(x, axis=-1, eps=1e-05):
    m = jnp.mean(x, axis=axis, keepdims=True)
    v = jnp.var(x, axis=axis, keepdims=True)
    return (x - m) / jnp.sqrt(v + eps)

def _scatter_add(tgt, idx, src, axis=0):
    return tgt.at[idx].add(src)

def _segment_sum(src, seg, n):
    return jax.ops.segment_sum(src, seg, n)
kernel_name = 'mk_cond_seq_d2_seqx_r4_fa4fac'

def setup_inputs(seed: int=0):
    np.random.seed(seed)
    _w = jnp.asarray

    def _rec_inputs():
        import jax
        import jax.numpy as jnp
        _rk = jax.random.key(seed)
        x = 7.22e-05 + 1 * jax.random.normal(jax.random.fold_in(_rk, 1), (8, 512, 256), jnp.float32)
        _lenS = 512 - jax.random.randint(jax.random.fold_in(_rk, 7), (8,), 0, max(1, 512 // 4) + 1, jnp.int32)
        _lenS2 = 512 - jax.random.randint(jax.random.fold_in(_rk, 8), (8,), 0, max(1, 512 // 4) + 1, jnp.int32)
        cond_256 = -0.0209273 + 1.04763 * jax.random.normal(jax.random.fold_in(_rk, 11), (8, 64), jnp.float32)
        return (x, cond_256)
    x, cond_256 = _rec_inputs()

    def _L0_cond_setup():
        import jax, jax.numpy as jnp
        import numpy as np
        from math import sqrt
        D_MODEL = 256
        N_HEADS = 16
        D_T = 64
        D_HID = 4 * D_MODEL
        EPS = 1e-06

        def _rmsnorm(x):
            return x * jax.lax.rsqrt(jnp.mean(x * x, axis=-1, keepdims=True) + EPS)

        def _ada_rmsnorm(x, t, gamma_w, beta_w):
            gamma = (t @ gamma_w.T)[:, None, :]
            beta = (t @ beta_w.T)[:, None, :]
            return gamma * _rmsnorm(x) + beta

        def _attention(x, W_q, W_k, W_v, W_o):
            b, l, dm = x.shape
            d_head = dm // N_HEADS
            scale = sqrt(N_HEADS / dm)

            def split(y):
                return y.reshape(b, l, N_HEADS, d_head).transpose(0, 2, 1, 3)
            q = split(x @ W_q.T)
            k = split(x @ W_k.T)
            v = split(x @ W_v.T)
            attn = jax.nn.softmax(scale * jnp.einsum('bnqd,bnkd->bnqk', q, k), axis=-1)
            o = jnp.einsum('bnqk,bnkd->bnqd', attn, v)
            o = o.transpose(0, 2, 1, 3).reshape(b, l, dm)
            return o @ W_o.T

        def _swiglu(x, gate_w, hidden_w, out_w, out_b):
            return jax.nn.silu(x @ gate_w.T) * (x @ hidden_w.T) @ out_w.T + out_b
        key = jax.random.key(seed)
        ks = jax.random.split(key, 16)
        s = 0.02
        inp = {'x': jax.random.normal(ks[0], (4, 512, D_MODEL), dtype=jnp.float32), 't': jax.random.normal(ks[1], (4, D_T), dtype=jnp.float32), 'attn_gamma_w': jax.random.normal(ks[2], (D_MODEL, D_T), dtype=jnp.float32) * s, 'attn_beta_w': jax.random.normal(ks[3], (D_MODEL, D_T), dtype=jnp.float32) * s, 'W_q': jax.random.normal(ks[4], (D_MODEL, D_MODEL), dtype=jnp.float32) * s, 'W_k': jax.random.normal(ks[5], (D_MODEL, D_MODEL), dtype=jnp.float32) * s, 'W_v': jax.random.normal(ks[6], (D_MODEL, D_MODEL), dtype=jnp.float32) * s, 'W_o': jax.random.normal(ks[7], (D_MODEL, D_MODEL), dtype=jnp.float32) * s, 'attn_alpha_w': jax.random.normal(ks[8], (D_MODEL, D_T), dtype=jnp.float32) * s, 'ffn_gamma_w': jax.random.normal(ks[9], (D_MODEL, D_T), dtype=jnp.float32) * s, 'ffn_beta_w': jax.random.normal(ks[10], (D_MODEL, D_T), dtype=jnp.float32) * s, 'gate_w': jax.random.normal(ks[11], (D_HID, D_MODEL), dtype=jnp.float32) * s, 'hidden_w': jax.random.normal(ks[12], (D_HID, D_MODEL), dtype=jnp.float32) * s, 'out_w': jax.random.normal(ks[13], (D_MODEL, D_HID), dtype=jnp.float32) * s, 'out_b': jnp.zeros((D_MODEL,), dtype=jnp.float32), 'ffn_alpha_w': jax.random.normal(ks[14], (D_MODEL, D_T), dtype=jnp.float32) * s}
        return inp
    _L0_cond_all = _L0_cond_setup()
    _L0_cond_in = {k: v for k, v in _L0_cond_all.items() if k in ('attn_gamma_w', 'attn_beta_w', 'W_q', 'W_k', 'W_v', 'W_o', 'attn_alpha_w', 'ffn_gamma_w', 'ffn_beta_w', 'gate_w', 'hidden_w', 'out_w', 'out_b', 'ffn_alpha_w')}
    del _L0_cond_all

    def _L1_cond_setup():
        import jax, jax.numpy as jnp
        import numpy as np
        EPS = 1e-05
        key = jax.random.key(seed)
        k1, k2, k3, k4 = jax.random.split(key, 4)
        b, t, d, num_con = (8, 1024, 256, 64)
        return {'input': jax.random.normal(k1, (b, t, d), dtype=jnp.float32), 'convInfo': jax.random.normal(k2, (b, num_con), dtype=jnp.float32), 'weight': jnp.ones((d,), dtype=jnp.float32), 'bias': jnp.zeros((d,), dtype=jnp.float32), 'lin_w': jax.random.normal(k3, (d, num_con), dtype=jnp.float32) * (1.0 / np.sqrt(num_con)), 'lin_b': jax.random.normal(k4, (d,), dtype=jnp.float32) * 0.01}
    _L1_cond_all = _L1_cond_setup()
    _L1_cond_in = {k: v for k, v in _L1_cond_all.items() if k in ('weight', 'bias', 'lin_w', 'lin_b')}
    del _L1_cond_all
    return {'x': x, 'cond_256': cond_256, 'L0_cond_attn_gamma_w': _L0_cond_in['attn_gamma_w'], 'L0_cond_attn_beta_w': _L0_cond_in['attn_beta_w'], 'L0_cond_W_q': _L0_cond_in['W_q'], 'L0_cond_W_k': _L0_cond_in['W_k'], 'L0_cond_W_v': _L0_cond_in['W_v'], 'L0_cond_W_o': _L0_cond_in['W_o'], 'L0_cond_attn_alpha_w': _L0_cond_in['attn_alpha_w'], 'L0_cond_ffn_gamma_w': _L0_cond_in['ffn_gamma_w'], 'L0_cond_ffn_beta_w': _L0_cond_in['ffn_beta_w'], 'L0_cond_gate_w': _L0_cond_in['gate_w'], 'L0_cond_hidden_w': _L0_cond_in['hidden_w'], 'L0_cond_out_w': _L0_cond_in['out_w'], 'L0_cond_out_b': _L0_cond_in['out_b'], 'L0_cond_ffn_alpha_w': _L0_cond_in['ffn_alpha_w'], 'L1_cond_weight': _L1_cond_in['weight'], 'L1_cond_bias': _L1_cond_in['bias'], 'L1_cond_lin_w': _L1_cond_in['lin_w'], 'L1_cond_lin_b': _L1_cond_in['lin_b']}

def reference(x, cond_256, L0_cond_attn_gamma_w, L0_cond_attn_beta_w, L0_cond_W_q, L0_cond_W_k, L0_cond_W_v, L0_cond_W_o, L0_cond_attn_alpha_w, L0_cond_ffn_gamma_w, L0_cond_ffn_beta_w, L0_cond_gate_w, L0_cond_hidden_w, L0_cond_out_w, L0_cond_out_b, L0_cond_ffn_alpha_w, L1_cond_weight, L1_cond_bias, L1_cond_lin_w, L1_cond_lin_b):
    import jax
    import jax.numpy as jnp

    def _L0_cond_ref(x, t, attn_gamma_w, attn_beta_w, W_q, W_k, W_v, W_o, attn_alpha_w, ffn_gamma_w, ffn_beta_w, gate_w, hidden_w, out_w, out_b, ffn_alpha_w):
        import jax, jax.numpy as jnp
        import numpy as np
        from math import sqrt
        D_MODEL = 256
        N_HEADS = 16
        D_T = 64
        D_HID = 4 * D_MODEL
        EPS = 1e-06

        def _rmsnorm(x):
            return x * jax.lax.rsqrt(jnp.mean(x * x, axis=-1, keepdims=True) + EPS)

        def _ada_rmsnorm(x, t, gamma_w, beta_w):
            gamma = (t @ gamma_w.T)[:, None, :]
            beta = (t @ beta_w.T)[:, None, :]
            return gamma * _rmsnorm(x) + beta

        def _attention(x, W_q, W_k, W_v, W_o):
            b, l, dm = x.shape
            d_head = dm // N_HEADS
            scale = sqrt(N_HEADS / dm)

            def split(y):
                return y.reshape(b, l, N_HEADS, d_head).transpose(0, 2, 1, 3)
            q = split(x @ W_q.T)
            k = split(x @ W_k.T)
            v = split(x @ W_v.T)
            attn = jax.nn.softmax(scale * jnp.einsum('bnqd,bnkd->bnqk', q, k), axis=-1)
            o = jnp.einsum('bnqk,bnkd->bnqd', attn, v)
            o = o.transpose(0, 2, 1, 3).reshape(b, l, dm)
            return o @ W_o.T

        def _swiglu(x, gate_w, hidden_w, out_w, out_b):
            return jax.nn.silu(x @ gate_w.T) * (x @ hidden_w.T) @ out_w.T + out_b
        a_alpha = (t @ attn_alpha_w.T)[:, None, :]
        x = x + a_alpha * _attention(_ada_rmsnorm(x, t, attn_gamma_w, attn_beta_w), W_q, W_k, W_v, W_o)
        f_alpha = (t @ ffn_alpha_w.T)[:, None, :]
        return x + f_alpha * _swiglu(_ada_rmsnorm(x, t, ffn_gamma_w, ffn_beta_w), gate_w, hidden_w, out_w, out_b)

    def _L1_cond_ref(input, convInfo, weight, bias, lin_w, lin_b):
        import jax, jax.numpy as jnp
        import numpy as np
        EPS = 1e-05
        mean = jnp.mean(input, axis=-1, keepdims=True)
        var = jnp.mean(jnp.square(input - mean), axis=-1, keepdims=True)
        out = (input - mean) * jax.lax.rsqrt(var + EPS) * weight + bias
        tar_bias = jnp.tanh(convInfo @ lin_w.T + lin_b)[:, None, :]
        out = out + tar_bias
        return out * weight + bias
    x = _L0_cond_ref(x, cond_256, L0_cond_attn_gamma_w, L0_cond_attn_beta_w, L0_cond_W_q, L0_cond_W_k, L0_cond_W_v, L0_cond_W_o, L0_cond_attn_alpha_w, L0_cond_ffn_gamma_w, L0_cond_ffn_beta_w, L0_cond_gate_w, L0_cond_hidden_w, L0_cond_out_w, L0_cond_out_b, L0_cond_ffn_alpha_w)
    x = _L1_cond_ref(x, cond_256, L1_cond_weight, L1_cond_bias, L1_cond_lin_w, L1_cond_lin_b)
    return x

_drawn_inputs = setup_inputs


def setup_inputs(seed=0):
    import zlib

    import numpy as np

    out = dict(_drawn_inputs(seed))
    spreads = {'L0_cond_out_b': (0.0, 0.581), 'L1_cond_weight': (1.0, 0.2), 'L1_cond_bias': (0.0, 0.1)}
    factors = {'L0_cond_attn_gamma_w': 8.0,
     'L0_cond_attn_beta_w': 8.0,
     'L0_cond_W_q': 8.0,
     'L0_cond_W_k': 8.0,
     'L0_cond_W_v': 8.0,
     'L0_cond_W_o': 8.0,
     'L0_cond_attn_alpha_w': 8.0,
     'L0_cond_ffn_gamma_w': 8.0,
     'L0_cond_ffn_beta_w': 8.0,
     'L0_cond_gate_w': 8.0,
     'L0_cond_hidden_w': 8.0,
     'L0_cond_out_w': 8.0,
     'L0_cond_ffn_alpha_w': 3.829,
     'L1_cond_lin_b': 8.0}
    for name, (base, spread) in spreads.items():
        noise = np.random.default_rng([zlib.crc32(name.encode()), seed]).standard_normal(out[name].shape)
        drawn = base * np.exp(spread * noise) if base else spread * noise
        out[name] = jnp.asarray(drawn.astype(out[name].dtype))
    for name, factor in factors.items():
        out[name] = (out[name] * factor).astype(out[name].dtype)
    return out
```

```python
from contextlib import ExitStack

import concourse.bass as bass
from concourse import mybir

F32 = mybir.dt.float32
F32R = mybir.dt.float32r
ALU = mybir.AluOpType
ACT = mybir.ActivationFunctionType
AX = mybir.AxisListType

P = 128
B = 8
T = 512
D = 256
KC = D // P
TT = T // P
NH = 16
DH = D // NH
HG = 4
NG = NH // HG
DT = 64
HID = 4 * D
JC = HID // P
EPS_RMS = 1e-6
EPS_LN = 1e-5
SCALE = (NH / D) ** 0.5
UNITS = NG * TT
TAB = 3

PRO = ["COEF", "TR0", "TR1", "Q0", "K0", "Q1", "K1", "V0", "V1", "MT0"]
MID = {0: "MT1", 1: "TR0", 2: "TR1", 3: "Q0", 4: "K0", 5: "MT2", 6: "V0", 7: "V1", 8: "WO0", 9: "MT3",
       10: "WO1", 11: "Q1", 12: "K1", 13: "MT0"}
OWN = ("MT1", "MT2", "MT3")
PREV = ("WO0", "WO1")


def jobs_of(first, last):
    return {u: o for u, o in MID.items() if (o not in PREV or not first) and (o in OWN + PREV or not last)}


N_FIRST = len(jobs_of(True, False))
N_MID = len(jobs_of(False, False))


def job_base(b, first):
    return len(PRO) if first else len(PRO) + N_FIRST - N_MID + N_MID * b


def job_no(b, first, last, op):
    return job_base(b, first) + list(jobs_of(first, last).values()).index(op)


def attention_phase(nc, dram, tensors):
    x_all, tab, coef, ident, ss2 = (tensors[k] for k in ("x_all", "tab", "coef", "ident", "ss2"))
    with ExitStack() as ctx:
        def sb(name, shape, dt=F32):
            return ctx.enter_context(nc.sbuf_tensor(name, shape, dt))

        def sem(name):
            return ctx.enter_context(nc.semaphore(name))

        cond = sb("cond", [DT + 1, B])
        cond_rep = sb("cond_rep", [DT + 1, B, P])
        wb_rows = sb("wb_rows", [P, 2, D])
        w_hi = sb("w_hi", [P, KC, 4, D], F32R)
        w_lo = sb("w_lo", [P, KC, 4, D], F32R)
        ss1 = sb("ss1", [P, B * TT])
        rstd1 = sb("rstd1", [P, B * TT])
        junk = sb("junk", [P, D])
        xhat = sb("xhat", [P, TT, D])
        y_n = sb("y_n", [P, KC, T])
        n_hi = sb("n_hi", [P, KC, T], F32R)
        n_lo = sb("n_lo", [P, KC, T], F32R)
        qk_hi = sb("qk_hi", [P, 4, T], F32R)
        qk_lo = sb("qk_lo", [P, 4, T], F32R)
        qs = sb("qs", [P, NG, 2, T], F32R)
        ks = sb("ks", [P, NG, 2, T], F32R)
        v_st = sb("v_st", [P, NG, TT, HG, 32])
        v = sb("v", [P, NG, TT, HG, 32])
        mx = sb("mx", [P, 2, 2, 2, TT])
        m_hl = sb("m_hl", [2 * HG * 2, 2, P], F32R)
        prob = sb("prob", [P, 2, HG, T])
        flat = prob[:].rearrange("p u h n -> p u (h n)")
        w_raw = flat[:, 0].rearrange("p (k i n) -> p k i n", k=KC, n=D)
        ada_w = flat[0:DT + 1, 1, 0:7 * D].rearrange("p (i n) -> p i n", n=D)
        o_raw = sb("o_raw", [P, 2, T])
        o_c = sb("o_c", [P, 2, T])
        d_c = sb("d_c", [P, 2, T])
        on_hi = sb("on_hi", [P, 2, T], F32R)
        on_lo = sb("on_lo", [P, 2, T], F32R)
        wo_t = sb("wo_t", [P, 2, 2, D])
        ps_s = ctx.enter_context(nc.psum_tensor("ps_s", [P, HG, T], F32))
        ps_m = ctx.enter_context(nc.psum_tensor("ps_m", [P, 2, T], F32))
        ps_o = ctx.enter_context(nc.psum_tensor("ps_o", [P, T], F32))
        ps_j = ctx.enter_context(nc.psum_tensor("ps_j", [P, T], F32))
        stack_d = nc.dram_tensor("stack_scratch", (2, 2, HG, P * T), F32, kind="Internal").ap()
        o_d = nc.dram_tensor("out_scratch", (2, 2, P, T), F32, kind="Internal").ap()
        m_d = nc.dram_tensor("max_scratch", (2, 2, 2 * TT * P), F32, kind="Internal").ap()

        x0_in = sem("x0_in"); x_in = sem("x_in"); small_in = sem("small_in"); w_in = sem("w_in"); tab_in = sem("tab_in")
        consts = sem("consts"); rep_ready = sem("rep_ready"); pad_written = sem("pad_written")
        w_hi_r = sem("w_hi_r"); w_lo_r = sem("w_lo_r")
        sq1 = sem("sq1"); ms1 = sem("ms1"); root1 = sem("root1"); rstd_r = sem("rstd_r")
        coef_r = sem("coef_r"); tab_full = sem("tab_full"); tab_r = sem("tab_r"); shift_r = sem("shift_r")
        xhat_r = sem("xhat_r"); y_r = sem("y_r"); n_r = sem("n_r")
        qk_hi_r = sem("qk_hi_r"); qk_lo_r = sem("qk_lo_r"); v_r = sem("v_r")
        scr_w = sem("scr_w"); stack_in = sem("stack_in"); v_in = sem("v_in")
        mx_full = sem("mx_full"); mx_red = sem("mx_red"); m_r = sem("m_r"); m_w = sem("m_w"); m_in = sem("m_in")
        s_full = sem("s_full"); p_r = sem("p_r"); av_done = sem("av_done")
        o_r = sem("o_r"); oc_in = sem("oc_in"); on_r = sem("on_r"); x1_r = sem("x1_r"); sq2 = sem("sq2")
        job_full = sem("job_full"); job_free = sem("job_free"); sp_waited = sem("sp_waited")
        ow_w = sem("ow_w"); x1_begun = sem("x1_begun")

        block = ctx.enter_context(nc.Block())

        @block.sync
        def _(sp):
            sp.dma_start(x_all[:, 0], dram["x"][0]).then_inc(x0_in, 16)
            sp.dma_start(cond[0:DT, :], dram["cond"]).then_inc(small_in, 16)
            for i, name in enumerate(("gamma1", "beta1", "gamma2", "beta2", "alpha1", "alpha2", "lin_w")):
                sp.dma_start(ada_w[0:DT, i, :], dram[name]).then_inc(small_in, 16)
            sp.dma_start(ada_w[DT:DT + 1, 6, :], dram["lin_b"].rearrange("(a n) -> a n", a=1)).then_inc(small_in, 16)
            for i, name in enumerate(("wq", "wk", "wv", "wo")):
                sp.dma_start(w_raw[:, :, i, :], dram[name].rearrange("(k p) n -> p k n", p=P)).then_inc(w_in, 16)
            for b in range(1, B):
                sp.dma_start(x_all[:, b], dram["x"][b]).then_inc(x_in, 16)
            for i, name in enumerate(("l1_w", "l1_b")):
                sp.dma_start(wb_rows[:, i, :], dram[name].partition_broadcast(P)).then_inc(tab_in, 16)
            sp.wait_ge(consts, 5)
            for c in range(2):
                for i, pad in enumerate((xhat[:, 0:2, :], y_n[:, 0, :])):
                    rows = stack_d[i, c].rearrange("j (r t n) -> (j r) t n", t=4, n=T)
                    sp.dma_start(rows[:, 3, :], pad).then_inc(pad_written, 16)
            sp.wait_ge(pad_written, 64)

            def wait(semaphore, value):
                sp.wait_ge(semaphore, value)
                sp.sem_inc(sp_waited, 1)

            def stack_write(nb, c):
                wait(qk_hi_r, 4 * nb + 2 * c + 2)
                wait(qk_lo_r, 4 * nb + 2 * c + 2)
                for i, terms in enumerate(((qk_hi, qk_lo, qk_hi), (qk_hi, qk_hi, qk_lo))):
                    rows = stack_d[i, c].rearrange("j (r t n) -> (j r) t n", t=4, n=T)
                    for t, src in enumerate(terms):
                        sp.dma_start(rows[:, t, :], src[:, 2 * c + i, :].bitcast(F32)).then_inc(scr_w, 16)
                wait(scr_w, 96 * (2 * nb + c + 1))

            def stack_read(nb, g, reuse):
                if reuse:
                    wait(av_done, UNITS * (nb - 1) + TT * (g + 1))
                for i, dst in enumerate((qs, ks)):
                    src = stack_d[i, g // 2, 2 * (g % 2):2 * (g % 2) + 2].rearrange("j (r n) -> r j n", n=T)
                    sp.dma_start(dst[:, g].bitcast(F32), src).then_inc(stack_in, 16)

            def v_copy(nb, g):
                wait(v_r, TT * (nb + 1))
                sp.dma_start(v[:, g], v_st[:, g]).then_inc(v_in, 16)

            def max_rows(b, g):
                n = NG * b + g
                wait(m_r, 2 * (n + 1))
                sp.dma_start(m_d.rearrange("l s (c n) -> (s c) l n", n=P), m_hl[:].bitcast(F32)).then_inc(m_w, 16)
                wait(m_w, 16 * (n + 1))
                for s in range(2):
                    for hl in range(2):
                        r = 64 * s + 4 * hl + 3
                        sp.dma_start(qs[r:r + 1, g].rearrange("p j n -> p (j n)").bitcast(F32), m_d[hl, s:s + 1, :])\
                          .then_inc(m_in, 16)
                wait(m_in, 64 * (n + 1))

            for c in range(2):
                stack_write(0, c)
                for g in (2 * c, 2 * c + 1):
                    stack_read(0, g, False)
                    wait(stack_in, 32 * (g + 1))
            for g in range(NG - 1):
                v_copy(0, g)
                wait(v_in, 16 * (g + 1))
            max_rows(0, 0)

            def batch(b, first, last):
                nb = b + 1
                if first:
                    v_copy(b, 3)
                    wait(v_in, 64)
                else:
                    stack_read(b, 3, True)
                    v_copy(b, 3)
                    wait(stack_in, 128 * (b + 1))
                    wait(v_in, 64 * (b + 1))
                max_rows(b, 1)
                if last:
                    max_rows(b, 2)
                    max_rows(b, 3)
                    return
                stack_write(nb, 0)
                stack_read(nb, 0, True)
                wait(stack_in, 32 * (NG * nb + 1))
                max_rows(b, 2)
                v_copy(nb, 0)
                wait(v_in, 16 * (NG * nb + 1))
                stack_read(nb, 1, True)
                v_copy(nb, 1)
                wait(stack_in, 32 * (NG * nb + 2))
                wait(v_in, 16 * (NG * nb + 2))
                max_rows(b, 3)
                stack_write(nb, 1)
                stack_read(nb, 2, True)
                v_copy(nb, 2)
                wait(stack_in, 32 * (NG * nb + 3))
                wait(v_in, 16 * (NG * nb + 3))
                max_rows(nb, 0)

            batch(0, True, False)
            with sp.Fori(1, B - 1) as b:
                batch(b, False, False)
            batch(B - 1, False, True)

        @block.gpsimd
        def _(pool):
            for n, (ap, value) in enumerate(((ident[:], 0.0), (cond[DT:DT + 1, :], 1.0), (xhat[:, 0:2, :], 0.0),
                                             (y_n[:, 0, :], 1.0), (v_st[:, :, :, :, DH:32], 1.0))):
                pool.memset(ap, value).then_inc(consts, 1)
                pool.wait_ge(consts, n + 1)
            pool.affine_select(out=ident[:], in_=ident[:], compare_op=ALU.not_equal, fill=1.0, base=0,
                               pattern=[[-1, P]], channel_multiplier=1).then_inc(consts, 1)

            def update_x(b, first_no):
                for w in range(2):
                    pool.wait_ge(job_free, first_no[w] + 1)
                    pool.sem_inc(x1_begun, 1)
                    xs = x_all[:, bass.ds(b, 1), 2 * w:2 * w + 2, :].rearrange("p a t n -> p (a t) n")
                    pool.tensor_tensor(xs, xs, wo_t[:, w], ALU.add).then_inc(x1_r, 1)

            with pool.Fori(1, B - 1) as b:
                update_x(b - 1, [job_no(b, False, False, o) for o in PREV])
            update_x(B - 2, [job_no(B - 1, False, True, o) for o in PREV])
            end = job_no(B - 1, False, True, "WO1") + 1
            update_x(B - 1, [end, end + 1])

        @block.scalar
        def _(act):
            for t in range(TT):
                if t == 0:
                    act.wait_ge(x0_in, 16)
                else:
                    act.wait_ge(sq1, t)
                nc.scalar.activation(junk[:], x_all[:, 0, t, :], ACT.Square, scale=1.0 / DH,
                                     accum_out=ss1[:, t:t + 1]).then_inc(sq1, 1)
            act.wait_ge(ms1, 1)
            nc.scalar.activation(ss1[:, 0:TT], ss1[:, 0:TT], ACT.Sqrt).then_inc(root1, 1)

            act.wait_ge(w_in, 64)
            nc.scalar.activation(w_hi[:], w_raw, ACT.Copy).then_inc(w_hi_r, 1)
            act.wait_ge(job_full, 1)
            nc.scalar.activation(coef[:], ps_j[:, 0:4 * KC * B], ACT.Copy).then_inc(job_free, 1)

            def y_copy(nb, k, no, reuse):
                act.wait_ge(job_full, no + 1)
                if reuse:
                    act.wait_ge(n_r, 4 * nb)
                cf = coef[:, :, k:k + 1, bass.ds(nb, 1)].rearrange("p i k b -> p i (k b)")
                act.activation(y_n[:, k, :], ps_j[:], ACT.Identity, scale=cf[:, 0], bias=cf[:, 1])\
                   .then_inc(job_free, 1)

            def qk_copy(nb, i, no, reuse):
                act.wait_ge(job_full, no + 1)
                if reuse:
                    act.wait_ge(scr_w, 96 * (2 * (nb - 1) + i // 2 + 1))
                act.activation(qk_hi[:, i, :], ps_j[:], ACT.Copy).then_inc(qk_hi_r, 1)

            def v_evac(nb, w, no, reuse):
                act.wait_ge(job_full, no + 1)
                if reuse:
                    act.wait_ge(v_in, 64 * nb)
                for t in (2 * w, 2 * w + 1):
                    src = ps_j[:, D * (t % 2):D * (t % 2) + D].rearrange("p (g i d) -> p g i d", g=NG, i=HG)
                    act.activation(v_st[:, :, t, :, 0:DH], src, ACT.Copy).then_inc(v_r, 1)
                act.wait_ge(v_r, TT * nb + 2 * w + 2)
                act.sem_inc(job_free, 1)

            def exps(b, u, warm):
                n = UNITS * b + u
                for h in range(2):
                    act.wait_ge(s_full, 2 * n + h + 1)
                    if warm:
                        act.wait_ge(av_done, n - 1)
                    act.activation(prob[:, u % 2, 2 * h:2 * h + 2, :], ps_s[:, 2 * h:2 * h + 2, :], ACT.Exp,
                                   scale=SCALE).then_inc(p_r, 1)

            def o_evac(b, g, reuse):
                n = NG * b + g
                act.wait_ge(av_done, TT * (n + 1))
                if reuse:
                    act.wait_ge(ow_w, 16 * (n - 1))
                act.activation(o_raw[:, g % 2, :], ps_o[:], ACT.Copy).then_inc(o_r, 1)

            def o_write(b, g):
                act.wait_ge(o_r, NG * b + g + 1)
                act.dma_start(o_d[g // 2, g % 2], o_raw[:, g % 2, :]).then_inc(ow_w, 16)

            def o_read(b, c, fresh):
                act.wait_ge(ow_w, 16 * (NG * b + 2 * c + 2))
                if not fresh:
                    act.wait_ge(on_r, 8 * b + 4 * c)
                rows = o_d[c].rearrange("g (i k d) n -> k (g i) d n", i=HG, k=2)
                for k, dst in enumerate((o_c, d_c)):
                    act.dma_start(dst[:, c, :], rows[k]).then_inc(oc_in, 16)

            def squares2(b):
                for t in range(TT):
                    act.wait_ge(x1_r, 2 * b + 1 + t // 2)
                    if t > 0:
                        act.wait_ge(sq2, TT * b + t)
                    col = ss2[:, bass.ds(b, 1), t:t + 1].rearrange("p a b -> p (a b)")
                    act.activation(junk[:], x_all[:, bass.ds(b, 1), t, :].rearrange("p a n -> p (a n)"), ACT.Square,
                                   scale=1.0 / DH, accum_out=col).then_inc(sq2, 1)

            def job(nb, op, no, reuse):
                if op in ("TR0", "TR1"):
                    y_copy(nb, int(op[2]), no, reuse)
                elif op[0] in "QK":
                    qk_copy(nb, 2 * int(op[1]) + "QK".index(op[0]), no, reuse)
                elif op[0] == "V":
                    v_evac(nb, int(op[1]), no, reuse)

            for no, op in enumerate(PRO):
                job(0, op, no, False)
            for k in range(TAB):
                for q in range(B // 2):
                    n = (B // 2) * k + q
                    act.wait_ge(tab_full, n + 1)
                    act.activation(tab[:, k, 2 * q:2 * q + 2, :], ps_s[:, n % HG, :],
                                   ACT.Tanh if k == 2 else ACT.Copy).then_inc(tab_r, 1)
            act.wait_ge(x_in, 16 * (B - 1))
            for n in range(TT, B * TT):
                act.wait_ge(sq1, n)
                act.activation(junk[:], x_all[:, n // TT, n % TT, :], ACT.Square, scale=1.0 / DH,
                               accum_out=ss1[:, n:n + 1]).then_inc(sq1, 1)
            act.wait_ge(ms1, 2)
            act.activation(ss1[:, TT:], ss1[:, TT:], ACT.Sqrt).then_inc(root1, 1)

            def batch(b, first, last):
                jobs = jobs_of(first, last)
                for u in range(UNITS):
                    exps(b, u, not (first and u < 2))
                    if u in jobs:
                        job(b + 1, jobs[u], job_no(b, first, last, jobs[u]), True)
                    if u % TT == 0 and not (first and u == 0):
                        o_evac(b - (u == 0), (u // TT - 1) % NG, not (first and u < 12))
                    if u % TT == 1 and not (first and u == 1):
                        o_write(b - (u == 1), (u // TT - 1) % NG)
                    if u == 3 and not first:
                        o_read(b - 1, 1, False)
                    if u == 11:
                        o_read(b, 0, first)
                    if u == 13 and not first:
                        squares2(b - 1)

            batch(0, True, False)
            with act.Fori(1, B - 1) as b:
                batch(b, False, False)
            batch(B - 1, False, True)
            o_evac(B - 1, 3, True)
            o_write(B - 1, 3)
            o_read(B - 1, 1, False)
            squares2(B - 1)

        @block.vector
        def _(dve):
            dve.wait_ge(sq1, TT)
            dve.tensor_scalar(ss1[:, 0:TT], ss1[:, 0:TT], EPS_RMS, None, ALU.add).then_inc(ms1, 1)
            dve.wait_ge(root1, 1)
            dve.reciprocal(rstd1[:, 0:TT], ss1[:, 0:TT]).then_inc(rstd_r, 1)

            def norm(nb, reuse):
                if reuse:
                    dve.wait_ge(y_done[0], y_done[1])
                for t in range(TT):
                    xs = x_all[:, bass.ds(nb, 1), t, :].rearrange("p a n -> p (a n)")
                    dve.tensor_scalar(xhat[:, t, :], xs, rstd1[:, bass.ds(TT * nb + t, 1)], None, ALU.mult)\
                       .then_inc(xhat_r, 1)

            y_done = [None, None]
            dve.wait_ge(rstd_r, 1)
            dve.wait_ge(pad_written, 64)
            norm(0, False)
            dve.wait_ge(small_in, 16 * 9)
            dve.wait_ge(consts, 2)
            dve.tensor_copy(cond_rep[:], cond[:].unsqueeze(2).broadcast_to([DT + 1, B, P])).then_inc(rep_ready, 1)
            dve.wait_ge(w_hi_r, 1)
            dve.tensor_tensor(w_lo[:], w_raw, w_hi[:].bitcast(F32), ALU.subtract).then_inc(w_lo_r, 1)

            def split_n(nb, k, no, last_read):
                dve.wait_ge(job_free, no + 1)
                if last_read is not None:
                    dve.wait_ge(job_full, last_read + 1)
                dve.tensor_copy(n_hi[:, k, :], y_n[:, k, :]).then_inc(n_r, 1)
                dve.wait_ge(n_r, 4 * nb + 2 * k + 1)
                dve.tensor_tensor(n_lo[:, k, :], y_n[:, k, :], n_hi[:, k, :].bitcast(F32), ALU.subtract)\
                   .then_inc(n_r, 1)

            def qk_low(nb, i, no, reuse):
                dve.wait_ge(qk_hi_r, 4 * nb + i + 1)
                if reuse:
                    dve.wait_ge(scr_w, 96 * (2 * (nb - 1) + i // 2 + 1))
                dve.tensor_tensor(qk_lo[:, i, :], ps_j[:], qk_hi[:, i, :].bitcast(F32), ALU.subtract)\
                   .then_inc(qk_lo_r, 1)
                dve.wait_ge(qk_lo_r, 4 * nb + i + 1)
                dve.sem_inc(job_free, 1)

            def max_parts(b, g, no):
                n = NG * b + g
                src = ps_j[0:2 * HG * 2, 0:P]
                dve.wait_ge(job_full, no + 1)
                if not (isinstance(n, int) and n == 0):
                    dve.wait_ge(m_w, 16 * n)
                dve.tensor_scalar(m_hl[:, 0, :], src, -1.0, None, ALU.mult).then_inc(m_r, 1)
                dve.wait_ge(m_r, 2 * n + 1)
                dve.scalar_tensor_tensor(out=m_hl[:, 1, :], in0=src, scalar=-1.0, in1=m_hl[:, 0, :].bitcast(F32),
                                         op0=ALU.mult, op1=ALU.subtract).then_inc(m_r, 1)
                dve.wait_ge(m_r, 2 * n + 2)
                dve.sem_inc(job_free, 1)

            def wo_scale(b, w, no, reuse):
                dve.wait_ge(job_full, no + 1)
                if reuse:
                    dve.wait_ge(x1_r, 2 * (b - 1) + w + 1)
                al = tab[:, 0, bass.ds(b, 1), :].broadcast_to([P, 2, D])
                dve.tensor_tensor(wo_t[:, w], ps_j[:].rearrange("p (t n) -> p t n", t=2), al, ALU.mult)\
                   .then_inc(job_free, 1)

            def o_norm(b, c, last_read):
                n = 8 * b + 4 * c
                dve.wait_ge(oc_in, 32 * (2 * b + c + 1))
                dve.reciprocal(d_c[:, c, :], d_c[:, c, :]).then_inc(on_r, 1)
                dve.wait_ge(on_r, n + 1)
                dve.tensor_tensor(o_c[:, c, :], o_c[:, c, :], d_c[:, c, :], ALU.mult).then_inc(on_r, 1)
                dve.wait_ge(on_r, n + 2)
                if last_read is not None:
                    dve.wait_ge(job_full, last_read + 1)
                dve.tensor_copy(on_hi[:, c, :], o_c[:, c, :]).then_inc(on_r, 1)
                dve.wait_ge(on_r, n + 3)
                dve.tensor_tensor(on_lo[:, c, :], o_c[:, c, :], on_hi[:, c, :].bitcast(F32), ALU.subtract)\
                   .then_inc(on_r, 1)

            def reduce_max(b, g, qt, i, free):
                n = UNITS * HG // NG * (NG * b + g) + HG * qt + i
                dve.wait_ge(mx_full, n + 1)
                if free is not None:
                    dve.wait_ge(job_full, free + 1)
                dve.tensor_reduce(mx[:, g % 2, i % 2, i // 2, qt:qt + 1], ps_m[:, i % 2, :], AX.X, ALU.max)\
                   .then_inc(mx_red, 1)

            for k in range(2):
                split_n(0, k, PRO.index(f"TR{k}"), None)
            for i, op in enumerate(("Q0", "K0", "Q1", "K1")):
                qk_low(0, i, PRO.index(op), False)
            dve.wait_ge(sq1, B * TT)
            dve.tensor_scalar(ss1[:, TT:], ss1[:, TT:], EPS_RMS, None, ALU.add).then_inc(ms1, 1)
            for g in range(2):
                for qt in range(TT):
                    for i in range(HG):
                        reduce_max(0, g, qt, i, None)
                if g == 0:
                    max_parts(0, 0, PRO.index("MT0"))
            dve.wait_ge(root1, 2)
            dve.reciprocal(rstd1[:, TT:], ss1[:, TT:]).then_inc(rstd_r, 1)
            dve.wait_ge(tab_r, TAB * B // 2)
            dve.wait_ge(tab_in, 32)
            shift = tab[:, 2]
            wrow, brow = (wb_rows[:, i:i + 1, :].broadcast_to([P, B, D]) for i in range(2))
            dve.tensor_tensor(shift, shift, brow, ALU.add).then_inc(shift_r, 1)
            dve.wait_ge(shift_r, 1)
            dve.tensor_tensor(shift, shift, wrow, ALU.mult).then_inc(shift_r, 1)
            dve.wait_ge(shift_r, 2)
            dve.tensor_tensor(shift, shift, brow, ALU.add).then_inc(shift_r, 1)
            dve.wait_ge(rstd_r, 2)

            def batch(b, first, last, second):
                jobs = jobs_of(first, last)
                for u in range(UNITS):
                    g, qt = (u // TT + 2) % NG, u % TT
                    gb = b + (u // TT + 2) // NG
                    live = not (last and u >= UNITS // 2)
                    if u == 0 and not last:
                        y_done[0], y_done[1] = job_full, job_base(b, first)
                        norm(b + 1, True)
                    if live:
                        for i in (0, 1):
                            if u // TT < 2:
                                free = job_base(b, first) - (1 if u // TT == 0 else 0)
                            else:
                                free = job_no(b, first, last, "MT2" if u // TT == 2 else "MT3")
                            reduce_max(gb, g, qt, i, free if (qt == 0 and i == 0) else None)
                    op = jobs.get(u - 1)
                    if u > 0 and op is not None:
                        no = job_no(b, first, last, op)
                        if op in ("TR0", "TR1"):
                            split_n(b + 1, int(op[2]), no, job_base(b, first) - 1)
                        elif op[0] in "QK":
                            qk_low(b + 1, 2 * int(op[1]) + "QK".index(op[0]), no, True)
                        elif op in PREV:
                            wo_scale(b - 1, int(op[2]), no, not second)
                    if live:
                        for i in (2, 3):
                            reduce_max(gb, g, qt, i, None)
                    op = jobs.get(u)
                    if op is not None and op[0:2] == "MT":
                        g_m = int(op[2])
                        max_parts(b + (g_m == 0), g_m, job_no(b, first, last, op))
                    if u == 6 and not first:
                        o_norm(b - 1, 1, None if second else job_no_prev(b))
                    if u == 14:
                        o_norm(b, 0, None if first else job_no(b, first, last, "WO1"))

            def job_no_prev(b):
                return job_no(b - 1, False, False, "WO1")

            batch(0, True, False, False)
            with dve.Fori(1, 2) as b:
                batch(b, False, False, True)
            with dve.Fori(2, B - 1) as b:
                batch(b, False, False, False)
            batch(B - 1, False, True, False)
            end = job_no(B - 1, False, True, "WO1") + 1
            o_norm(B - 1, 1, end - 1)
            for w in range(2):
                wo_scale(B - 1, w, end + w, True)

        @block.tensor
        def _(pe):
            def job_wait(no):
                if not (isinstance(no, int) and no == 0):
                    pe.wait_ge(job_free, no)

            pe.wait_ge(small_in, 16 * 9)
            pe.wait_ge(consts, 6)
            n = 0
            for i in range(4):
                for k in range(KC):
                    mm = pe.matmul(ps_j[:, n * B:(n + 1) * B], ada_w[0:DT, i, k * P:(k + 1) * P], cond[0:DT, :],
                                   start=(n == 0), stop=True, skip_group_check=True)
                    n += 1
            mm.then_inc(job_full, 1)

            def transposes(nb, k, no):
                job_wait(no)
                pe.wait_ge(xhat_r, TT * (nb + 1))
                for t in range(TT):
                    mm = pe.transpose(ps_j[:, t * P:(t + 1) * P], xhat[:, t, k * P:(k + 1) * P], ident[:])
                mm.then_inc(job_full, 1)

            def split_product(out, lhs, rhs, inc=None):
                steps = [(a, c, k) for k in range(KC) for a, c in ((0, 0), (1, 0), (0, 1))]
                for n, (a, c, k) in enumerate(steps):
                    mm = pe.matmul(out, lhs(a, k), rhs(c, k), start=(n == 0), stop=(n == len(steps) - 1))
                return mm

            W, N, ON = (w_hi, w_lo), (n_hi, n_lo), (on_hi, on_lo)

            def project_qk(nb, op, no):
                job_wait(no)
                pe.wait_ge(n_r, 4 * (nb + 1))
                i, c = "QK".index(op[0]), int(op[1])
                split_product(ps_j[:], lambda a, k: W[a][:, k, i, c * P:(c + 1) * P], lambda a, k: N[a][:, k, :])\
                    .then_inc(job_full, 1)

            def project_v(nb, w, no):
                job_wait(no)
                pe.wait_ge(n_r, 4 * (nb + 1))
                for t in (2 * w, 2 * w + 1):
                    mm = split_product(ps_j[:, D * (t % 2):D * (t % 2 + 1)],
                                       lambda a, k: N[a][:, k, t * P:(t + 1) * P], lambda a, k: W[a][:, k, 2, :])
                mm.then_inc(job_full, 1)

            def project_o(b, w, no):
                job_wait(no)
                pe.wait_ge(on_r, 8 * (b + 1))
                for t in (2 * w, 2 * w + 1):
                    mm = split_product(ps_j[:, D * (t % 2):D * (t % 2 + 1)],
                                       lambda a, k: ON[a][:, k, t * P:(t + 1) * P], lambda a, k: W[a][:, k, 3, :])
                mm.then_inc(job_full, 1)

            def max_transpose(b, g, no):
                job_wait(no)
                pe.wait_ge(mx_red, UNITS * (NG * b + g + 1))
                pe.transpose(ps_j[0:2 * HG * 2, 0:P], mx[:, g % 2].rearrange("p s j t -> p (s j t)"), ident[:])\
                  .then_inc(job_full, 1)

            def max_scores(b, g, qt, i, fresh):
                n = UNITS * (NG * b + g) + HG * qt + i
                if qt == 0 and i == 0:
                    pe.wait_ge(stack_in, 32 * (NG * b + g + 1))
                if not fresh:
                    pe.wait_ge(mx_red, n - 1)
                j, r = i // 2, 64 * (i % 2)
                pe.matmul(ps_m[:, i % 2, :], qs[r:r + 64, g, j, qt * P:(qt + 1) * P], ks[r:r + 64, g, j, :],
                          start=True, stop=True).then_inc(mx_full, 1)

            def scores(b, g, kb, i, fresh):
                n = UNITS * b + TT * g + kb
                if kb == 0 and i == 0:
                    pe.wait_ge(m_in, 64 * (NG * b + g + 1))
                if not fresh and i % 2 == 0:
                    pe.wait_ge(p_r, 2 * n - 1 + i // 2)
                j, r = i // 2, 64 * (i % 2)
                mm = pe.matmul(ps_s[:, i, :], ks[r:r + 64, g, j, kb * P:(kb + 1) * P], qs[r:r + 64, g, j, :],
                               start=True, stop=True)
                if i % 2 == 1:
                    mm.then_inc(s_full, 1)

            def attend(b, u, fresh):
                g, kb = u // TT, u % TT
                pe.wait_ge(p_r, 2 * (UNITS * b + u + 1))
                if kb == 0:
                    pe.wait_ge(v_in, 16 * (NG * b + g + 1))
                    if not fresh:
                        pe.wait_ge(o_r, NG * b + g)
                for i in range(HG):
                    mm = pe.matmul(ps_o[32 * i:32 * i + 32, :], v[:, g, kb, i, :], prob[:, u % 2, i, :],
                                   start=(kb == 0), stop=(kb == TT - 1), skip_group_check=True)
                mm.then_inc(av_done, 1)

            def job(b, op, no):
                if op[0:2] == "TR":
                    transposes(b, int(op[2]), no)
                elif op[0] in "QK":
                    project_qk(b, op, no)
                elif op[0] == "V":
                    project_v(b, int(op[1]), no)
                elif op[0:2] == "MT":
                    max_transpose(b, int(op[2]), no)
                else:
                    project_o(b, int(op[2]), no)

            pe.wait_ge(w_lo_r, 1)
            for no, op in enumerate(PRO[1:-1], 1):
                job(0, op, no)
            pe.wait_ge(rep_ready, 1)
            for k in range(TAB):
                rows = DT + (k == 2)
                for q in range(B // 2):
                    n = (B // 2) * k + q
                    if n >= HG:
                        pe.wait_ge(tab_r, n - HG + 1)
                    for e in range(2):
                        mm = pe.matmul(ps_s[:, n % HG, D * e:D * (e + 1)], cond_rep[0:rows, 2 * q + e, :],
                                       ada_w[0:rows, 4 + k, :], start=True, stop=True)
                    mm.then_inc(tab_full, 1)
            for g in range(2):
                for qt in range(TT):
                    for i in range(HG):
                        max_scores(0, g, qt, i, g == 0 and qt == 0 and i < 2)
                if g == 0:
                    max_transpose(0, 0, PRO.index("MT0"))
            pe.wait_ge(tab_r, TAB * B // 2)

            def batch(b, first, last):
                jobs = jobs_of(first, last)
                for u in range(UNITS):
                    g, kb = u // TT, u % TT
                    for i in range(HG):
                        scores(b, g, kb, i, first and u == 0)
                        if not (last and g >= 2):
                            max_scores(b + (g + 2) // NG, (g + 2) % NG, kb, i, False)
                    if u in jobs:
                        op = jobs[u]
                        job(b if op in OWN else b - 1 if op in PREV else b + 1, op, job_no(b, first, last, op))
                    if u > 0:
                        attend(b, u - 1, first and u == 1)
                    elif not first:
                        attend(b - 1, UNITS - 1, False)

            batch(0, True, False)
            with pe.Fori(1, B - 1) as b:
                batch(b, False, False)
            batch(B - 1, False, True)
            attend(B - 1, UNITS - 1, False)
            end = job_no(B - 1, False, True, "WO1") + 1
            for w in range(2):
                project_o(B - 1, w, end + w)


def ffn_phase(nc, dram, tensors):
    x_all, tab, coef, ident, ss2 = (tensors[k] for k in ("x_all", "tab", "coef", "ident", "ss2"))
    with ExitStack() as ctx:
        def sb(name, shape, dt=F32):
            return ctx.enter_context(nc.sbuf_tensor(name, shape, dt))

        def sem(name):
            return ctx.enter_context(nc.semaphore(name))

        gh_raw = sb("gh_raw", [P, KC, 2, HID])
        gh_hi = sb("gh_hi", [P, KC, 2, HID], F32R)
        gh_lo = sb("gh_lo", [P, KC, 2, HID], F32R)
        ow_raw = sb("ow_raw", [P, JC, D])
        ow_hi = sb("ow_hi", [P, JC, D], F32R)
        ow_lo = sb("ow_lo", [P, JC, D], F32R)
        rows = sb("rows", [P, 3, D])
        rstd2 = sb("rstd2", [P, B * TT])
        xhat = sb("f_xhat", [P, TT, D])
        y_n = sb("f_y_n", [P, KC, T])
        n_hi = sb("f_n_hi", [P, 2, KC, T], F32R)
        n_lo = sb("f_n_lo", [P, 2, KC, T], F32R)
        sil = sb("sil", [P, 2, T])
        act_y = sb("act_y", [P, 2, T])
        a_hi = sb("a_hi", [P, 4, T], F32R)
        a_lo = sb("a_lo", [P, 4, T], F32R)
        f_t = sb("f_t", [P, TT, D])
        st = sb("st", [P, TT, 6])
        mv = sb("mv", [P, TT, 2])
        sd = sb("sd", [P, TT])
        z = sb("z", [P, 2, TT, D])
        ps_g = ctx.enter_context(nc.psum_tensor("ps_g", [P, 2, T], F32))
        ps_h = ctx.enter_context(nc.psum_tensor("ps_h", [P, 2, T], F32))
        ps_t = ctx.enter_context(nc.psum_tensor("ps_t", [P, KC, T], F32))
        ps_f = ctx.enter_context(nc.psum_tensor("ps_f", [P, TT, D], F32))

        gh_in = sem("gh_in"); ow_in = sem("ow_in"); rows_in = sem("rows_in")
        gh_hi_r = sem("gh_hi_r"); gh_lo_r = sem("gh_lo_r"); ow_hi_r = sem("ow_hi_r"); ow_lo_r = sem("ow_lo_r")
        ms2 = sem("ms2"); root2 = sem("root2"); rstd2_r = sem("rstd2_r"); rows_r = sem("rows_r")
        xhat_r = sem("f_xhat_r"); tr_full = sem("tr_full"); y_r = sem("f_y_r"); n_r = sem("f_n_r")
        gh_full = sem("gh_full"); sil_r = sem("sil_r"); act_r = sem("act_r"); a_hi_r = sem("a_hi_r")
        a_lo_r = sem("a_lo_r"); out_used = sem("out_used"); f_add = sem("f_add")
        f_mul = sem("f_mul"); x2_r = sem("x2_r"); stat_r = sem("stat_r"); sd_r = sem("sd_r"); rs_r = sem("rs_r")
        mul_begun = sem("mul_begun"); sp_waited = sem("f_sp_waited"); z_r = sem("z_r"); stored = sem("stored")

        block = ctx.enter_context(nc.Block())

        @block.sync
        def _(sp):
            for i, name in enumerate(("gate", "hidden")):
                sp.dma_start(gh_raw[:, :, i, :], dram[name].rearrange("(k p) n -> p k n", p=P)).then_inc(gh_in, 16)
            sp.dma_start(ow_raw[:], dram["out_w"].rearrange("(j p) n -> p j n", p=P)).then_inc(ow_in, 16)
            for i, name in enumerate(("out_b", "l1_w")):
                sp.dma_start(rows[:, i, :], dram[name].partition_broadcast(P)).then_inc(rows_in, 16)

            def batch(b, par):
                sp.wait_ge(z_r, 6 * (b + 1))
                sp.sem_inc(sp_waited, 1)
                sp.dma_start(dram["out"][bass.ds(b, 1)].rearrange("a p t n -> p (a t) n"), z[:, par]).then_inc(stored, 16)
                sp.wait_ge(stored, 16 * (b + 1))
                sp.sem_inc(sp_waited, 1)

            with sp.Fori(0, B // 2) as i:
                batch(2 * i, 0)
                batch(2 * i + 1, 1)

        @block.scalar
        def _(act):
            act.wait_ge(ms2, 1)
            act.activation(rstd2[:], rstd2[:], ACT.Sqrt).then_inc(root2, 1)
            act.wait_ge(gh_in, 32)
            for i in range(2):
                for k in range(KC):
                    act.activation(gh_hi[:, k, i, :], gh_raw[:, k, i, :], ACT.Copy).then_inc(gh_hi_r, 1)

            def y_copy(b):
                for k in range(KC):
                    act.wait_ge(tr_full, KC * b + k + 1)
                    if not (isinstance(b, int) and b == 0):
                        act.wait_ge(n_r, 4 * b)
                    cf = coef[:, :, k:k + 1, bass.ds(b, 1)].rearrange("p i k b -> p i (k b)")
                    act.activation(y_n[:, k, :], ps_t[:, k, :], ACT.Identity, scale=cf[:, 2], bias=cf[:, 3])\
                       .then_inc(y_r, 1)

            def silu(n, j, fresh):
                act.wait_ge(gh_full, 2 * n + 1)
                if not fresh:
                    act.wait_ge(act_r, n - 1)
                act.activation(sil[:, j % 2, :], ps_g[:, j % 2, :], ACT.Silu).then_inc(sil_r, 1)

            def high(n, j, fresh):
                act.wait_ge(act_r, n + 1)
                if not fresh:
                    act.wait_ge(out_used, n - 3)
                act.activation(a_hi[:, j % 4, :], act_y[:, j % 2, :], ACT.Copy).then_inc(a_hi_r, 1)

            def deviation(b):
                act.wait_ge(stat_r, 9 * b + 9)
                act.activation(sd[:], sd[:], ACT.Sqrt).then_inc(sd_r, 1)

            y_copy(0)
            act.wait_ge(ow_in, 16)
            act.activation(ow_hi[:], ow_raw[:], ACT.Copy).then_inc(ow_hi_r, 1)

            def batch(b, first, last):
                for j in range(JC):
                    n = JC * b + j
                    silu(n, j, first and j < 2)
                    if j > 0:
                        high(n - 1, j - 1, first and j <= 4)
                    elif not first:
                        high(n - 1, JC - 1, False)
                    if j == 4 and not last:
                        y_copy(b + 1)
                    if j == 5 and not first:
                        deviation(b - 1)

            batch(0, True, False)
            with act.Fori(1, B - 1) as b:
                batch(b, False, False)
            batch(B - 1, False, True)
            high(JC * B - 1, JC - 1, False)
            deviation(B - 1)

        @block.vector
        def _(dve):
            dve.tensor_scalar(rstd2[:], ss2[:].rearrange("p b t -> p (b t)"), EPS_RMS, None, ALU.add).then_inc(ms2, 1)
            dve.wait_ge(root2, 1)
            dve.reciprocal(rstd2[:], rstd2[:]).then_inc(rstd2_r, 1)
            dve.wait_ge(rstd2_r, 1)

            def norm(b, fresh):
                if not fresh:
                    dve.wait_ge(tr_full, KC * b)
                for t in range(TT):
                    xs = x_all[:, bass.ds(b, 1), t, :].rearrange("p a n -> p (a n)")
                    dve.tensor_scalar(xhat[:, t, :], xs, rstd2[:, bass.ds(TT * b + t, 1)], None, ALU.mult)\
                       .then_inc(xhat_r, 1)

            norm(0, True)
            for i in range(2):
                for k in range(KC):
                    dve.wait_ge(gh_hi_r, KC * i + k + 1)
                    dve.tensor_tensor(gh_lo[:, k, i, :], gh_raw[:, k, i, :], gh_hi[:, k, i, :].bitcast(F32), ALU.subtract)\
                       .then_inc(gh_lo_r, 1)

            def split_n(b, par, fresh):
                for k in range(KC):
                    dve.wait_ge(y_r, KC * b + k + 1)
                    if not fresh:
                        dve.wait_ge(gh_full, 2 * JC * (b - 1))
                    dve.tensor_copy(n_hi[:, par, k, :], y_n[:, k, :]).then_inc(n_r, 1)
                    dve.wait_ge(n_r, 4 * b + 2 * k + 1)
                    dve.tensor_tensor(n_lo[:, par, k, :], y_n[:, k, :], n_hi[:, par, k, :].bitcast(F32), ALU.subtract)\
                       .then_inc(n_r, 1)

            split_n(0, 0, True)
            dve.wait_ge(ow_hi_r, 1)
            dve.tensor_tensor(ow_lo[:], ow_raw[:], ow_hi[:].bitcast(F32), ALU.subtract).then_inc(ow_lo_r, 1)
            dve.wait_ge(rows_in, 32)
            dve.tensor_tensor(rows[:, 2, :], rows[:, 1, :], rows[:, 1, :], ALU.mult).then_inc(rows_r, 1)
            dve.wait_ge(rows_r, 1)

            def gate(n, j, fresh):
                dve.wait_ge(sil_r, n + 1)
                dve.wait_ge(gh_full, 2 * n + 2)
                if not fresh:
                    dve.wait_ge(a_lo_r, n - 1)
                dve.tensor_tensor(act_y[:, j % 2, :], ps_h[:, j % 2, :], sil[:, j % 2, :], ALU.mult).then_inc(act_r, 1)

            def low(n, j, fresh):
                dve.wait_ge(a_hi_r, n + 1)
                if not fresh:
                    dve.wait_ge(out_used, n - 3)
                dve.tensor_tensor(a_lo[:, j % 4, :], act_y[:, j % 2, :], a_hi[:, j % 4, :].bitcast(F32), ALU.subtract)\
                   .then_inc(a_lo_r, 1)

            def add_bias(b, fresh):
                dve.wait_ge(out_used, JC * (b + 1))
                if not fresh:
                    dve.wait_ge(x2_r, 2 * b)
                for w in range(2):
                    dve.tensor_tensor(f_t[:, 2 * w:2 * w + 2], ps_f[:, 2 * w:2 * w + 2],
                                      rows[:, 0:1, :].broadcast_to([P, 2, D]), ALU.add).then_inc(f_add, 1)

            def stats(b):
                for w in range(2):
                    dve.wait_ge(f_mul, 2 * b + w + 1)
                    xs = x_all[:, bass.ds(b, 1), 2 * w:2 * w + 2, :].rearrange("p a t n -> p (a t) n")
                    dve.tensor_tensor(xs, xs, f_t[:, 2 * w:2 * w + 2], ALU.add).then_inc(x2_r, 1)
                for t in range(TT):
                    dve.wait_ge(x2_r, 2 * b + t // 2 + 1)
                    xs = x_all[:, bass.ds(b, 1), t, :].rearrange("p a n -> p (a n)")
                    dve.bn_stats(st[:, t, :], xs).then_inc(stat_r, 1)
                for t in range(TT):
                    dve.wait_ge(stat_r, 9 * b + t + 1)
                    dve.bn_aggr(mv[:, t, :], st[:, t, :]).then_inc(stat_r, 1)
                dve.wait_ge(stat_r, 9 * b + 8)
                dve.tensor_scalar(sd[:], mv[:, :, 1], EPS_LN, None, ALU.add).then_inc(stat_r, 1)

            def layer_norm(b, par, fresh):
                dve.wait_ge(sd_r, b + 1)
                dve.reciprocal(sd[:], sd[:]).then_inc(rs_r, 1)
                dve.wait_ge(rs_r, b + 1)
                if not fresh:
                    dve.wait_ge(stored, 16 * (b - 1))
                for t in range(TT):
                    xs = x_all[:, bass.ds(b, 1), t, :].rearrange("p a n -> p (a n)")
                    dve.tensor_scalar(z[:, par, t, :], xs, mv[:, t, 0:1], sd[:, t:t + 1], ALU.subtract, ALU.mult)\
                       .then_inc(z_r, 1)
                dve.wait_ge(z_r, 6 * b + 4)
                zz = z[:, par]
                dve.tensor_tensor(zz, zz, rows[:, 2:3, :].broadcast_to([P, TT, D]), ALU.mult).then_inc(z_r, 1)
                dve.wait_ge(z_r, 6 * b + 5)
                dve.tensor_tensor(zz, zz, tab[:, 2, bass.ds(b, 1), :].broadcast_to([P, TT, D]), ALU.add).then_inc(z_r, 1)

            def batch(b, par, first, last):
                for j in range(JC):
                    n = JC * b + j
                    gate(n, j, first and j < 2)
                    if j > 0:
                        low(n - 1, j - 1, first and j <= 4)
                    elif not first:
                        low(n - 1, JC - 1, False)
                    if j == 1 and not last:
                        norm(b + 1, False)
                    if j == 2 and not first:
                        add_bias(b - 1, first or False)
                    if j == 4 and not first:
                        stats(b - 1)
                    if j == 5 and not last:
                        split_n(b + 1, 1 - par, first)
                    if j == 6 and not first:
                        layer_norm(b - 1, 1 - par, False)

            def pair(i, first, last):
                batch(2 * i, 0, first, False)
                batch(2 * i + 1, 1, False, last)

            def first_pair():
                for b in (0, 1):
                    for j in range(JC):
                        n = JC * b + j
                        gate(n, j, n < 2)
                        if n > 0:
                            low(n - 1, (j - 1) % JC, n <= 4)
                        if j == 1:
                            norm(b + 1, False)
                        if j == 2 and b == 1:
                            add_bias(0, True)
                        if j == 4 and b == 1:
                            stats(0)
                        if j == 5:
                            split_n(b + 1, 1 - b, b == 0)
                        if j == 6 and b == 1:
                            layer_norm(0, 0, True)

            def next_batch(b, par, fresh, last):
                for j in range(JC):
                    n = JC * b + j
                    gate(n, j, False)
                    low(n - 1, (j - 1) % JC, False)
                    if j == 1 and not last:
                        norm(b + 1, False)
                    if j == 2:
                        add_bias(b - 1, False)
                    if j == 4:
                        stats(b - 1)
                    if j == 5 and not last:
                        split_n(b + 1, 1 - par, False)
                    if j == 6:
                        layer_norm(b - 1, 1 - par, fresh)

            first_pair()
            with dve.Fori(1, 2) as i:
                next_batch(2 * i, 0, True, False)
                next_batch(2 * i + 1, 1, False, False)
            with dve.Fori(2, B // 2 - 1) as i:
                next_batch(2 * i, 0, False, False)
                next_batch(2 * i + 1, 1, False, False)
            next_batch(B - 2, 0, False, False)
            next_batch(B - 1, 1, False, True)
            low(JC * B - 1, JC - 1, False)
            add_bias(B - 1, False)
            stats(B - 1)
            layer_norm(B - 1, 1, False)

        @block.gpsimd
        def _(pool):
            def batch(b):
                for w in range(2):
                    pool.wait_ge(f_add, 2 * b + w + 1)
                    pool.sem_inc(mul_begun, 1)
                    t = f_t[:, 2 * w:2 * w + 2]
                    pool.tensor_tensor(t, t, tab[:, 1, bass.ds(b, 1), :].broadcast_to([P, 2, D]), ALU.mult)\
                        .then_inc(f_mul, 1)

            with pool.Fori(0, B) as b:
                batch(b)

        @block.tensor
        def _(pe):
            GH, N, OW, A = (gh_hi, gh_lo), (n_hi, n_lo), (ow_hi, ow_lo), (a_hi, a_lo)
            PARTS = ((0, 0), (1, 0), (0, 1))

            def transposes(b, fresh):
                pe.wait_ge(xhat_r, TT * (b + 1))
                for k in range(KC):
                    if not fresh:
                        pe.wait_ge(y_r, KC * (b - 1) + k + 1)
                    for t in range(TT):
                        mm = pe.transpose(ps_t[:, k, t * P:(t + 1) * P], xhat[:, t, k * P:(k + 1) * P], ident[:])
                    mm.then_inc(tr_full, 1)

            def gate_hidden(n, par, j, fresh):
                if j == 0:
                    pe.wait_ge(n_r, n // JC * 4 + 4 if isinstance(n, int) else 4 * n_batch[0] + 4)
                for i, (ps, used) in enumerate(((ps_g, sil_r), (ps_h, act_r))):
                    if not fresh:
                        pe.wait_ge(used, n - 1)
                    m = 0
                    for k in range(KC):
                        for a, c in PARTS:
                            mm = pe.matmul(ps[:, j % 2, :], GH[a][:, k, i, j * P:(j + 1) * P], N[c][:, par, k, :],
                                           start=(m == 0), stop=(m == 5))
                            m += 1
                    mm.then_inc(gh_full, 1)

            n_batch = [None]

            def project_out(n, j, b, fresh):
                pe.wait_ge(a_hi_r, n + 1)
                pe.wait_ge(a_lo_r, n + 1)
                if j == 0 and not fresh:
                    pe.wait_ge(f_add, 2 * b)
                for t in range(TT):
                    for m, (a, c) in enumerate(PARTS):
                        mm = pe.matmul(ps_f[:, t, :], A[a][:, j % 4, t * P:(t + 1) * P], OW[c][:, j, :],
                                       start=(j == 0 and m == 0 and t % 2 == 0), stop=(j == JC - 1 and m == 2),
                                       skip_group_check=True)
                mm.then_inc(out_used, 1)

            transposes(0, True)
            pe.wait_ge(gh_lo_r, 2 * KC)
            LAG = 2

            def batch(b, par, first, last):
                for j in range(JC):
                    n = JC * b + j
                    n_batch[0] = b
                    gate_hidden(n, par, j, first and j < 2)
                    if j >= LAG:
                        if first and j == LAG:
                            pe.wait_ge(ow_lo_r, 1)
                        project_out(n - LAG, j - LAG, b, first)
                    elif not first:
                        project_out(n - LAG, j - LAG + JC, b - 1, False)
                    if j == 3 and not last:
                        transposes(b + 1, False)

            batch(0, 0, True, False)
            batch(1, 1, False, False)
            with pe.Fori(1, B // 2 - 1) as i:
                batch(2 * i, 0, False, False)
                batch(2 * i + 1, 1, False, False)
            batch(B - 2, 0, False, False)
            batch(B - 1, 1, False, True)
            for j in (JC - 2, JC - 1):
                project_out(JC * (B - 1) + j, j, B - 1, False)


def build(nc, dram):
    with ExitStack() as ctx:
        def sb(name, shape, dt=F32):
            return ctx.enter_context(nc.sbuf_tensor(name, shape, dt))

        tensors = {
            "x_all": sb("x_all", [P, B, TT, D]),
            "tab": sb("tab", [P, TAB, B, D]),
            "coef": sb("coef", [P, 4, KC, B]),
            "ident": sb("ident", [P, P]),
            "ss2": sb("ss2", [P, B, TT]),
        }
        attention_phase(nc, dram, tensors)
        ffn_phase(nc, dram, tensors)


_TRANSPOSED = {
    "gamma1": "L0_cond_attn_gamma_w", "beta1": "L0_cond_attn_beta_w", "gamma2": "L0_cond_ffn_gamma_w",
    "beta2": "L0_cond_ffn_beta_w", "alpha1": "L0_cond_attn_alpha_w", "alpha2": "L0_cond_ffn_alpha_w",
    "lin_w": "L1_cond_lin_w", "wq": "L0_cond_W_q", "wk": "L0_cond_W_k", "wv": "L0_cond_W_v", "wo": "L0_cond_W_o",
    "gate": "L0_cond_gate_w", "hidden": "L0_cond_hidden_w", "out_w": "L0_cond_out_w", "cond": "cond_256",
}
_PLAIN = {"lin_b": "L1_cond_lin_b", "l1_w": "L1_cond_weight", "l1_b": "L1_cond_bias", "out_b": "L0_cond_out_b"}


def kernel(**inputs):
    import numpy as _np
    import concourse.bacc as _bacc
    from concourse.bass_utils import run_bass_kernel_spmd as _run

    nc = _bacc.Bacc("TRN2", target_bir_lowering=False, num_devices=1)
    arrays = {"in_x": _np.ascontiguousarray(_np.asarray(inputs["x"])).reshape(B, P, TT, D)}
    for name, key in _TRANSPOSED.items():
        arrays["in_" + name] = _np.ascontiguousarray(_np.asarray(inputs[key]).T)
    for name, key in _PLAIN.items():
        arrays["in_" + name] = _np.ascontiguousarray(_np.asarray(inputs[key]))
    dram = {k[3:]: nc.dram_tensor(k, a.shape, mybir.dt.from_np(a.dtype), kind="ExternalInput").ap()
            for k, a in arrays.items()}
    dram["out"] = nc.dram_tensor("out_y", (B, P, TT, D), F32, kind="ExternalOutput").ap()
    build(nc, dram)
    r = _run(nc, [arrays], core_ids=[0])
    return r.results[0]["out_y"].reshape(B, P * TT, D)
```

```python
from contextlib import ExitStack

import concourse.bass as bass
from concourse import mybir

F32 = mybir.dt.float32
F32R = mybir.dt.float32r
ALU = mybir.AluOpType
ACT = mybir.ActivationFunctionType
AX = mybir.AxisListType

P = 128
B = 8
T = 512
D = 256
KC = D // P
TT = T // P
NH = 16
DH = D // NH
HG = 4
NG = NH // HG
DT = 64
HID = 4 * D
JC = HID // P
EPS_RMS = 1e-6
EPS_LN = 1e-5
SCALE = (NH / D) ** 0.5
UNITS = NG * TT
TAB = 3

PRO = ["COEF", "TR0", "TR1", "Q0", "K0", "Q1", "K1", "V0", "V1", "MT0"]
MID = {0: "MT1", 1: "TR0", 2: "TR1", 3: "Q0", 4: "K0", 5: "MT2", 6: "V0", 7: "V1", 8: "Q1", 9: "MT3",
       10: "K1", 12: "WO0", 13: "MT0", 14: "WO1"}
ORDER = ("S0", "S1", "M0", "M1", "S2", "S3", "A", "M2", "M3", "J")
RT = (B - 2) * TT
DS = T * NH // 2 // P
OWN = ("MT1", "MT2", "MT3")
PREV = ("WO0", "WO1")


def jobs_of(first, last):
    return {u: o for u, o in MID.items() if (o not in PREV or not first) and (o in OWN + PREV or not last)}


N_FIRST = len(jobs_of(True, False))
N_MID = len(jobs_of(False, False))


def job_base(b, first):
    return len(PRO) if first else len(PRO) + N_FIRST - N_MID + N_MID * b


def job_no(b, first, last, op):
    return job_base(b, first) + list(jobs_of(first, last).values()).index(op)


def attention_phase(nc, dram, tensors):
    x_all, tab, coef, ident, ss2, rstd2 = (tensors[k] for k in ("x_all", "tab", "coef", "ident", "ss2", "rstd2"))
    wo_hi, wo_lo, o_raw, o_c, d_c, on_hi, on_lo, wo_t, raw = (
        tensors[k] for k in ("wo_hi", "wo_lo", "o_raw", "o_c", "d_c", "on_hi", "on_lo", "wo_t", "raw"))
    with ExitStack() as ctx:
        def sb(name, shape, dt=F32):
            return ctx.enter_context(nc.sbuf_tensor(name, shape, dt))

        def sem(name):
            return ctx.enter_context(nc.semaphore(name))

        cond = sb("cond", [DT + 1, B])
        cond_rep = sb("cond_rep", [DT + 1, B, P])
        d_s = sb("d_s", [P, 2, DS])
        w_hi = sb("w_hi", [P, KC, 3, D], F32R)
        w_lo = sb("w_lo", [P, KC, 3, D], F32R)
        ss1 = sb("ss1", [P, B * TT])
        rstd1 = sb("rstd1", [P, B * TT])
        junk = sb("junk", [P, D])
        xhat = raw[:, 0:TT * D].rearrange("p (t n) -> p t n", n=D)
        y_n = raw[:, TT * D:2 * TT * D].rearrange("p (k n) -> p k n", n=T)
        v_st = raw[:, 2 * TT * D:].rearrange("p (g t i d) -> p g t i d", g=NG, t=TT, i=HG)
        n_hi = sb("n_hi", [P, KC, T], F32R)
        n_lo = sb("n_lo", [P, KC, T], F32R)
        qk_hi = sb("qk_hi", [P, 4, T], F32R)
        qk_lo = sb("qk_lo", [P, 4, T], F32R)
        qs = sb("qs", [P, NG, 2, T], F32R)
        ks = sb("ks", [P, NG, 2, T], F32R)
        v = sb("v", [P, NG, TT, HG, 32])
        mx = sb("mx", [P, 2, 2, 2, TT])
        m_hl = sb("m_hl", [2 * HG * 2, 2, P], F32R)
        prob = sb("prob", [P, 2, HG, T])
        flat = prob[:].rearrange("p u h n -> p u (h n)")
        w_raw = flat[:, 0].rearrange("p (k i n) -> p k i n", k=KC, n=D)
        ada_w = flat[0:DT + 1, 1, 0:7 * D].rearrange("p (i n) -> p i n", n=D)
        ps_s = ctx.enter_context(nc.psum_tensor("ps_s", [P, HG, T], F32))
        ps_m = ctx.enter_context(nc.psum_tensor("ps_m", [P, 2, T], F32))
        ps_o = ctx.enter_context(nc.psum_tensor("ps_o", [P, T], F32))
        ps_j = ctx.enter_context(nc.psum_tensor("ps_j", [P, T], F32))
        stack_d = nc.dram_tensor("stack_scratch", (2, 2, HG, P * T), F32, kind="Internal").ap()
        o_d = nc.dram_tensor("out_scratch", (2, 2, P, T), F32, kind="Internal").ap()
        r_d = nc.dram_tensor("reciprocal_scratch", (2, P * DS), F32, kind="Internal").ap()

        x0_in = sem("x0_in"); x1_in = sem("x1_in"); x_in = sem("x_in"); small_in = sem("small_in")
        wqk_in = sem("wqk_in"); wvo_in = sem("wvo_in")
        consts = sem("consts"); rep_ready = sem("rep_ready"); pad_written = sem("pad_written")
        w_hi_r = sem("w_hi_r"); w_lo_r = sem("w_lo_r")
        sq1 = sem("sq1"); ms1 = sem("ms1"); root1 = sem("root1"); rstd_r = sem("rstd_r")
        coef_r = sem("coef_r"); tab_full = sem("tab_full"); tab_r = sem("tab_r")
        xhat_r = sem("xhat_r"); y_r = sem("y_r"); n_r = sem("n_r")
        qk_hi_r = sem("qk_hi_r"); qk_lo_r = sem("qk_lo_r"); v_r = sem("v_r")
        scr_w = sem("scr_w"); stack_in = sem("stack_in"); v_in = sem("v_in")
        mx_full = sem("mx_full"); mx_red = sem("mx_red"); m_r = sem("m_r"); m_in = sem("m_in")
        s_full = sem("s_full"); p_r = sem("p_r"); av_done = sem("av_done")
        o_r = sem("o_r"); oc_in = sem("oc_in"); x1_r = sem("x1_r"); sq2 = sem("sq2")
        den_in = sem("den_in"); rec_r = sem("rec_r"); rec_w = sem("rec_w"); rec_in = sem("rec_in")
        omul_r = sem("omul_r"); ohi_r = sem("ohi_r"); olo_r = sem("olo_r")
        job_full = sem("job_full"); job_free = sem("job_free"); sp_waited = sem("sp_waited"); ffn_in = sem("ffn_in")
        ms2 = sem("ms2"); root2 = sem("root2"); rstd2_r = sem("rstd2_r")
        ow_w = sem("ow_w"); pool_waited = sem("pool_waited")

        block = ctx.enter_context(nc.Block())

        @block.sync
        def _(sp):
            sp.dma_start(x_all[:, 0], dram["x"][0]).then_inc(x0_in, 16)
            sp.dma_start(cond[0:DT, :], dram["cond"]).then_inc(small_in, 16)
            for i, name in enumerate(("gamma1", "beta1", "gamma2", "beta2", "alpha1", "alpha2", "lin_w")):
                sp.dma_start(ada_w[0:DT, i, :], dram[name]).then_inc(small_in, 16)
            sp.dma_start(ada_w[DT:DT + 1, 6, :], dram["lin_b"].rearrange("(a n) -> a n", a=1)).then_inc(small_in, 16)
            sp.dma_start(x_all[:, 1], dram["x"][1]).then_inc(x1_in, 16)
            sp.wait_ge(consts, 5)
            for c in range(2):
                for i in range(2):
                    rows = stack_d[i, c].rearrange("j (r t n) -> (j r) t n", t=4, n=T)
                    sp.dma_start(rows[:, 3, :], o_raw[:, i, :]).then_inc(pad_written, 16)
            sp.wait_ge(pad_written, 64)

            def wait(semaphore, value):
                sp.wait_ge(semaphore, value)
                sp.sem_inc(sp_waited, 1)

            def stack_write(nb, c):
                for i, terms in enumerate(((qk_hi, qk_lo, qk_hi), (qk_hi, qk_hi, qk_lo))):
                    wait(qk_lo_r, 4 * nb + 2 * c + i + 1)
                    rows = stack_d[i, c].rearrange("j (r t n) -> (j r) t n", t=4, n=T)
                    for t, src in enumerate(terms):
                        sp.dma_start(rows[:, t, :], src[:, 2 * c + i, :].bitcast(F32)).then_inc(scr_w, 16)
                wait(scr_w, 96 * (2 * nb + c + 1))

            def stack_read(nb, g, reuse):
                if reuse:
                    wait(av_done, UNITS * (nb - 1) + TT * (g + 1))
                for i, dst in enumerate((qs, ks)):
                    src = stack_d[i, g // 2, 2 * (g % 2):2 * (g % 2) + 2].rearrange("j (r n) -> r j n", n=T)
                    sp.dma_start(dst[:, g].bitcast(F32), src).then_inc(stack_in, 16)

            def v_copy(nb, g):
                wait(v_r, TT * (nb + 1))
                sp.dma_start(v[:, g], v_st[:, g]).then_inc(v_in, 16)

            for c in range(2):
                stack_write(0, c)
                for g in (2 * c, 2 * c + 1):
                    stack_read(0, g, False)
                    wait(stack_in, 32 * (g + 1))
            for b in range(2, B):
                sp.dma_start(x_all[:, b], dram["x"][b]).then_inc(x_in, 16)
            for g in range(NG - 1):
                v_copy(0, g)
                wait(v_in, 16 * (g + 1))

            def batch(b, first, last):
                nb = b + 1
                if not first:
                    stack_read(b, 3, True)
                    wait(stack_in, 128 * (b + 1))
                v_copy(b, 3)
                wait(v_in, 64 * (b + 1))
                if last:
                    wait(job_full, job_base(b, first))
                    gh_raw = raw[:].rearrange("p (k i n) -> p k i n", k=KC, i=2)
                    for i, name in enumerate(("gate", "hidden")):
                        sp.dma_start(gh_raw[:, :, i, :], dram[name].rearrange("(k p) n -> p k n", p=P)).then_inc(ffn_in, 16)
                    sp.wait_ge(ffn_in, 32)
                    return
                stack_write(nb, 0)
                for g in range(3):
                    if g == 2:
                        stack_write(nb, 1)
                    stack_read(nb, g, True)
                    wait(stack_in, 32 * (NG * nb + g + 1))
                    v_copy(nb, g)
                    wait(v_in, 16 * (NG * nb + g + 1))

            batch(0, True, False)
            with sp.Fori(1, B - 1) as b:
                batch(b, False, False)
            batch(B - 1, False, True)

        @block.gpsimd
        def _(pool):
            for n, (ap, value) in enumerate(((ident[:], 0.0), (cond[DT:DT + 1, :], 1.0), (o_raw[:, 0, :], 0.0),
                                             (o_raw[:, 1, :], 1.0), (v_st[:, :, :, :, DH:32], 1.0))):
                pool.memset(ap, value).then_inc(consts, 1)
                pool.wait_ge(consts, n + 1)
            pool.affine_select(out=ident[:], in_=ident[:], compare_op=ALU.not_equal, fill=1.0, base=0,
                               pattern=[[-1, P]], channel_multiplier=1).then_inc(consts, 1)

            def max_rows(b, g):
                n = NG * b + g
                if not (isinstance(n, int) and n == 0):
                    pool.wait_ge(m_in, 64 * n)
                pool.wait_ge(m_r, 2 * (n + 1))
                pool.sem_inc(pool_waited, 1)
                for s in range(2):
                    for hl in range(2):
                        r = 64 * s + 4 * hl + 3
                        pool.dma_start(qs[r:r + 1, g].rearrange("r j n -> r (j n)").bitcast(F32),
                                       m_hl[2 * TT * s:2 * TT * (s + 1), hl, :].bitcast(F32)).then_inc(m_in, 16)

            def update_x(b, w, no):
                pool.wait_ge(job_free, no + 1)
                pool.sem_inc(pool_waited, 1)
                xs = x_all[:, bass.ds(b, 1), 2 * w:2 * w + 2, :].rearrange("p a t n -> p (a t) n")
                pool.tensor_tensor(xs, xs, wo_t[:, w], ALU.add).then_inc(x1_r, 1)

            def o_norm(b, c):
                pool.wait_ge(oc_in, 16 * (2 * b + c + 1))
                pool.wait_ge(rec_in, 16 * (2 * b + c + 1))
                pool.tensor_tensor(o_c[:, c, :], o_c[:, c, :], d_c[:, c, :], ALU.mult).then_inc(omul_r, 1)

            def o_low(b, c):
                pool.wait_ge(ohi_r, 2 * b + c + 1)
                pool.tensor_tensor(on_lo[:, c, :], o_c[:, c, :], on_hi[:, c, :].bitcast(F32), ALU.subtract)\
                    .then_inc(olo_r, 1)

            max_rows(0, 0)

            def batch(b, first, last):
                max_rows(b, 1)
                if not first:
                    o_low(b - 1, 0)
                max_rows(b, 2)
                if not first:
                    o_norm(b - 1, 1)
                max_rows(b, 3)
                if not first:
                    o_low(b - 1, 1)
                if not first:
                    update_x(b - 1, 0, job_no(b, first, last, "WO0"))
                if not last:
                    max_rows(b + 1, 0)
                if not first:
                    update_x(b - 1, 1, job_no(b, first, last, "WO1"))
                o_norm(b, 0)

            batch(0, True, False)
            with pool.Fori(1, B - 1) as b:
                batch(b, False, False)
            batch(B - 1, False, True)
            o_low(B - 1, 0)

        @block.scalar
        def _(act):
            for i, (name, arrived) in enumerate((("wq", wqk_in), ("wk", wqk_in), ("wv", wvo_in), ("wo", wvo_in))):
                act.dma_start(w_raw[:, :, i, :], dram[name].rearrange("(k p) n -> p k n", p=P)).then_inc(arrived, 16)

            def square1(n):
                if n > 0:
                    act.wait_ge(sq1, n)
                nc.scalar.activation(junk[:], x_all[:, n // TT, n % TT, :], ACT.Square, scale=1.0 / DH,
                                     accum_out=ss1[:, n:n + 1]).then_inc(sq1, 1)

            act.wait_ge(x0_in, 16)
            for t in range(TT):
                square1(t)
            act.wait_ge(ms1, 1)
            nc.scalar.activation(ss1[:, 0:TT], ss1[:, 0:TT], ACT.Sqrt).then_inc(root1, 1)

            for i, arrived in ((0, wqk_in), (2, wvo_in)):
                act.wait_ge(arrived, 32)
                for dst, src in ((w_hi[:, :, 0:2], w_raw[:, :, 0:2]),) if i == 0 else \
                        ((w_hi[:, :, 2], w_raw[:, :, 2]), (wo_hi[:], w_raw[:, :, 3])):
                    act.activation(dst, src, ACT.Copy).then_inc(w_hi_r, 1)
            act.wait_ge(job_full, 1)
            nc.scalar.activation(coef[:], ps_j[:, 0:4 * KC * B], ACT.Copy).then_inc(job_free, 1)

            def y_copy(nb, k, no, reuse):
                act.wait_ge(job_full, no + 1)
                if reuse:
                    act.wait_ge(n_r, 4 * nb)
                cf = coef[:, :, k:k + 1, bass.ds(nb, 1)].rearrange("p i k b -> p i (k b)")
                act.activation(y_n[:, k, :], ps_j[:], ACT.Identity, scale=cf[:, 0], bias=cf[:, 1])\
                   .then_inc(job_free, 1)

            def qk_copy(nb, i, no, reuse):
                act.wait_ge(job_full, no + 1)
                if reuse:
                    act.wait_ge(scr_w, 96 * (2 * (nb - 1) + i // 2 + 1))
                act.activation(qk_hi[:, i, :], ps_j[:] if reuse else ps_s[:, i], ACT.Copy).then_inc(qk_hi_r, 1)

            def v_evac(nb, w, no, reuse):
                act.wait_ge(job_full, no + 1)
                if reuse:
                    act.wait_ge(v_in, 64 * nb)
                for t in (2 * w, 2 * w + 1):
                    src = ps_j[:, D * (t % 2):D * (t % 2) + D].rearrange("p (g i d) -> p g i d", g=NG, i=HG)
                    act.activation(v_st[:, :, t, :, 0:DH], src, ACT.Copy).then_inc(v_r, 1)
                act.wait_ge(v_r, TT * nb + 2 * w + 2)
                act.sem_inc(job_free, 1)

            def exps(b, u, warm):
                n = UNITS * b + u
                for h in range(2):
                    act.wait_ge(s_full, 2 * n + h + 1)
                    if warm:
                        act.wait_ge(av_done, n - 1)
                    act.activation(prob[:, u % 2, 2 * h:2 * h + 2, :], ps_s[:, 2 * h:2 * h + 2, :], ACT.Exp,
                                   scale=SCALE).then_inc(p_r, 1)

            def o_evac(b, g, reuse):
                n = NG * b + g
                act.wait_ge(av_done, TT * (n + 1))
                if reuse:
                    act.wait_ge(ow_w, 16 * (n - 1))
                act.activation(o_raw[:, g % 2, :], ps_o[:], ACT.Copy).then_inc(o_r, 1)

            def o_write(b, g):
                act.wait_ge(o_r, NG * b + g + 1)
                act.dma_start(o_d[g // 2, g % 2], o_raw[:, g % 2, :]).then_inc(ow_w, 16)

            def o_read(b, c, fresh):
                act.wait_ge(ow_w, 16 * (NG * b + 2 * c + 2))
                if not fresh:
                    act.wait_ge(olo_r, 2 * (b - 1) + c + 1)
                if not (fresh and c == 0):
                    act.wait_ge(omul_r, 2 * b + c)
                act.dma_start(d_s[:, c, :], o_d[c].rearrange("g (i r) (e n) -> (g i) r e n", r=2 * DH, n=DS)[:, DH])\
                   .then_inc(den_in, 16)
                rows = o_d[c].rearrange("g (i k d) n -> k (g i) d n", i=HG, k=2)
                act.dma_start(o_c[:, c, :], rows[0]).then_inc(oc_in, 16)

            def rec_write(b, c):
                act.wait_ge(rec_r, 2 * b + c + 1)
                act.dma_start(r_d[c].rearrange("(p n) -> p n", n=DS), d_s[:, c, :]).then_inc(rec_w, 16)

            def rec_read(b, c):
                act.wait_ge(rec_w, 16 * (2 * b + c + 1))
                act.dma_start(d_c[:, c, :], r_d[c].rearrange("(h r n) -> h r n", r=1, n=T)
                              .broadcast_to([NH // 2, DH, T])).then_inc(rec_in, 16)

            def squares2(b, tiles):
                for t in tiles:
                    act.wait_ge(x1_r, 2 * b + 1 + t // 2)
                    if t > 0:
                        act.wait_ge(sq2, TT * b + t)
                    col = ss2[:, bass.ds(b, 1), t:t + 1].rearrange("p a b -> p (a b)")
                    act.activation(junk[:], x_all[:, bass.ds(b, 1), t, :].rearrange("p a n -> p (a n)"), ACT.Square,
                                   scale=1.0 / DH, accum_out=col).then_inc(sq2, 1)

            def job(nb, op, no, reuse):
                if op in ("TR0", "TR1"):
                    y_copy(nb, int(op[2]), no, reuse)
                elif op[0] in "QK":
                    qk_copy(nb, 2 * int(op[1]) + "QK".index(op[0]), no, reuse)
                elif op[0] == "V":
                    v_evac(nb, int(op[1]), no, reuse)

            for no, op in enumerate(PRO):
                job(0, op, no, False)
            act.wait_ge(x1_in, 16)
            for n in range(TT, 2 * TT):
                square1(n)
            act.wait_ge(ms1, 2)
            act.activation(ss1[:, TT:2 * TT], ss1[:, TT:2 * TT], ACT.Sqrt).then_inc(root1, 1)
            for k in range(TAB):
                for q in range(B // 2):
                    n = (B // 2) * k + q
                    act.wait_ge(tab_full, n + 1)
                    act.activation(tab[:, k, 2 * q:2 * q + 2, :], ps_s[:, n % HG, :],
                                   ACT.Tanh if k == 2 else ACT.Copy).then_inc(tab_r, 1)
            act.wait_ge(pad_written, 64)

            def batch(b, first, last, second=False):
                jobs = jobs_of(first, last)
                for u in range(UNITS):
                    exps(b, u, not (first and u < 2))
                    if u in jobs:
                        job(b + 1, jobs[u], job_no(b, first, last, jobs[u]), True)
                    if u % TT == 0 and not (first and u == 0):
                        o_evac(b - (u == 0), (u // TT - 1) % NG, not (first and u < 12))
                    if u % TT == 1 and not (first and u == 1) and not (last and u == 13):
                        o_write(b - (u == 1), (u // TT - 1) % NG)
                    if u == 2 and not first:
                        o_read(b - 1, 1, second)
                    if u == 5 and not first:
                        rec_write(b - 1, 1)
                    if u == 6 and not first:
                        rec_read(b - 1, 1)
                    if u == 10:
                        o_read(b, 0, first)
                    if u == 13:
                        rec_write(b, 0)
                    if u == 14:
                        rec_read(b, 0)
                    if u == 2 and not (first or second):
                        squares2(b - 2, (2, 3))
                    if u == 15 and not first:
                        squares2(b - 1, (0, 1))
                    if first and 2 <= u < 14:
                        if u == 2:
                            act.wait_ge(x_in, 16 * (B - 2))
                        for n in (2 * (u + 2), 2 * (u + 2) + 1):
                            square1(n)
                    if last and u == 11:
                        act.wait_ge(ms2, 1)
                        act.activation(rstd2[:, 0:RT], rstd2[:, 0:RT], ACT.Sqrt).then_inc(root2, 1)
                    if first and u == 14:
                        act.wait_ge(ms1, 3)
                        act.activation(ss1[:, 2 * TT:], ss1[:, 2 * TT:], ACT.Sqrt).then_inc(root1, 1)

            batch(0, True, False)
            with act.Fori(1, 2) as b:
                batch(b, False, False, True)
            with act.Fori(2, B - 1) as b:
                batch(b, False, False)
            batch(B - 1, False, True)
            o_evac(B - 1, 3, True)
            squares2(B - 2, (2, 3))

        @block.vector
        def _(dve):
            dve.wait_ge(sq1, TT)
            dve.tensor_scalar(ss1[:, 0:TT], ss1[:, 0:TT], EPS_RMS, None, ALU.add).then_inc(ms1, 1)
            dve.wait_ge(root1, 1)
            dve.reciprocal(rstd1[:, 0:TT], ss1[:, 0:TT]).then_inc(rstd_r, 1)

            def norm(nb, reuse):
                if reuse:
                    dve.wait_ge(y_done[0], y_done[1])
                for t in range(TT):
                    xs = x_all[:, bass.ds(nb, 1), t, :].rearrange("p a n -> p (a n)")
                    dve.tensor_scalar(xhat[:, t, :], xs, rstd1[:, bass.ds(TT * nb + t, 1)], None, ALU.mult)\
                       .then_inc(xhat_r, 1)

            y_done = [None, None]
            dve.wait_ge(rstd_r, 1)
            norm(0, False)
            dve.wait_ge(small_in, 16 * 9)
            dve.wait_ge(consts, 2)
            dve.tensor_copy(cond_rep[:], cond[:].unsqueeze(2).broadcast_to([DT + 1, B, P])).then_inc(rep_ready, 1)

            def w_low(n, low, high, src):
                dve.wait_ge(w_hi_r, n)
                dve.tensor_tensor(low, src, high.bitcast(F32), ALU.subtract).then_inc(w_lo_r, 1)

            w_low(1, w_lo[:, :, 0:2], w_hi[:, :, 0:2], w_raw[:, :, 0:2])

            def split_n(nb, k, no, last_read):
                dve.wait_ge(job_free, no + 1)
                if last_read is not None:
                    dve.wait_ge(job_full, last_read + 1)
                dve.tensor_copy(n_hi[:, k, :], y_n[:, k, :]).then_inc(n_r, 1)
                dve.wait_ge(n_r, 4 * nb + 2 * k + 1)
                dve.tensor_tensor(n_lo[:, k, :], y_n[:, k, :], n_hi[:, k, :].bitcast(F32), ALU.subtract)\
                   .then_inc(n_r, 1)

            def qk_low(nb, i, no, reuse):
                dve.wait_ge(qk_hi_r, 4 * nb + i + 1)
                if reuse:
                    dve.wait_ge(scr_w, 96 * (2 * (nb - 1) + i // 2 + 1))
                dve.tensor_tensor(qk_lo[:, i, :], ps_j[:] if reuse else ps_s[:, i], qk_hi[:, i, :].bitcast(F32), ALU.subtract)\
                   .then_inc(qk_lo_r, 1)
                dve.wait_ge(qk_lo_r, 4 * nb + i + 1)
                dve.sem_inc(job_free, 1)

            def max_parts(b, g, no):
                n = NG * b + g
                src = ps_j[0:2 * HG * 2, 0:P]
                dve.wait_ge(job_full, no + 1)
                if not (isinstance(n, int) and n == 0):
                    dve.wait_ge(m_in, 64 * n)
                dve.tensor_scalar(m_hl[:, 0, :], src, -1.0, None, ALU.mult).then_inc(m_r, 1)
                dve.wait_ge(m_r, 2 * n + 1)
                dve.scalar_tensor_tensor(out=m_hl[:, 1, :], in0=src, scalar=-1.0, in1=m_hl[:, 0, :].bitcast(F32),
                                         op0=ALU.mult, op1=ALU.subtract).then_inc(m_r, 1)
                dve.wait_ge(m_r, 2 * n + 2)
                dve.sem_inc(job_free, 1)

            def wo_scale(b, w, no, reuse):
                dve.wait_ge(job_full, no + 1)
                if reuse:
                    dve.wait_ge(x1_r, 2 * (b - 1) + w + 1)
                al = tab[:, 0, bass.ds(b, 1), :].broadcast_to([P, 2, D])
                dve.tensor_tensor(wo_t[:, w], ps_j[:].rearrange("p (t n) -> p t n", t=2), al, ALU.mult)\
                   .then_inc(job_free, 1)

            def o_recip(b, c):
                dve.wait_ge(den_in, 16 * (2 * b + c + 1))
                dve.reciprocal(d_s[:, c, :], d_s[:, c, :]).then_inc(rec_r, 1)

            def o_high(b, c, last_read):
                if last_read is not None:
                    dve.wait_ge(job_full, last_read + 1)
                dve.wait_ge(omul_r, 2 * b + c + 1)
                dve.tensor_copy(on_hi[:, c, :], o_c[:, c, :]).then_inc(ohi_r, 1)

            def reduce_max(b, g, qt, i, free):
                n = UNITS * HG // NG * (NG * b + g) + HG * qt + i
                dve.wait_ge(mx_full, n + 1)
                if free is not None:
                    dve.wait_ge(job_full, free + 1)
                dve.tensor_reduce(mx[:, g % 2, i % 2, i // 2, qt:qt + 1], ps_m[:, i % 2, :], AX.X, ALU.max)\
                   .then_inc(mx_red, 1)

            for k in range(2):
                split_n(0, k, PRO.index(f"TR{k}"), None)
            w_low(2, w_lo[:, :, 2], w_hi[:, :, 2], w_raw[:, :, 2])
            w_low(3, wo_lo[:], wo_hi[:], w_raw[:, :, 3])
            for i, op in enumerate(("Q0", "K0", "Q1", "K1")):
                qk_low(0, i, PRO.index(op), False)
            dve.wait_ge(sq1, 2 * TT)
            dve.tensor_scalar(ss1[:, TT:2 * TT], ss1[:, TT:2 * TT], EPS_RMS, None, ALU.add).then_inc(ms1, 1)
            for g in range(2):
                for qt in range(TT):
                    for i in range(HG):
                        reduce_max(0, g, qt, i, None)
                if g == 0:
                    max_parts(0, 0, PRO.index("MT0"))
                    dve.wait_ge(root1, 2)
                    dve.reciprocal(rstd1[:, TT:2 * TT], ss1[:, TT:2 * TT]).then_inc(rstd_r, 1)
            dve.wait_ge(rstd_r, 2)

            def batch(b, first, last, second):
                jobs = jobs_of(first, last)
                for u in range(UNITS):
                    g, qt = (u // TT + 2) % NG, u % TT
                    gb = b + (u // TT + 2) // NG
                    live = not (last and u >= UNITS // 2)
                    if u == 0 and not last:
                        y_done[0], y_done[1] = job_full, job_base(b, first)
                        norm(b + 1, True)
                    if live:
                        for i in (0, 1):
                            if u // TT < 2:
                                free = job_base(b, first) - (1 if u // TT == 0 else 0)
                            else:
                                free = job_no(b, first, last, "MT2" if u // TT == 2 else "MT3")
                            reduce_max(gb, g, qt, i, free if (qt == 0 and i == 0) else None)
                    op = jobs.get(u - 1)
                    if u > 0 and op is not None:
                        no = job_no(b, first, last, op)
                        if op in ("TR0", "TR1"):
                            split_n(b + 1, int(op[2]), no, job_base(b, first) - 1)
                        elif op[0] in "QK":
                            qk_low(b + 1, 2 * int(op[1]) + "QK".index(op[0]), no, True)
                        elif op in PREV:
                            wo_scale(b - 1, int(op[2]), no, not second)
                    if live:
                        for i in (2, 3):
                            reduce_max(gb, g, qt, i, None)
                    op = jobs.get(u)
                    if op is not None and op[0:2] == "MT":
                        g_m = int(op[2])
                        max_parts(b + (g_m == 0), g_m, job_no(b, first, last, op))
                    if not first:
                        before = None if second else job_no_prev(b)
                        if u == 1:
                            o_high(b - 1, 0, before)
                        if u == 4:
                            o_recip(b - 1, 1)
                        if u == 9:
                            o_high(b - 1, 1, before)
                    if u == 12:
                        o_recip(b, 0)
                    if last and u == 10:
                        dve.wait_ge(sq2, RT)
                        dve.tensor_scalar(rstd2[:, 0:RT], ss2[:].rearrange("p b t -> p (b t)")[:, 0:RT], EPS_RMS, None,
                                          ALU.add).then_inc(ms2, 1)
                    if last and u == 13:
                        dve.wait_ge(root2, 1)
                        dve.reciprocal(rstd2[:, 0:RT], rstd2[:, 0:RT]).then_inc(rstd2_r, 1)
                    if first and u == 14:
                        dve.wait_ge(sq1, B * TT)
                        dve.tensor_scalar(ss1[:, 2 * TT:], ss1[:, 2 * TT:], EPS_RMS, None, ALU.add).then_inc(ms1, 1)
                    if first and u == 15:
                        dve.wait_ge(root1, 3)
                        dve.reciprocal(rstd1[:, 2 * TT:], ss1[:, 2 * TT:]).then_inc(rstd_r, 1)
                        dve.wait_ge(rstd_r, 3)

            def job_no_prev(b):
                return job_no(b - 1, False, False, "WO1")

            batch(0, True, False, False)
            with dve.Fori(1, 2) as b:
                batch(b, False, False, True)
            with dve.Fori(2, B - 1) as b:
                batch(b, False, False, False)
            batch(B - 1, False, True, False)
            o_high(B - 1, 0, job_no(B - 1, False, True, "WO1"))

        @block.tensor
        def _(pe):
            def job_wait(no):
                if not (isinstance(no, int) and no == 0):
                    pe.wait_ge(job_free, no)

            pe.wait_ge(small_in, 16 * 9)
            pe.wait_ge(consts, 6)
            n = 0
            for i in range(4):
                for k in range(KC):
                    mm = pe.matmul(ps_j[:, n * B:(n + 1) * B], ada_w[0:DT, i, k * P:(k + 1) * P], cond[0:DT, :],
                                   start=(n == 0), stop=True, skip_group_check=True)
                    n += 1
            mm.then_inc(job_full, 1)

            def transposes(nb, k, no):
                job_wait(no)
                pe.wait_ge(xhat_r, TT * (nb + 1))
                for t in range(TT):
                    mm = pe.transpose(ps_j[:, t * P:(t + 1) * P], xhat[:, t, k * P:(k + 1) * P], ident[:])
                mm.then_inc(job_full, 1)

            def split_product(out, lhs, rhs, inc=None):
                steps = [(a, c, k) for k in range(KC) for a, c in ((0, 0), (1, 0), (0, 1))]
                for n, (a, c, k) in enumerate(steps):
                    mm = pe.matmul(out, lhs(a, k), rhs(c, k), start=(n == 0), stop=(n == len(steps) - 1))
                return mm

            W, WO, N, O = (w_hi, w_lo), (wo_hi, wo_lo), (n_hi, n_lo), (on_hi, on_lo)

            def project_qk(nb, op, no, bank=None):
                if bank is None:
                    job_wait(no)
                pe.wait_ge(n_r, 4 * (nb + 1))
                i, c = "QK".index(op[0]), int(op[1])
                split_product(ps_j[:] if bank is None else ps_s[:, bank], lambda a, k: W[a][:, k, i, c * P:(c + 1) * P], lambda a, k: N[a][:, k, :])\
                    .then_inc(job_full, 1)

            def project_v(nb, w, no):
                job_wait(no)
                pe.wait_ge(n_r, 4 * (nb + 1))
                for t in (2 * w, 2 * w + 1):
                    mm = split_product(ps_j[:, D * (t % 2):D * (t % 2 + 1)],
                                       lambda a, k: N[a][:, k, t * P:(t + 1) * P], lambda a, k: W[a][:, k, 2, :])
                mm.then_inc(job_full, 1)

            def project_o(b, w, no):
                job_wait(no)
                pe.wait_ge(olo_r, 2 * (b + 1))
                for t in (2 * w, 2 * w + 1):
                    mm = split_product(ps_j[:, D * (t % 2):D * (t % 2 + 1)],
                                       lambda a, k: O[a][:, k, t * P:(t + 1) * P], lambda a, k: WO[a][:, k, :])
                mm.then_inc(job_full, 1)

            def max_transpose(b, g, no):
                job_wait(no)
                pe.wait_ge(mx_red, UNITS * (NG * b + g + 1))
                pe.transpose(ps_j[0:2 * HG * 2, 0:P], mx[:, g % 2].rearrange("p s j t -> p (s j t)"), ident[:])\
                  .then_inc(job_full, 1)

            def max_scores(b, g, qt, i, fresh):
                n = UNITS * (NG * b + g) + HG * qt + i
                if qt == 0 and i == 0:
                    pe.wait_ge(stack_in, 32 * (NG * b + g + 1))
                if not fresh:
                    pe.wait_ge(mx_red, n - 1)
                j, r = i // 2, 64 * (i % 2)
                pe.matmul(ps_m[:, i % 2, :], qs[r:r + 64, g, j, qt * P:(qt + 1) * P], ks[r:r + 64, g, j, :],
                          start=True, stop=True).then_inc(mx_full, 1)

            def scores(b, g, kb, i, fresh):
                n = UNITS * b + TT * g + kb
                if kb == 0 and i == 0:
                    pe.wait_ge(m_in, 64 * (NG * b + g + 1))
                if not fresh and i % 2 == 0:
                    pe.wait_ge(p_r, 2 * n - 1 + i // 2)
                j, r = i // 2, 64 * (i % 2)
                mm = pe.matmul(ps_s[:, i, :], ks[r:r + 64, g, j, kb * P:(kb + 1) * P], qs[r:r + 64, g, j, :],
                               start=True, stop=True)
                if i % 2 == 1:
                    mm.then_inc(s_full, 1)

            def attend(b, u, fresh):
                g, kb = u // TT, u % TT
                pe.wait_ge(p_r, 2 * (UNITS * b + u + 1))
                if kb == 0:
                    pe.wait_ge(v_in, 16 * (NG * b + g + 1))
                    if not fresh:
                        pe.wait_ge(o_r, NG * b + g)
                for i in range(HG):
                    mm = pe.matmul(ps_o[32 * i:32 * i + 32, :], v[:, g, kb, i, :], prob[:, u % 2, i, :],
                                   start=(kb == 0), stop=(kb == TT - 1), skip_group_check=True)
                mm.then_inc(av_done, 1)

            def job(b, op, no):
                if op[0:2] == "TR":
                    transposes(b, int(op[2]), no)
                elif op[0] in "QK":
                    project_qk(b, op, no)
                elif op[0] == "V":
                    project_v(b, int(op[1]), no)
                elif op[0:2] == "MT":
                    max_transpose(b, int(op[2]), no)
                else:
                    project_o(b, int(op[2]), no)

            for k in range(KC):
                transposes(0, k, PRO.index(f"TR{k}"))
            pe.wait_ge(w_lo_r, 1)
            for bank, op in enumerate(("Q0", "K0", "Q1", "K1")):
                project_qk(0, op, PRO.index(op), bank)
            pe.wait_ge(w_lo_r, 3)
            for w in range(2):
                project_v(0, w, PRO.index(f"V{w}"))

            def table(n):
                k, q = n // (B // 2), n % (B // 2)
                rows = DT + (k == 2)
                if n >= HG:
                    pe.wait_ge(tab_r, n - HG + 1)
                for e in range(2):
                    mm = pe.matmul(ps_s[:, n % HG, D * e:D * (e + 1)], cond_rep[0:rows, 2 * q + e, :],
                                   ada_w[0:rows, 4 + k, :], start=True, stop=True)
                mm.then_inc(tab_full, 1)

            pe.wait_ge(rep_ready, 1)
            for n in range(HG):
                table(n)
            for g in range(2):
                for qt in range(TT):
                    for i in range(HG):
                        max_scores(0, g, qt, i, g == 0 and qt == 0 and i < 2)
                    if HG + TT * g + qt < TAB * B // 2:
                        table(HG + TT * g + qt)
                if g == 0:
                    max_transpose(0, 0, PRO.index("MT0"))
            pe.wait_ge(tab_r, TAB * B // 2)

            def batch(b, first, last):
                jobs = jobs_of(first, last)
                for u in range(UNITS):
                    g, kb = u // TT, u % TT
                    for step in ORDER:
                        if step[0] == "S":
                            scores(b, g, kb, int(step[1]), first and u == 0)
                        elif step[0] == "M" and not (last and g >= 2):
                            max_scores(b + (g + 2) // NG, (g + 2) % NG, kb, int(step[1]), False)
                        elif step == "A" and u > 0:
                            attend(b, u - 1, first and u == 1)
                        elif step == "A" and not first:
                            attend(b - 1, UNITS - 1, False)
                        elif step == "J" and u in jobs:
                            op = jobs[u]
                            job(b if op in OWN else b - 1 if op in PREV else b + 1, op, job_no(b, first, last, op))

            batch(0, True, False)
            with pe.Fori(1, B - 1) as b:
                batch(b, False, False)
            batch(B - 1, False, True)
            attend(B - 1, UNITS - 1, False)


def ffn_phase(nc, dram, tensors):
    x_all, tab, coef, ident, ss2, rstd2 = (tensors[k] for k in ("x_all", "tab", "coef", "ident", "ss2", "rstd2"))
    wo_hi, wo_lo, o_raw, o_c, d_c, on_hi, on_lo, wo_t, raw = (
        tensors[k] for k in ("wo_hi", "wo_lo", "o_raw", "o_c", "d_c", "on_hi", "on_lo", "wo_t", "raw"))
    HJ = JC // 2
    LB = B - 1
    with ExitStack() as ctx:
        def sb(name, shape, dt=F32):
            return ctx.enter_context(nc.sbuf_tensor(name, shape, dt))

        def sem(name):
            return ctx.enter_context(nc.semaphore(name))

        gh_raw = raw[:].rearrange("p (k i n) -> p k i n", k=KC, i=2)
        z = raw[:, 0:2 * TT * D].rearrange("p (u t n) -> p u t n", u=2, t=TT)
        f_t = raw[:, 2 * TT * D:3 * TT * D].rearrange("p (t n) -> p t n", t=TT)
        rows = raw[:, 3 * TT * D:].rearrange("p (i n) -> p i n", n=D)
        ow_raw = (sb("ow_raw", [P, JC // 2, D]), o_raw[:].rearrange("p g (j n) -> p (g j) n", n=D))
        junk = wo_t[:, 0, 0, :]
        gh_hi = sb("gh_hi", [P, KC, 2, HID], F32R)
        gh_lo = sb("gh_lo", [P, KC, 2, HID], F32R)
        ow_hi = sb("ow_hi", [P, JC, D], F32R)
        ow_lo = sb("ow_lo", [P, JC, D], F32R)
        xhat = sb("f_xhat", [P, TT, D])
        y_n = sb("f_y_n", [P, KC, T])
        n_hi = sb("f_n_hi", [P, 2, KC, T], F32R)
        n_lo = sb("f_n_lo", [P, 2, KC, T], F32R)
        sil = sb("sil", [P, 2, T])
        act_y = (o_c[:, 0, :], d_c[:, 0, :])
        a_hi = sb("a_hi", [P, 4, T], F32R)
        a_lo = sb("a_lo", [P, 4, T], F32R)
        st = sb("st", [P, TT, 6])
        mv = sb("mv", [P, TT, 2])
        sd = sb("sd", [P, TT])
        o_d = nc.dram_tensor("tail_scratch", (2, P, T), F32, kind="Internal").ap()
        ps_g = ctx.enter_context(nc.psum_tensor("ps_g", [P, 2, T], F32))
        ps_h = ctx.enter_context(nc.psum_tensor("ps_h", [P, 2, T], F32))
        ps_t = ctx.enter_context(nc.psum_tensor("ps_t", [P, KC, T], F32))
        ps_f = ctx.enter_context(nc.psum_tensor("ps_f", [P, TT, D], F32))

        ow_in = sem("ow_in"); rows_in = sem("rows_in")
        gh_hi_r = sem("gh_hi_r"); gh_lo_r = sem("gh_lo_r"); ow_hi_r = sem("ow_hi_r"); ow_lo_r = sem("ow_lo_r")
        ms2 = sem("f_ms2"); root2 = sem("f_root2"); rstd2_r = sem("f_rstd2_r"); rows_r = sem("rows_r")
        ow_w = sem("f_ow_w"); oc_in = sem("f_oc_in"); on_r = sem("f_on_r"); wo_full = sem("wo_full")
        wo_used = sem("wo_used"); x1_r = sem("f_x1_r"); sq2 = sem("f_sq2")
        xhat_r = sem("f_xhat_r"); tr_full = sem("tr_full"); y_r = sem("f_y_r"); n_r = sem("f_n_r")
        gh_full = sem("gh_full"); sil_r = sem("sil_r"); act_r = sem("act_r"); a_hi_r = sem("a_hi_r")
        a_lo_r = sem("a_lo_r"); out_used = sem("out_used"); f_add = sem("f_add")
        f_mul = sem("f_mul"); x2_r = sem("x2_r"); stat_r = sem("stat_r"); sd_r = sem("sd_r"); rs_r = sem("rs_r")
        mul_begun = sem("mul_begun"); shift_r = sem("shift_r"); sp_waited = sem("f_sp_waited"); z_r = sem("z_r"); stored = sem("stored")

        block = ctx.enter_context(nc.Block())

        @block.sync
        def _(sp):
            ow_halves = dram["out_w"].rearrange("(h j p) n -> h p j n", h=2, p=P)
            sp.dma_start(ow_raw[0][:], ow_halves[0]).then_inc(ow_in, 16)
            sp.dma_start(o_d.rearrange("g p n -> p g n"), o_raw[:]).then_inc(ow_w, 16)
            sp.wait_ge(ow_w, 16)
            parts = o_d.rearrange("g (i k d) n -> k (g i) d n", i=HG, k=2)
            for k, dst in enumerate((o_c, d_c)):
                sp.dma_start(dst[:, 1, :], parts[k]).then_inc(oc_in, 16)
            sp.wait_ge(ow_in, 16)
            sp.dma_start(ow_raw[1], ow_halves[1]).then_inc(ow_in, 16)
            sp.wait_ge(gh_lo_r, JC)
            for i, name in ((0, "out_b"), (1, "l1_w"), (3, "l1_b")):
                sp.dma_start(rows[:, i, :], dram[name].partition_broadcast(P)).then_inc(rows_in, 16)

            def batch(b, par):
                sp.wait_ge(z_r, 6 * (b + 1))
                sp.sem_inc(sp_waited, 1)
                sp.dma_start(dram["out"][bass.ds(b, 1)].rearrange("a p t n -> p (a t) n"), z[:, par]).then_inc(stored, 16)
                sp.wait_ge(stored, 16 * (b + 1))
                sp.sem_inc(sp_waited, 1)

            with sp.Fori(0, B // 2) as i:
                batch(2 * i, 0)
                batch(2 * i + 1, 1)

        @block.scalar
        def _(act):
            def split_high(j):
                cols = slice(j * P, (j + 1) * P)
                act.activation(gh_hi[:, :, :, cols], gh_raw[:, :, :, cols], ACT.Copy).then_inc(gh_hi_r, 1)
                act.wait_ge(ow_in, 16 * (j // HJ + 1))
                act.activation(ow_hi[:, j, :], ow_raw[j // HJ][:, j % HJ, :], ACT.Copy).then_inc(ow_hi_r, 1)

            split_high(0)

            def y_copy(b):
                for k in range(KC):
                    act.wait_ge(tr_full, KC * b + k + 1)
                    if not (isinstance(b, int) and b == 0):
                        act.wait_ge(n_r, 4 * b)
                    cf = coef[:, :, k:k + 1, bass.ds(b, 1)].rearrange("p i k b -> p i (k b)")
                    act.activation(y_n[:, k, :], ps_t[:, k, :], ACT.Identity, scale=cf[:, 2], bias=cf[:, 3])\
                       .then_inc(y_r, 1)

            def silu(n, j, fresh):
                act.wait_ge(gh_full, 2 * n + 1)
                if not fresh:
                    act.wait_ge(act_r, n - 1)
                act.activation(sil[:, j % 2, :], ps_g[:, j % 2, :], ACT.Silu).then_inc(sil_r, 1)

            def high(n, j, fresh):
                act.wait_ge(act_r, n + 1)
                if not fresh:
                    act.wait_ge(out_used, n - 3)
                act.activation(a_hi[:, j % 4, :], act_y[j % 2], ACT.Copy).then_inc(a_hi_r, 1)

            def deviation(b):
                act.wait_ge(stat_r, 9 * b + 9)
                act.activation(sd[:], sd[:], ACT.Sqrt).then_inc(sd_r, 1)

            y_copy(0)
            split_high(1)

            def batch(b, first, last):
                for j in range(JC):
                    n = JC * b + j
                    silu(n, j, first and j < 2)
                    if j > 0:
                        high(n - 1, j - 1, first and j <= 4)
                    elif not first:
                        high(n - 1, JC - 1, False)
                    if first and j + 2 < JC:
                        split_high(j + 2)
                    if j == 4 and not last:
                        y_copy(b + 1)
                    if isinstance(b, int) and b == 1 and j in (1, 2):
                        for t in (2 * j - 2, 2 * j - 1):
                            act.wait_ge(x1_r, j)
                            if t > 0:
                                act.wait_ge(sq2, t)
                            act.activation(junk, x_all[:, LB, t, :], ACT.Square, scale=1.0 / DH,
                                           accum_out=ss2[:, LB, t:t + 1]).then_inc(sq2, 1)
                    if j == 5 and not first:
                        deviation(b - 1)
                        if isinstance(b, int) and b == 1:
                            act.wait_ge(ms2, 1)
                            act.activation(rstd2[:, RT:], rstd2[:, RT:], ACT.Sqrt).then_inc(root2, 1)

            batch(0, True, False)
            batch(1, False, False)
            with act.Fori(2, B - 1) as b:
                batch(b, False, False)
            batch(B - 1, False, True)
            high(JC * B - 1, JC - 1, False)
            deviation(B - 1)

        @block.vector
        def _(dve):
            def norm(b, fresh):
                if not fresh:
                    dve.wait_ge(tr_full, KC * b)
                for t in range(TT):
                    xs = x_all[:, bass.ds(b, 1), t, :].rearrange("p a n -> p (a n)")
                    dve.tensor_scalar(xhat[:, t, :], xs, rstd2[:, bass.ds(TT * b + t, 1)], None, ALU.mult)\
                       .then_inc(xhat_r, 1)

            def split_low(j):
                cols = slice(j * P, (j + 1) * P)
                dve.wait_ge(gh_hi_r, j + 1)
                dve.tensor_tensor(gh_lo[:, :, :, cols], gh_raw[:, :, :, cols], gh_hi[:, :, :, cols].bitcast(F32),
                                  ALU.subtract).then_inc(gh_lo_r, 1)
                dve.wait_ge(ow_hi_r, j + 1)
                dve.tensor_tensor(ow_lo[:, j, :], ow_raw[j // HJ][:, j % HJ, :], ow_hi[:, j, :].bitcast(F32), ALU.subtract)\
                   .then_inc(ow_lo_r, 1)

            norm(0, True)
            split_low(0)

            def split_n(b, par, fresh):
                for k in range(KC):
                    dve.wait_ge(y_r, KC * b + k + 1)
                    if not fresh:
                        dve.wait_ge(gh_full, 2 * JC * (b - 1))
                    dve.tensor_copy(n_hi[:, par, k, :], y_n[:, k, :]).then_inc(n_r, 1)
                    dve.wait_ge(n_r, 4 * b + 2 * k + 1)
                    dve.tensor_tensor(n_lo[:, par, k, :], y_n[:, k, :], n_hi[:, par, k, :].bitcast(F32), ALU.subtract)\
                       .then_inc(n_r, 1)

            split_n(0, 0, True)
            split_low(1)
            def gate(n, j, fresh):
                dve.wait_ge(sil_r, n + 1)
                dve.wait_ge(gh_full, 2 * n + 2)
                if not fresh:
                    dve.wait_ge(a_lo_r, n - 1)
                dve.tensor_tensor(act_y[j % 2], ps_h[:, j % 2, :], sil[:, j % 2, :], ALU.mult).then_inc(act_r, 1)

            def low(n, j, fresh):
                dve.wait_ge(a_hi_r, n + 1)
                if not fresh:
                    dve.wait_ge(out_used, n - 3)
                dve.tensor_tensor(a_lo[:, j % 4, :], act_y[j % 2], a_hi[:, j % 4, :].bitcast(F32), ALU.subtract)\
                   .then_inc(a_lo_r, 1)

            def add_bias(b, fresh):
                dve.wait_ge(out_used, JC * (b + 1))
                if not fresh:
                    dve.wait_ge(x2_r, 2 * b)
                for w in range(2):
                    dve.tensor_tensor(f_t[:, 2 * w:2 * w + 2], ps_f[:, 2 * w:2 * w + 2],
                                      rows[:, 0:1, :].broadcast_to([P, 2, D]), ALU.add).then_inc(f_add, 1)

            def stats(b):
                for w in range(2):
                    dve.wait_ge(f_mul, 2 * b + w + 1)
                    xs = x_all[:, bass.ds(b, 1), 2 * w:2 * w + 2, :].rearrange("p a t n -> p (a t) n")
                    dve.tensor_tensor(xs, xs, f_t[:, 2 * w:2 * w + 2], ALU.add).then_inc(x2_r, 1)
                for t in range(TT):
                    dve.wait_ge(x2_r, 2 * b + t // 2 + 1)
                    xs = x_all[:, bass.ds(b, 1), t, :].rearrange("p a n -> p (a n)")
                    dve.bn_stats(st[:, t, :], xs).then_inc(stat_r, 1)
                for t in range(TT):
                    dve.wait_ge(stat_r, 9 * b + t + 1)
                    dve.bn_aggr(mv[:, t, :], st[:, t, :]).then_inc(stat_r, 1)
                dve.wait_ge(stat_r, 9 * b + 8)
                dve.tensor_scalar(sd[:], mv[:, :, 1], EPS_LN, None, ALU.add).then_inc(stat_r, 1)

            def layer_norm(b, par, fresh):
                dve.wait_ge(sd_r, b + 1)
                dve.reciprocal(sd[:], sd[:]).then_inc(rs_r, 1)
                dve.wait_ge(rs_r, b + 1)
                if not fresh:
                    dve.wait_ge(stored, 16 * (b - 1))
                for t in range(TT):
                    xs = x_all[:, bass.ds(b, 1), t, :].rearrange("p a n -> p (a n)")
                    dve.tensor_scalar(z[:, par, t, :], xs, mv[:, t, 0:1], sd[:, t:t + 1], ALU.subtract, ALU.mult)\
                       .then_inc(z_r, 1)
                dve.wait_ge(z_r, 6 * b + 4)
                zz = z[:, par]
                dve.tensor_tensor(zz, zz, rows[:, 2:3, :].broadcast_to([P, TT, D]), ALU.mult).then_inc(z_r, 1)
                dve.wait_ge(z_r, 6 * b + 5)
                if not (isinstance(b, int) and b > 0):
                    dve.wait_ge(shift_r, 3)
                dve.tensor_tensor(zz, zz, tab[:, 2, bass.ds(b, 1), :].broadcast_to([P, TT, D]), ALU.add).then_inc(z_r, 1)

            def attention_tail(j):
                for q in {1: (0, 1), 2: (2, 3)}.get(j, ()):
                    if q == 0:
                        dve.wait_ge(oc_in, 32)
                    part = d_c[:, 1, q * P:(q + 1) * P]
                    dve.reciprocal(part, part).then_inc(on_r, 1)
                if j == 3:
                    dve.wait_ge(on_r, 4)
                    dve.tensor_tensor(o_c[:, 1, :], o_c[:, 1, :], d_c[:, 1, :], ALU.mult).then_inc(on_r, 1)
                    dve.wait_ge(on_r, 5)
                    dve.tensor_copy(on_hi[:, 1, :], o_c[:, 1, :]).then_inc(on_r, 1)
                    dve.wait_ge(on_r, 6)
                    dve.tensor_tensor(on_lo[:, 1, :], o_c[:, 1, :], on_hi[:, 1, :].bitcast(F32), ALU.subtract)\
                       .then_inc(on_r, 1)
                if j in (6, 7):
                    w = j - 6
                    dve.wait_ge(wo_full, w + 1)
                    al = tab[:, 0, LB:LB + 1, :].broadcast_to([P, 2, D])
                    dve.tensor_tensor(wo_t[:, w], ps_t[:, w].rearrange("p (t n) -> p t n", t=2), al, ALU.mult)\
                       .then_inc(wo_used, 1)

            def first_pair():
                for b in (0, 1):
                    for j in range(JC):
                        n = JC * b + j
                        if j == 1 and b == 1:
                            dve.wait_ge(rows_in, 48)
                            dve.tensor_tensor(rows[:, 2, :], rows[:, 1, :], rows[:, 1, :], ALU.mult).then_inc(rows_r, 1)
                            dve.wait_ge(rows_r, 1)
                        if j == 2 and b == 1:
                            add_bias(0, True)
                        gate(n, j, n < 2)
                        if n > 0:
                            low(n - 1, (j - 1) % JC, n <= 4)
                        if j == 1:
                            norm(b + 1, False)
                        if b == 0:
                            attention_tail(j)
                            if j + 2 < JC:
                                split_low(j + 2)
                        if j == 4 and b == 1:
                            stats(0)
                            dve.wait_ge(sq2, TT)
                            dve.tensor_scalar(rstd2[:, RT:], ss2[:].rearrange("p b t -> p (b t)")[:, RT:], EPS_RMS,
                                              None, ALU.add).then_inc(ms2, 1)
                        if j == 5:
                            split_n(b + 1, 1 - b, b == 0)
                        if j == 6 and b == 1:
                            layer_norm(0, 0, True)
                            dve.wait_ge(root2, 1)
                            dve.reciprocal(rstd2[:, RT:], rstd2[:, RT:]).then_inc(rstd2_r, 1)
                            dve.wait_ge(rstd2_r, 1)

            def next_batch(b, par, fresh, last):
                for j in range(JC):
                    n = JC * b + j
                    if j == 2:
                        add_bias(b - 1, False)
                    gate(n, j, False)
                    low(n - 1, (j - 1) % JC, False)
                    if j == 1 and not last:
                        norm(b + 1, False)
                    if j == 4:
                        stats(b - 1)
                    if j == 5 and not last:
                        split_n(b + 1, 1 - par, False)
                    if j == 6:
                        layer_norm(b - 1, 1 - par, fresh)

            first_pair()
            with dve.Fori(1, 2) as i:
                next_batch(2 * i, 0, True, False)
                next_batch(2 * i + 1, 1, False, False)
            with dve.Fori(2, B // 2 - 1) as i:
                next_batch(2 * i, 0, False, False)
                next_batch(2 * i + 1, 1, False, False)
            next_batch(B - 2, 0, False, False)
            next_batch(B - 1, 1, False, True)
            low(JC * B - 1, JC - 1, False)
            add_bias(B - 1, False)
            stats(B - 1)
            layer_norm(B - 1, 1, False)

        @block.gpsimd
        def _(pool):
            def batch(b):
                for w in range(2):
                    pool.wait_ge(f_add, 2 * b + w + 1)
                    pool.sem_inc(mul_begun, 1)
                    t = f_t[:, 2 * w:2 * w + 2]
                    pool.tensor_tensor(t, t, tab[:, 1, bass.ds(b, 1), :].broadcast_to([P, 2, D]), ALU.mult)\
                        .then_inc(f_mul, 1)

            for w in range(2):
                pool.wait_ge(wo_used, w + 1)
                xs = x_all[:, LB, 2 * w:2 * w + 2, :]
                pool.tensor_tensor(xs, xs, wo_t[:, w], ALU.add).then_inc(x1_r, 1)
            pool.wait_ge(rows_in, 48)
            shift = tab[:, 2]
            wrow, brow = (rows[:, i:i + 1, :].broadcast_to([P, B, D]) for i in (1, 3))
            for n, (row, op) in enumerate(((brow, ALU.add), (wrow, ALU.mult), (brow, ALU.add))):
                pool.tensor_tensor(shift, shift, row, op).then_inc(shift_r, 1)
                pool.wait_ge(shift_r, n + 1)

            with pool.Fori(0, B) as b:
                batch(b)

        @block.tensor
        def _(pe):
            GH, N, OW, A = (gh_hi, gh_lo), (n_hi, n_lo), (ow_hi, ow_lo), (a_hi, a_lo)
            PARTS = ((0, 0), (1, 0), (0, 1))

            def transposes(b, fresh):
                pe.wait_ge(xhat_r, TT * (b + 1))
                if isinstance(b, int) and b == 2:
                    pe.wait_ge(wo_used, 2)
                for k in range(KC):
                    if not fresh:
                        pe.wait_ge(y_r, KC * (b - 1) + k + 1)
                    for t in range(TT):
                        mm = pe.transpose(ps_t[:, k, t * P:(t + 1) * P], xhat[:, t, k * P:(k + 1) * P], ident[:])
                    mm.then_inc(tr_full, 1)

            def gate_hidden(n, par, j, fresh):
                if j == 0:
                    pe.wait_ge(n_r, n // JC * 4 + 4 if isinstance(n, int) else 4 * n_batch[0] + 4)
                for i, (ps, used) in enumerate(((ps_g, sil_r), (ps_h, act_r))):
                    if not fresh:
                        pe.wait_ge(used, n - 1)
                    m = 0
                    for k in range(KC):
                        for a, c in PARTS:
                            mm = pe.matmul(ps[:, j % 2, :], GH[a][:, k, i, j * P:(j + 1) * P], N[c][:, par, k, :],
                                           start=(m == 0), stop=(m == 5))
                            m += 1
                    mm.then_inc(gh_full, 1)

            n_batch = [None]

            def project_out(n, j, b, fresh):
                pe.wait_ge(a_hi_r, n + 1)
                pe.wait_ge(a_lo_r, n + 1)
                if j == 0 and not fresh:
                    pe.wait_ge(f_add, 2 * b)
                for t in range(TT):
                    for m, (a, c) in enumerate(PARTS):
                        mm = pe.matmul(ps_f[:, t, :], A[a][:, j % 4, t * P:(t + 1) * P], OW[c][:, j, :],
                                       start=(j == 0 and m == 0 and t % 2 == 0), stop=(j == JC - 1 and m == 2),
                                       skip_group_check=True)
                mm.then_inc(out_used, 1)

            def project_o(w):
                pe.wait_ge(on_r, 7)
                pe.wait_ge(y_r, 2 * KC)
                for t in (2 * w, 2 * w + 1):
                    m = 0
                    for k in range(KC):
                        for a, c in PARTS:
                            mm = pe.matmul(ps_t[:, w, D * (t % 2):D * (t % 2 + 1)],
                                           (on_hi, on_lo)[a][:, k, t * P:(t + 1) * P], (wo_hi, wo_lo)[c][:, k, :],
                                           start=(m == 0), stop=(m == 5))
                            m += 1
                mm.then_inc(wo_full, 1)

            transposes(0, True)
            LAG = 2

            def batch(b, par, first, last):
                for j in range(JC):
                    n = JC * b + j
                    n_batch[0] = b
                    if first:
                        pe.wait_ge(gh_lo_r, j + 1)
                    gate_hidden(n, par, j, first and j < 2)
                    if j >= LAG:
                        if first:
                            pe.wait_ge(ow_lo_r, j - LAG + 1)
                        project_out(n - LAG, j - LAG, b, first)
                    elif not first:
                        project_out(n - LAG, j - LAG + JC, b - 1, False)
                    if j == 3 and not last:
                        transposes(b + 1, False)
                    if first and j in (5, 6):
                        project_o(j - 5)

            batch(0, 0, True, False)
            batch(1, 1, False, False)
            with pe.Fori(1, B // 2 - 1) as i:
                batch(2 * i, 0, False, False)
                batch(2 * i + 1, 1, False, False)
            batch(B - 2, 0, False, False)
            batch(B - 1, 1, False, True)
            for j in (JC - 2, JC - 1):
                project_out(JC * (B - 1) + j, j, B - 1, False)


def build(nc, dram):
    with ExitStack() as ctx:
        def sb(name, shape, dt=F32):
            return ctx.enter_context(nc.sbuf_tensor(name, shape, dt))

        tensors = {
            "x_all": sb("x_all", [P, B, TT, D]),
            "tab": sb("tab", [P, TAB, B, D]),
            "coef": sb("coef", [P, 4, KC, B]),
            "ident": sb("ident", [P, P]),
            "ss2": sb("ss2", [P, B, TT]),
            "rstd2": sb("rstd2", [P, B * TT]),
            "wo_hi": sb("wo_hi", [P, KC, D], F32R),
            "wo_lo": sb("wo_lo", [P, KC, D], F32R),
            "o_raw": sb("o_raw", [P, 2, T]),
            "o_c": sb("o_c", [P, 2, T]),
            "d_c": sb("d_c", [P, 2, T]),
            "on_hi": sb("on_hi", [P, 2, T], F32R),
            "on_lo": sb("on_lo", [P, 2, T], F32R),
            "wo_t": sb("wo_t", [P, 2, 2, D]),
            "raw": sb("raw", [P, KC * 2 * HID]),
        }
        attention_phase(nc, dram, tensors)
        ffn_phase(nc, dram, tensors)


_TRANSPOSED = {
    "gamma1": "L0_cond_attn_gamma_w", "beta1": "L0_cond_attn_beta_w", "gamma2": "L0_cond_ffn_gamma_w",
    "beta2": "L0_cond_ffn_beta_w", "alpha1": "L0_cond_attn_alpha_w", "alpha2": "L0_cond_ffn_alpha_w",
    "lin_w": "L1_cond_lin_w", "wq": "L0_cond_W_q", "wk": "L0_cond_W_k", "wv": "L0_cond_W_v", "wo": "L0_cond_W_o",
    "gate": "L0_cond_gate_w", "hidden": "L0_cond_hidden_w", "out_w": "L0_cond_out_w", "cond": "cond_256",
}
_PLAIN = {"lin_b": "L1_cond_lin_b", "l1_w": "L1_cond_weight", "l1_b": "L1_cond_bias", "out_b": "L0_cond_out_b"}


def kernel(**inputs):
    import numpy as _np
    import concourse.bacc as _bacc
    from concourse.bass_utils import run_bass_kernel_spmd as _run

    nc = _bacc.Bacc("TRN2", target_bir_lowering=False, num_devices=1)
    arrays = {"in_x": _np.ascontiguousarray(_np.asarray(inputs["x"])).reshape(B, P, TT, D)}
    for name, key in _TRANSPOSED.items():
        arrays["in_" + name] = _np.ascontiguousarray(_np.asarray(inputs[key]).T)
    for name, key in _PLAIN.items():
        arrays["in_" + name] = _np.ascontiguousarray(_np.asarray(inputs[key]))
    dram = {k[3:]: nc.dram_tensor(k, a.shape, mybir.dt.from_np(a.dtype), kind="ExternalInput").ap()
            for k, a in arrays.items()}
    dram["out"] = nc.dram_tensor("out_y", (B, P, TT, D), F32, kind="ExternalOutput").ap()
    build(nc, dram)
    r = _run(nc, [arrays], core_ids=[0])
    return r.results[0]["out_y"].reshape(B, P * TT, D)
```

```python
from contextlib import ExitStack

import concourse.bass as bass
from concourse import mybir

F32 = mybir.dt.float32
F32R = mybir.dt.float32r
ALU = mybir.AluOpType
ACT = mybir.ActivationFunctionType
AX = mybir.AxisListType

P = 128
B = 8
T = 512
D = 256
KC = D // P
TT = T // P
NH = 16
DH = D // NH
HG = 4
NG = NH // HG
DT = 64
HID = 4 * D
JC = HID // P
EPS_RMS = 1e-6
EPS_LN = 1e-5
SCALE = (NH / D) ** 0.5
UNITS = NG * TT
TAB = 3

RT = (B - 2) * TT
DS = T * NH // 2 // P

PRO = ["COEF", "TR0", "TR1", "Q0", "K0", "Q1", "K1", "V0", "V1", "MT0"]
MID = {0: "MT1", 1: "TR0", 2: "TR1", 3: "Q0", 4: "K0", 5: "MT2", 6: "V0", 7: "V1", 8: "MT3", 9: "Q1",
       10: "K1", 11: "WO0", 12: "MT0", 14: "WO1"}
OWN = ("MT1", "MT2", "MT3")
PREV = ("WO0", "WO1")
MOVED = {"Q1": 10, "K1": 11}
FFN = {13: "FT0", 15: "FT1"}
ORDER = ("S0", "S1", "M0", "S3", "S2", "M1", "A", "M2", "M3", "J")
BEFORE = {"K0": 0}
AHEAD = 4


def jobs_of(first, last):
    jobs = {MOVED.get(o, u) if first else u: o for u, o in MID.items()
            if (o not in PREV or not first) and (o in OWN + PREV or not last)}
    return dict(sorted((jobs | (FFN if last else {})).items()))


N_FIRST = len(jobs_of(True, False))
N_MID = len(jobs_of(False, False))


def job_base(b, first):
    return len(PRO) if first else len(PRO) + N_FIRST - N_MID + N_MID * b


def job_no(b, first, last, op):
    return job_base(b, first) + list(jobs_of(first, last).values()).index(op)


def attention_phase(nc, dram, tensors):
    x_all, tab, coef, ident, ss2, rstd2 = (tensors[k] for k in ("x_all", "tab", "coef", "ident", "ss2", "rstd2"))
    wo_hi, wo_lo, o_raw, o_c, d_c, on_hi, on_lo, wo_t, raw, n_hi, n_lo = (
        tensors[k] for k in ("wo_hi", "wo_lo", "o_raw", "o_c", "d_c", "on_hi", "on_lo", "wo_t", "raw", "n_hi", "n_lo"))
    with ExitStack() as ctx:
        def sb(name, shape, dt=F32):
            return ctx.enter_context(nc.sbuf_tensor(name, shape, dt))

        def sem(name):
            return ctx.enter_context(nc.semaphore(name))

        cond = sb("cond", [DT + 1, B])
        tab_rows = o_c[0:B].rearrange("b c n -> b (c n)")[:, 0:TAB * D].rearrange("b (k n) -> b k n", n=D)
        d_s = sb("d_s", [P, 2, DS])
        w_hi = sb("w_hi", [P, KC, 3, D], F32R)
        w_lo = sb("w_lo", [P, KC, 3, D], F32R)
        ss1 = sb("ss1", [P, B * TT])
        rstd1 = sb("rstd1", [P, B * TT])
        junk = sb("junk", [P, D])
        xhat = raw[:, 0:TT * D].rearrange("p (t n) -> p t n", n=D)
        y_n = raw[:, TT * D:2 * TT * D].rearrange("p (k n) -> p k n", n=T)
        v_st = raw[:, 2 * TT * D:].rearrange("p (g t i d) -> p g t i d", g=NG, t=TT, i=HG)
        qk_hi = sb("qk_hi", [P, 4, T], F32R)
        qk_lo = sb("qk_lo", [P, 4, T], F32R)
        qs = sb("qs", [P, NG, 2, T], F32R)
        ks = sb("ks", [P, NG, 2, T], F32R)
        v = sb("v", [P, NG, TT, HG, 32])
        xhat_f = v[:, 0:2].rearrange("p g t i d -> p (g t i d)").rearrange("p (t n) -> p t n", n=D)
        y_f = (o_c[:, 1, :], d_c[:, 1, :])
        mx = sb("mx", [P, 2, 2, 2, TT])
        m_hl = sb("m_hl", [2 * HG * 2, 2, P], F32R)
        prob = sb("prob", [P, 2, HG, T])
        flat = prob[:].rearrange("p u h n -> p u (h n)")
        w_raw = flat[:, 0].rearrange("p (k i n) -> p k i n", k=KC, n=D)
        ada_w = flat[0:DT + 1, 1, 0:7 * D].rearrange("p (i n) -> p i n", n=D)
        ps_s = ctx.enter_context(nc.psum_tensor("ps_s", [P, HG, T], F32))
        ps_m = ctx.enter_context(nc.psum_tensor("ps_m", [P, 2, T], F32))
        ps_o = ctx.enter_context(nc.psum_tensor("ps_o", [P, T], F32))
        ps_j = ctx.enter_context(nc.psum_tensor("ps_j", [P, T], F32))
        stack_d = nc.dram_tensor("stack_scratch", (2, 2, HG, P * T), F32, kind="Internal").ap()
        o_d = nc.dram_tensor("out_scratch", (2, 2, P, T), F32, kind="Internal").ap()
        tab_d = nc.dram_tensor("table_scratch", (TAB, B, D), F32, kind="Internal").ap()
        r_d = nc.dram_tensor("reciprocal_scratch", (2, P * DS), F32, kind="Internal").ap()

        x0_in = sem("x0_in"); x1_in = sem("x1_in"); x_in = sem("x_in"); small_in = sem("small_in")
        table_w_in = sem("table_w_in"); wqk_in = sem("wqk_in"); wvo_in = sem("wvo_in")
        consts = sem("consts"); tab_w = sem("tab_w"); tab_in = sem("tab_in"); pad_written = sem("pad_written")
        w_hi_r = sem("w_hi_r"); w_lo_r = sem("w_lo_r")
        sq1 = sem("sq1"); ms1 = sem("ms1"); root1 = sem("root1"); rstd_r = sem("rstd_r")
        tab_full = sem("tab_full"); tab_r = sem("tab_r")
        xhat_r = sem("xhat_r"); n_hi_r = sem("n_hi_r"); n_lo_r = sem("n_lo_r")
        qk_hi_r = sem("qk_hi_r"); qk_lo_r = sem("qk_lo_r"); v_r = sem("v_r")
        scr_w = sem("scr_w")
        stack_in = [sem(f"stack_in{g}") for g in range(NG)]; v_in = [sem(f"v_in{g}") for g in range(NG)]
        mx_full = sem("mx_full"); mx_red = sem("mx_red"); m_hi_r = sem("m_hi_r"); m_lo_r = sem("m_lo_r"); m_in = sem("m_in")
        s_full = sem("s_full"); p_r = sem("p_r"); av_done = sem("av_done")
        o_r = sem("o_r"); oc_in = sem("oc_in"); x1_r = sem("x1_r"); sq2 = sem("sq2")
        den_in = sem("den_in"); rec_r = sem("rec_r"); rec_w = sem("rec_w"); rec_in = sem("rec_in")
        omul_r = sem("omul_r"); ohi_r = sem("ohi_r"); olo_r = sem("olo_r")
        job_full = sem("job_full"); job_free = sem("job_free"); sp_waited = sem("sp_waited"); ffn_in = sem("ffn_in")
        ms2 = sem("ms2"); root2 = sem("root2"); rstd2_r = sem("rstd2_r")
        ow_w = sem("ow_w"); pool_waited = sem("pool_waited")

        def max_bank(n):
            n %= 2 + HG
            return ps_m[:, n, :] if n < 2 else ps_s[:, n - 2, :]

        block = ctx.enter_context(nc.Block())

        @block.sync
        def _(sp):
            sp.dma_start(x_all[:, 0], dram["x"][0]).then_inc(x0_in, 16)
            sp.dma_start(cond[0:DT, :], dram["cond"]).then_inc(small_in, 16)
            for i, name in enumerate(("gamma1", "beta1", "gamma2", "beta2")):
                sp.dma_start(ada_w[0:DT, i, :], dram[name]).then_inc(small_in, 16)
            sp.dma_start(x_all[:, 1], dram["x"][1]).then_inc(x1_in, 16)
            sp.wait_ge(consts, 5)
            for c in range(2):
                for i in range(2):
                    rows = stack_d[i, c].rearrange("j (r t n) -> (j r) t n", t=4, n=T)
                    sp.dma_start(rows[:, 3, :], o_raw[:, i, :]).then_inc(pad_written, 16)
            sp.wait_ge(pad_written, 64)

            def wait(semaphore, value):
                sp.wait_ge(semaphore, value)
                sp.sem_inc(sp_waited, 1)

            def stack_write(nb, c):
                for i, terms in enumerate(((qk_hi, qk_lo, qk_hi), (qk_hi, qk_hi, qk_lo))):
                    wait(qk_lo_r, 4 * nb + 2 * c + i + 1)
                    rows = stack_d[i, c].rearrange("j (r t n) -> (j r) t n", t=4, n=T)
                    for t, src in enumerate(terms):
                        sp.dma_start(rows[:, t, :], src[:, 2 * c + i, :].bitcast(F32)).then_inc(scr_w, 16)
                wait(scr_w, 96 * (2 * nb + c + 1))

            def stack_read(nb, g, reuse):
                if reuse:
                    wait(av_done, UNITS * (nb - 1) + TT * (g + 1))
                for i, dst in enumerate((qs, ks)):
                    src = stack_d[i, g // 2, 2 * (g % 2):2 * (g % 2) + 2].rearrange("j (r n) -> r j n", n=T)
                    sp.dma_start(dst[:, g].bitcast(F32), src).then_inc(stack_in[g], 16)

            def v_copy(nb, g):
                wait(v_r, TT * (nb + 1))
                sp.dma_start(v[:, g], v_st[:, g]).then_inc(v_in[g], 16)

            for c in range(2):
                stack_write(0, c)
                for g in (2 * c, 2 * c + 1):
                    stack_read(0, g, False)
            for g in range(NG - 1):
                v_copy(0, g)
            sp.wait_ge(m_in, 64)
            for b in range(2, B):
                sp.dma_start(x_all[:, b], dram["x"][b]).then_inc(x_in, 16)
            sp.wait_ge(tab_r, 2)
            sp.dma_start(tab_d.rearrange("k b n -> b k n"), tab_rows).then_inc(tab_w, 16)
            sp.wait_ge(tab_w, 16)
            sp.dma_start(tab[:], tab_d.partition_broadcast(P)).then_inc(tab_in, 16)

            def batch(b, first, last):
                nb = b + 1
                if not first:
                    stack_read(b, 3, True)
                v_copy(b, 3)
                if last:
                    for g in range(NG):
                        wait(v_in[g], 16 * (b + 1))
                    wait(job_full, job_base(b, first))
                    gh_raw = raw[:].rearrange("p (k i n) -> p k i n", k=KC, i=2)
                    for i, name in enumerate(("gate", "hidden")):
                        sp.dma_start(gh_raw[:, :, i, :], dram[name].rearrange("(k p) n -> p k n", p=P)).then_inc(ffn_in, 16)
                    sp.wait_ge(ffn_in, 32)
                    return
                stack_write(nb, 0)
                for g in range(3):
                    if g == 2:
                        stack_write(nb, 1)
                    stack_read(nb, g, True)
                    v_copy(nb, g)

            batch(0, True, False)
            with sp.Fori(1, B - 1) as b:
                batch(b, False, False)
            batch(B - 1, False, True)

        @block.gpsimd
        def _(pool):
            for i, name in ((4, "alpha1"), (5, "alpha2"), (6, "lin_w")):
                pool.dma_start(ada_w[0:DT, i, :], dram[name]).then_inc(table_w_in, 16)
            pool.dma_start(ada_w[DT:DT + 1, 6, :], dram["lin_b"].rearrange("(a n) -> a n", a=1)).then_inc(table_w_in, 16)
            for n, (ap, value) in enumerate(((ident[:], 0.0), (cond[DT:DT + 1, :], 1.0), (o_raw[:, 0, :], 0.0),
                                             (o_raw[:, 1, :], 1.0), (v_st[:, :, :, :, DH:32], 1.0))):
                pool.memset(ap, value).then_inc(consts, 1)
                pool.wait_ge(consts, n + 1)
            pool.affine_select(out=ident[:], in_=ident[:], compare_op=ALU.not_equal, fill=1.0, base=0,
                               pattern=[[-1, P]], channel_multiplier=1).then_inc(consts, 1)

            def max_rows(b, g):
                n = NG * b + g
                if not (isinstance(n, int) and n == 0):
                    pool.wait_ge(m_in, 64 * n)
                pool.wait_ge(m_lo_r, n + 1)
                pool.sem_inc(pool_waited, 1)
                for s in range(2):
                    for hl in range(2):
                        r = 64 * s + 4 * hl + 3
                        pool.dma_start(qs[r:r + 1, g].rearrange("r j n -> r (j n)").bitcast(F32),
                                       m_hl[2 * TT * s:2 * TT * (s + 1), hl, :].bitcast(F32)).then_inc(m_in, 16)

            def update_x(b, w, no):
                pool.wait_ge(job_free, no + 1)
                pool.sem_inc(pool_waited, 1)
                xs = x_all[:, bass.ds(b, 1), 2 * w:2 * w + 2, :].rearrange("p a t n -> p (a t) n")
                pool.tensor_tensor(xs, xs, wo_t[:, w], ALU.add).then_inc(x1_r, 1)

            def o_norm(b, c):
                pool.wait_ge(oc_in, 16 * (2 * b + c + 1))
                pool.wait_ge(rec_in, 16 * (2 * b + c + 1))
                pool.tensor_tensor(o_c[:, c, :], o_c[:, c, :], d_c[:, c, :], ALU.mult).then_inc(omul_r, 1)

            def o_low(b, c):
                pool.wait_ge(ohi_r, 2 * b + c + 1)
                pool.tensor_tensor(on_lo[:, c, :], o_c[:, c, :], on_hi[:, c, :].bitcast(F32), ALU.subtract)\
                    .then_inc(olo_r, 1)

            max_rows(0, 0)

            def batch(b, first, last):
                max_rows(b, 1)
                if not first:
                    o_low(b - 1, 0)
                max_rows(b, 2)
                if not first:
                    o_norm(b - 1, 1)
                max_rows(b, 3)
                if not first:
                    o_low(b - 1, 1)
                if not first:
                    update_x(b - 1, 0, job_no(b, first, last, "WO0"))
                if not last:
                    max_rows(b + 1, 0)
                o_norm(b, 0)
                if not first:
                    update_x(b - 1, 1, job_no(b, first, last, "WO1"))

            batch(0, True, False)
            with pool.Fori(1, B - 1) as b:
                batch(b, False, False)
            batch(B - 1, False, True)

        @block.scalar
        def _(act):
            for i, (name, arrived) in enumerate((("wq", wqk_in), ("wk", wqk_in), ("wv", wvo_in), ("wo", wvo_in))):
                act.dma_start(w_raw[:, :, i, :], dram[name].rearrange("(k p) n -> p k n", p=P)).then_inc(arrived, 16)

            def square1(n):
                if n > 0:
                    act.wait_ge(sq1, n)
                act.activation(junk[:], x_all[:, n // TT, n % TT, :], ACT.Square, scale=1.0 / DH,
                                     accum_out=ss1[:, n:n + 1]).then_inc(sq1, 1)

            act.wait_ge(x0_in, 16)
            for t in range(TT):
                square1(t)
            act.wait_ge(ms1, 1)
            act.activation(ss1[:, 0:TT], ss1[:, 0:TT], ACT.Sqrt).then_inc(root1, 1)

            for i, arrived in ((0, wqk_in), (2, wvo_in)):
                act.wait_ge(arrived, 32)
                for dst, src in ((w_hi[:, :, 0:2], w_raw[:, :, 0:2]),) if i == 0 else \
                        ((w_hi[:, :, 2], w_raw[:, :, 2]), (wo_hi[:], w_raw[:, :, 3])):
                    act.activation(dst, src, ACT.Copy).then_inc(w_hi_r, 1)
            act.wait_ge(job_full, 1)
            act.activation(coef[:], ps_j[:, 0:4 * KC * B], ACT.Copy).then_inc(job_free, 1)

            def y_copy(nb, k, no, reuse):
                act.wait_ge(job_full, no + 1)
                if reuse:
                    act.wait_ge(n_lo_r, 2 * nb)
                cf = coef[:, :, k:k + 1, bass.ds(nb, 1)].rearrange("p i k b -> p i (k b)")
                act.activation(n_hi[:, k, :], ps_j[:], ACT.Identity, scale=cf[:, 0], bias=cf[:, 1]).then_inc(n_hi_r, 1)
                act.activation(y_n[:, k, :], ps_j[:], ACT.Identity, scale=cf[:, 0], bias=cf[:, 1])\
                   .then_inc(job_free, 1)

            def qk_copy(nb, i, no, reuse):
                act.wait_ge(job_full, no + 1)
                if reuse:
                    act.wait_ge(scr_w, 96 * (2 * (nb - 1) + i // 2 + 1))
                act.activation(qk_hi[:, i, :], ps_j[:] if reuse else ps_s[:, i], ACT.Copy).then_inc(qk_hi_r, 1)

            def v_evac(nb, w, no, reuse):
                act.wait_ge(job_full, no + 1)
                if reuse:
                    for g in range(NG):
                        act.wait_ge(v_in[g], 16 * nb)
                for t in (2 * w, 2 * w + 1):
                    src = ps_j[:, D * (t % 2):D * (t % 2) + D].rearrange("p (g i d) -> p g i d", g=NG, i=HG)
                    act.activation(v_st[:, :, t, :, 0:DH], src, ACT.Copy).then_inc(v_r, 1)
                act.wait_ge(v_r, TT * nb + 2 * w + 2)
                act.sem_inc(job_free, 1)

            def exps(b, u, warm):
                n = UNITS * b + u
                for h in range(2):
                    act.wait_ge(s_full, 2 * n + h + 1)
                    if warm:
                        act.wait_ge(av_done, n - 1)
                    act.activation(prob[:, u % 2, 2 * h:2 * h + 2, :], ps_s[:, 2 * h:2 * h + 2, :], ACT.Exp,
                                   scale=SCALE).then_inc(p_r, 1)

            def norm(nb, made):
                act.wait_ge(rstd_r, 2 if isinstance(nb, int) and nb == 1 else 3)
                act.wait_ge(job_full, made)
                for t in range(TT):
                    xs = x_all[:, bass.ds(nb, 1), t, :].rearrange("p a n -> p (a n)")
                    act.activation(xhat[:, t, :], xs, ACT.Copy, scale=rstd1[:, bass.ds(TT * nb + t, 1)]).then_inc(xhat_r, 1)

            def o_evac(b, g, reuse):
                n = NG * b + g
                act.wait_ge(av_done, TT * (n + 1))
                if reuse:
                    act.wait_ge(ow_w, 16 * (n - 1))
                act.activation(o_raw[:, g % 2, :], ps_o[:], ACT.Copy).then_inc(o_r, 1)

            def o_write(b, g):
                act.wait_ge(o_r, NG * b + g + 1)
                act.dma_start(o_d[g // 2, g % 2], o_raw[:, g % 2, :]).then_inc(ow_w, 16)

            def o_read(b, c, fresh):
                act.wait_ge(ow_w, 16 * (NG * b + 2 * c + 2))
                if not fresh:
                    act.wait_ge(olo_r, 2 * (b - 1) + c + 1)
                if not (fresh and c == 0):
                    act.wait_ge(omul_r, 2 * b + c)
                act.dma_start(d_s[:, c, :], o_d[c].rearrange("g (i r) (e n) -> (g i) r e n", r=2 * DH, n=DS)[:, DH])\
                   .then_inc(den_in, 16)
                rows = o_d[c].rearrange("g (i k d) n -> k (g i) d n", i=HG, k=2)
                act.dma_start(o_c[:, c, :], rows[0]).then_inc(oc_in, 16)

            def rec_write(b, c):
                act.wait_ge(rec_r, 2 * b + c + 1)
                act.dma_start(r_d[c].rearrange("(p n) -> p n", n=DS), d_s[:, c, :]).then_inc(rec_w, 16)

            def rec_read(b, c):
                act.wait_ge(rec_w, 16 * (2 * b + c + 1))
                act.dma_start(d_c[:, c, :], r_d[c].rearrange("(h r n) -> h r n", r=1, n=T)
                              .broadcast_to([NH // 2, DH, T])).then_inc(rec_in, 16)

            def squares2(b, tiles):
                for t in tiles:
                    act.wait_ge(x1_r, 2 * b + 1 + t // 2)
                    if t > 0:
                        act.wait_ge(sq2, TT * b + t)
                    col = ss2[:, bass.ds(b, 1), t:t + 1].rearrange("p a b -> p (a b)")
                    act.activation(junk[:], x_all[:, bass.ds(b, 1), t, :].rearrange("p a n -> p (a n)"), ACT.Square,
                                   scale=1.0 / DH, accum_out=col).then_inc(sq2, 1)

            def max_high(b, g, no):
                n = NG * b + g
                act.wait_ge(job_full, no + 1)
                if not (isinstance(n, int) and n == 0):
                    act.wait_ge(m_in, 64 * n)
                act.activation(m_hl[:, 0, :], ps_j[0:2 * HG * 2, 0:P], ACT.Copy, scale=-1.0).then_inc(m_hi_r, 1)

            def o_high(b, c):
                act.wait_ge(omul_r, 2 * b + c + 1)
                act.activation(on_hi[:, c, :], o_c[:, c, :], ACT.Copy).then_inc(ohi_r, 1)

            def job(nb, op, no, reuse):
                if op in ("TR0", "TR1"):
                    y_copy(nb, int(op[2]), no, reuse)
                elif op[0] in "QK":
                    qk_copy(nb, 2 * int(op[1]) + "QK".index(op[0]), no, reuse)
                elif op[0] == "V":
                    v_evac(nb, int(op[1]), no, reuse)
                elif op[0:2] == "FT":
                    k = int(op[2])
                    act.wait_ge(job_full, no + 1)
                    act.activation(n_hi[:, k, :], ps_j[:], ACT.Identity, scale=coef[:, 2, k, 0:1],
                                   bias=coef[:, 3, k, 0:1]).then_inc(n_hi_r, 1)
                    act.activation(y_f[k], ps_j[:], ACT.Identity, scale=coef[:, 2, k, 0:1],
                                   bias=coef[:, 3, k, 0:1]).then_inc(job_free, 1)
                elif op[0:2] == "MT":
                    max_high(nb - (op != "MT0"), int(op[2]), no)

            for no, op in enumerate(PRO[:-1]):
                job(0, op, no, False)
            act.wait_ge(x1_in, 16)
            for n in range(TT, 2 * TT):
                square1(n)
            act.wait_ge(ms1, 2)
            act.activation(ss1[:, TT:2 * TT], ss1[:, TT:2 * TT], ACT.Sqrt).then_inc(root1, 1)
            act.wait_ge(tab_full, 1)
            act.activation(tab_rows[:, 0:2].rearrange("b k n -> b (k n)"), ps_s[0:B, 2, :], ACT.Copy).then_inc(tab_r, 1)
            act.activation(tab_rows[:, 2], ps_s[0:B, 3, 0:D], ACT.Tanh).then_inc(tab_r, 1)
            max_high(0, 0, PRO.index("MT0"))
            act.wait_ge(pad_written, 64)

            def batch(b, first, last, second=False):
                jobs = jobs_of(first, last)
                for u in range(UNITS):
                    exps(b, u, not (first and u < 2))
                    if u == 0 and not last:
                        norm(b + 1, job_base(b, first))
                    if u in jobs:
                        job(b + 1, jobs[u], job_no(b, first, last, jobs[u]), True)
                    if u % TT == 0 and not (first and u == 0):
                        o_evac(b - (u == 0), (u // TT - 1) % NG, not (first and u < 12))
                    if u % TT == 1 and not (first and u == 1) and not (last and u == 13):
                        o_write(b - (u == 1), (u // TT - 1) % NG)
                    if u in (1, 9) and not first:
                        if not second:
                            act.wait_ge(job_full, job_no(b - 1, False, False, "WO1") + 1)
                        o_high(b - 1, u // 8)
                    if u == 2 and not first:
                        o_read(b - 1, 1, second)
                    if u == 5 and not first:
                        rec_write(b - 1, 1)
                    if u == 6 and not first:
                        rec_read(b - 1, 1)
                    if u == 10:
                        if first:
                            act.wait_ge(tab_w, 16)
                        o_read(b, 0, first)
                    if u == 13:
                        rec_write(b, 0)
                    if u == 14:
                        rec_read(b, 0)
                    if u == 2 and not (first or second):
                        squares2(b - 2, (2, 3))
                    if u == 15 and not (first or last):
                        squares2(b - 1, (0, 1))
                    if first and 2 <= u < 14:
                        if u == 2:
                            act.wait_ge(x_in, 16 * (B - 2))
                        for n in (2 * (u + 2), 2 * (u + 2) + 1):
                            square1(n)
                    if last and u == 4:
                        act.wait_ge(ms2, 1)
                        act.activation(rstd2[:, 0:RT], rstd2[:, 0:RT], ACT.Sqrt).then_inc(root2, 1)
                    if first and u == 14:
                        act.wait_ge(ms1, 3)
                        act.activation(ss1[:, 2 * TT:], ss1[:, 2 * TT:], ACT.Sqrt).then_inc(root1, 1)

            batch(0, True, False)
            with act.Fori(1, 2) as b:
                batch(b, False, False, True)
            with act.Fori(2, B - 1) as b:
                batch(b, False, False)
            batch(B - 1, False, True)
            act.wait_ge(job_full, job_no(B - 1, False, True, "WO1") + 1)
            o_high(B - 1, 0)
            o_evac(B - 1, 3, True)

        @block.vector
        def _(dve):
            dve.wait_ge(sq1, TT)
            dve.tensor_scalar(ss1[:, 0:TT], ss1[:, 0:TT], EPS_RMS, None, ALU.add).then_inc(ms1, 1)
            dve.wait_ge(root1, 1)
            dve.reciprocal(rstd1[:, 0:TT], ss1[:, 0:TT]).then_inc(rstd_r, 1)

            dve.wait_ge(rstd_r, 1)
            for t in range(TT):
                dve.tensor_scalar(xhat[:, t, :], x_all[:, 0, t, :], rstd1[:, t:t + 1], None, ALU.mult).then_inc(xhat_r, 1)
            def w_low(n, low, high, src):
                dve.wait_ge(w_hi_r, n)
                dve.tensor_tensor(low, src, high.bitcast(F32), ALU.subtract).then_inc(w_lo_r, 1)

            w_low(1, w_lo[:, :, 0:2], w_hi[:, :, 0:2], w_raw[:, :, 0:2])

            def n_low(nb, k, no):
                dve.wait_ge(n_hi_r, 2 * nb + k + 1)
                dve.wait_ge(job_free, no + 1)
                dve.tensor_tensor(n_lo[:, k, :], y_n[:, k, :], n_hi[:, k, :].bitcast(F32), ALU.subtract)\
                   .then_inc(n_lo_r, 1)

            def ffn_low(k, no):
                dve.wait_ge(n_hi_r, 2 * B + k + 1)
                dve.wait_ge(job_free, no + 1)
                dve.tensor_tensor(n_lo[:, k, :], y_f[k], n_hi[:, k, :].bitcast(F32), ALU.subtract).then_inc(n_lo_r, 1)

            def qk_low(nb, i, no, reuse):
                dve.wait_ge(qk_hi_r, 4 * nb + i + 1)
                if reuse:
                    dve.wait_ge(scr_w, 96 * (2 * (nb - 1) + i // 2 + 1))
                dve.tensor_tensor(qk_lo[:, i, :], ps_j[:] if reuse else ps_s[:, i], qk_hi[:, i, :].bitcast(F32), ALU.subtract)\
                   .then_inc(qk_lo_r, 1)
                dve.wait_ge(qk_lo_r, 4 * nb + i + 1)
                dve.sem_inc(job_free, 1)

            def max_low(b, g, no):
                n = NG * b + g
                dve.wait_ge(m_hi_r, n + 1)
                dve.scalar_tensor_tensor(out=m_hl[:, 1, :], in0=ps_j[0:2 * HG * 2, 0:P], scalar=-1.0,
                                         in1=m_hl[:, 0, :].bitcast(F32), op0=ALU.mult, op1=ALU.subtract)\
                   .then_inc(m_lo_r, 1)
                dve.wait_ge(m_lo_r, n + 1)
                dve.sem_inc(job_free, 1)

            def wo_scale(b, w, no, reuse):
                dve.wait_ge(job_full, no + 1)
                if reuse:
                    dve.wait_ge(x1_r, 2 * (b - 1) + w + 1)
                al = tab[:, 0, bass.ds(b, 1), :].broadcast_to([P, 2, D])
                dve.tensor_tensor(wo_t[:, w], ps_j[:].rearrange("p (t n) -> p t n", t=2), al, ALU.mult)\
                   .then_inc(job_free, 1)

            def o_recip(b, c):
                dve.wait_ge(den_in, 16 * (2 * b + c + 1))
                dve.reciprocal(d_s[:, c, :], d_s[:, c, :]).then_inc(rec_r, 1)

            def reduce_max(b, g, qt, i, free, bank=None):
                n = UNITS * HG // NG * (NG * b + g) + HG * qt + i
                dve.wait_ge(mx_full, n + 1)
                if free is not None:
                    dve.wait_ge(job_full, free + 1)
                dve.tensor_reduce(mx[:, g % 2, i % 2, i // 2, qt:qt + 1], ps_m[:, i % 2, :] if bank is None else bank, AX.X, ALU.max)\
                   .then_inc(mx_red, 1)

            for k in range(2):
                n_low(0, k, PRO.index(f"TR{k}"))
            w_low(2, w_lo[:, :, 2], w_hi[:, :, 2], w_raw[:, :, 2])
            w_low(3, wo_lo[:], wo_hi[:], w_raw[:, :, 3])
            for i, op in enumerate(("Q0", "K0", "Q1", "K1")):
                qk_low(0, i, PRO.index(op), False)
            dve.wait_ge(sq1, 2 * TT)
            dve.tensor_scalar(ss1[:, TT:2 * TT], ss1[:, TT:2 * TT], EPS_RMS, None, ALU.add).then_inc(ms1, 1)
            for n in range(2 * UNITS):
                reduce_max(0, n // UNITS, n % UNITS // HG, n % HG, None, max_bank(n))
                if n == UNITS - 1 + AHEAD:
                    max_low(0, 0, PRO.index("MT0"))
                    dve.wait_ge(root1, 2)
                    dve.reciprocal(rstd1[:, TT:2 * TT], ss1[:, TT:2 * TT]).then_inc(rstd_r, 1)
            dve.wait_ge(rstd_r, 2)

            def batch(b, first, last, second):
                jobs = jobs_of(first, last)
                for u in range(UNITS):
                    g, qt = (u // TT + 2) % NG, u % TT
                    gb = b + (u // TT + 2) // NG
                    live = not (last and u >= UNITS // 2)
                    def reductions(heads):
                        for i in heads if live else ():
                            if u // TT < 2:
                                free = job_base(b, first) - (1 if u // TT == 0 else 0)
                            else:
                                free = job_no(b, first, last, "MT2" if u // TT == 2 else "MT3")
                            reduce_max(gb, g, qt, i, free if (qt == 0 and i == 0) else None)

                    op = jobs.get(u - 1)
                    before = BEFORE.get(op, 2)
                    reductions(range(before))
                    if u > 0 and op is not None:
                        no = job_no(b, first, last, op)
                        if op in ("TR0", "TR1"):
                            n_low(b + 1, int(op[2]), no)
                        elif op[0] in "QK":
                            qk_low(b + 1, 2 * int(op[1]) + "QK".index(op[0]), no, True)
                        elif op in PREV:
                            wo_scale(b - 1, int(op[2]), no, not second)
                        elif op == "FT0":
                            ffn_low(0, no)
                    reductions(range(before, HG))
                    op = jobs.get(u)
                    if op is not None and op[0:2] == "MT":
                        g_m = int(op[2])
                        max_low(b + (g_m == 0), g_m, job_no(b, first, last, op))
                    if u == 4 and not first:
                        o_recip(b - 1, 1)
                    if u == 12:
                        o_recip(b, 0)
                    if last and u == 3:
                        dve.wait_ge(sq2, RT)
                        dve.tensor_scalar(rstd2[:, 0:RT], ss2[:].rearrange("p b t -> p (b t)")[:, 0:RT], EPS_RMS, None,
                                          ALU.add).then_inc(ms2, 1)
                    if last and u == 6:
                        dve.wait_ge(root2, 1)
                        dve.reciprocal(rstd2[:, 0:RT], rstd2[:, 0:RT]).then_inc(rstd2_r, 1)
                    if last and u == 10:
                        dve.wait_ge(rstd2_r, 1)
                        dve.wait_ge(av_done, UNITS * b + 2 * TT)
                        for t in range(TT):
                            dve.tensor_scalar(xhat_f[:, t, :], x_all[:, 0, t, :], rstd2[:, t:t + 1], None, ALU.mult)\
                               .then_inc(xhat_r, 1)
                    if first and u == 14:
                        dve.wait_ge(sq1, B * TT)
                        dve.tensor_scalar(ss1[:, 2 * TT:], ss1[:, 2 * TT:], EPS_RMS, None, ALU.add).then_inc(ms1, 1)
                    if first and u == 15:
                        dve.wait_ge(root1, 3)
                        dve.reciprocal(rstd1[:, 2 * TT:], ss1[:, 2 * TT:]).then_inc(rstd_r, 1)
                        dve.wait_ge(rstd_r, 3)

            batch(0, True, False, False)
            dve.wait_ge(tab_in, 16)
            with dve.Fori(1, 2) as b:
                batch(b, False, False, True)
            with dve.Fori(2, B - 1) as b:
                batch(b, False, False, False)
            batch(B - 1, False, True, False)
            ffn_low(1, job_no(B - 1, False, True, "FT1"))
            dve.wait_ge(ohi_r, 2 * B - 1)
            dve.tensor_tensor(on_lo[:, 0, :], o_c[:, 0, :], on_hi[:, 0, :].bitcast(F32), ALU.subtract).then_inc(olo_r, 1)

        @block.tensor
        def _(pe):
            def job_wait(no):
                if not (isinstance(no, int) and no == 0):
                    pe.wait_ge(job_free, no)

            pe.wait_ge(small_in, 16 * 5)
            pe.wait_ge(consts, 6)
            n = 0
            for i in range(4):
                for k in range(KC):
                    mm = pe.matmul(ps_j[:, n * B:(n + 1) * B], ada_w[0:DT, i, k * P:(k + 1) * P], cond[0:DT, :],
                                   start=(n == 0), stop=True, skip_group_check=True)
                    n += 1
            mm.then_inc(job_full, 1)

            def transposes(nb, k, no):
                job_wait(no)
                pe.wait_ge(xhat_r, TT * (nb + 1))
                for t in range(TT):
                    mm = pe.transpose(ps_j[:, t * P:(t + 1) * P], xhat[:, t, k * P:(k + 1) * P], ident[:])
                mm.then_inc(job_full, 1)

            def split_product(out, lhs, rhs, inc=None):
                steps = [(a, c, k) for k in range(KC) for a, c in ((0, 0), (1, 0), (0, 1))]
                for n, (a, c, k) in enumerate(steps):
                    mm = pe.matmul(out, lhs(a, k), rhs(c, k), start=(n == 0), stop=(n == len(steps) - 1))
                return mm

            W, WO, N, O = (w_hi, w_lo), (wo_hi, wo_lo), (n_hi, n_lo), (on_hi, on_lo)

            def project_qk(nb, op, no, bank=None):
                if bank is None:
                    job_wait(no)
                pe.wait_ge(n_lo_r, 2 * (nb + 1))
                i, c = "QK".index(op[0]), int(op[1])
                split_product(ps_j[:] if bank is None else ps_s[:, bank], lambda a, k: W[a][:, k, i, c * P:(c + 1) * P], lambda a, k: N[a][:, k, :])\
                    .then_inc(job_full, 1)

            def project_v(nb, w, no):
                job_wait(no)
                pe.wait_ge(n_lo_r, 2 * (nb + 1))
                for t in (2 * w, 2 * w + 1):
                    mm = split_product(ps_j[:, D * (t % 2):D * (t % 2 + 1)],
                                       lambda a, k: N[a][:, k, t * P:(t + 1) * P], lambda a, k: W[a][:, k, 2, :])
                mm.then_inc(job_full, 1)

            def project_o(b, w, no):
                job_wait(no)
                pe.wait_ge(olo_r, 2 * (b + 1))
                for t in (2 * w, 2 * w + 1):
                    mm = split_product(ps_j[:, D * (t % 2):D * (t % 2 + 1)],
                                       lambda a, k: O[a][:, k, t * P:(t + 1) * P], lambda a, k: WO[a][:, k, :])
                mm.then_inc(job_full, 1)

            def max_transpose(b, g, no):
                job_wait(no)
                pe.wait_ge(mx_red, UNITS * (NG * b + g + 1))
                pe.transpose(ps_j[0:2 * HG * 2, 0:P], mx[:, g % 2].rearrange("p s j t -> p (s j t)"), ident[:])\
                  .then_inc(job_full, 1)

            def max_scores(b, g, qt, i, bank=None):
                n = UNITS * (NG * b + g) + HG * qt + i
                if qt == 0 and i == 0:
                    pe.wait_ge(stack_in[g], 32 * (b + 1))
                if bank is None:
                    pe.wait_ge(mx_red, n - 1)
                elif n >= 2 + HG:
                    pe.wait_ge(mx_red, n - 1 - HG)
                j, r = i // 2, 64 * (i % 2)
                pe.matmul(ps_m[:, i % 2, :] if bank is None else bank, qs[r:r + 64, g, j, qt * P:(qt + 1) * P], ks[r:r + 64, g, j, :],
                          start=True, stop=True).then_inc(mx_full, 1)

            def scores(b, g, kb, i, fresh):
                n = UNITS * b + TT * g + kb
                pair, at = (i - i % 2, i - i % 2 + 1), lambda h: ORDER.index(f"S{h}")
                if kb == 0 and i == 0:
                    pe.wait_ge(m_in, 64 * (NG * b + g + 1))
                opens = min(pair, key=at) == i
                if not fresh and opens:
                    pe.wait_ge(p_r, 2 * n - 1 + i // 2)
                j, r = i // 2, 64 * (i % 2)
                mm = pe.matmul(ps_s[:, i, :], ks[r:r + 64, g, j, kb * P:(kb + 1) * P], qs[r:r + 64, g, j, :],
                               start=True, stop=True)
                if not opens:
                    mm.then_inc(s_full, 1)

            def attend(b, u, fresh):
                g, kb = u // TT, u % TT
                pe.wait_ge(p_r, 2 * (UNITS * b + u + 1))
                if kb == 0:
                    pe.wait_ge(v_in[g], 16 * (b + 1))
                    if not fresh:
                        pe.wait_ge(o_r, NG * b + g)
                for i in range(HG):
                    mm = pe.matmul(ps_o[32 * i:32 * i + 32, :], v[:, g, kb, i, :], prob[:, u % 2, i, :],
                                   start=(kb == 0), stop=(kb == TT - 1), skip_group_check=True)
                mm.then_inc(av_done, 1)

            def job(b, op, no):
                if op[0:2] == "TR":
                    transposes(b, int(op[2]), no)
                elif op[0] in "QK":
                    project_qk(b, op, no)
                elif op[0] == "V":
                    project_v(b, int(op[1]), no)
                elif op[0:2] == "MT":
                    max_transpose(b, int(op[2]), no)
                elif op[0:2] == "FT":
                    job_wait(no)
                    pe.wait_ge(xhat_r, TT * (B + 1))
                    k = int(op[2])
                    for t in range(TT):
                        mm = pe.transpose(ps_j[:, t * P:(t + 1) * P], xhat_f[:, t, k * P:(k + 1) * P], ident[:])
                    mm.then_inc(job_full, 1)
                else:
                    project_o(b, int(op[2]), no)

            for k in range(KC):
                transposes(0, k, PRO.index(f"TR{k}"))
            pe.wait_ge(w_lo_r, 1)
            for bank, op in enumerate(("Q0", "K0", "Q1", "K1")):
                project_qk(0, op, PRO.index(op), bank)
            pe.wait_ge(w_lo_r, 3)
            for w in range(2):
                project_v(0, w, PRO.index(f"V{w}"))

            pe.wait_ge(table_w_in, 64)
            for k in range(TAB):
                rows = DT + (k == 2)
                mm = pe.matmul(ps_s[0:B, 2 + k // 2, D * (k % 2):D * (k % 2 + 1)], cond[0:rows, :], ada_w[0:rows, 4 + k, :],
                               start=(k != 1), stop=True, skip_group_check=True)
            mm.then_inc(tab_full, 1)
            for n in range(2 * UNITS):
                if n == HG:
                    pe.wait_ge(tab_r, 2)
                max_scores(0, n // UNITS, n % UNITS // HG, n % HG, max_bank(n))
                if n == UNITS - 1 + AHEAD:
                    max_transpose(0, 0, PRO.index("MT0"))
            pe.wait_ge(mx_red, 2 * UNITS - 2)

            def batch(b, first, last):
                jobs = jobs_of(first, last)
                for u in range(UNITS):
                    g, kb = u // TT, u % TT
                    for step in ORDER:
                        if step[0] == "S":
                            scores(b, g, kb, int(step[1]), first and u == 0)
                        elif step[0] == "M" and not (last and g >= 2):
                            max_scores(b + (g + 2) // NG, (g + 2) % NG, kb, int(step[1]))
                        elif step == "A" and u > 0:
                            attend(b, u - 1, first and u == 1)
                        elif step == "A" and not first:
                            attend(b - 1, UNITS - 1, False)
                        elif step == "J" and u in jobs:
                            op = jobs[u]
                            job(b if op in OWN else b - 1 if op in PREV else b + 1, op, job_no(b, first, last, op))

            batch(0, True, False)
            with pe.Fori(1, B - 1) as b:
                batch(b, False, False)
            batch(B - 1, False, True)
            attend(B - 1, UNITS - 1, False)


def ffn_phase(nc, dram, tensors):
    x_all, tab, coef, ident, ss2, rstd2 = (tensors[k] for k in ("x_all", "tab", "coef", "ident", "ss2", "rstd2"))
    wo_hi, wo_lo, o_raw, o_c, d_c, on_hi, on_lo, wo_t, raw, n_hi0, n_lo0 = (
        tensors[k] for k in ("wo_hi", "wo_lo", "o_raw", "o_c", "d_c", "on_hi", "on_lo", "wo_t", "raw", "n_hi", "n_lo"))
    HJ = JC // 2
    LB = B - 1
    with ExitStack() as ctx:
        def sb(name, shape, dt=F32):
            return ctx.enter_context(nc.sbuf_tensor(name, shape, dt))

        def sem(name):
            return ctx.enter_context(nc.semaphore(name))

        gh_raw = raw[:].rearrange("p (k i n) -> p k i n", k=KC, i=2)
        z = raw[:, 0:2 * TT * D].rearrange("p (u t n) -> p u t n", u=2, t=TT)
        f_t = raw[:, 2 * TT * D:3 * TT * D].rearrange("p (t n) -> p t n", t=TT)
        rows = raw[:, 3 * TT * D:].rearrange("p (i n) -> p i n", n=D)
        ow_raw = (sb("ow_raw", [P, JC // 2, D]), o_raw[:].rearrange("p g (j n) -> p (g j) n", n=D))
        gh_hi = sb("gh_hi", [P, KC, 2, HID], F32R)
        gh_lo = sb("gh_lo", [P, KC, 2, HID], F32R)
        ow_hi = sb("ow_hi", [P, JC, D], F32R)
        ow_lo = sb("ow_lo", [P, JC, D], F32R)
        xhat = sb("f_xhat", [P, TT, D])
        y_n = sb("f_y_n", [P, KC, T])
        n_hi = (n_hi0, sb("f_n_hi", [P, KC, T], F32R))
        n_lo = (n_lo0, sb("f_n_lo", [P, KC, T], F32R))
        sil = sb("sil", [P, 2, T])
        act_y = (o_c[:, 0, :], d_c[:, 0, :])
        a_hi = sb("a_hi", [P, 4, T], F32R)
        a_lo = sb("a_lo", [P, 4, T], F32R)
        t_bias = sb("t_bias", [P, D])
        t_junk = sb("t_junk", [P, D])
        st = sb("st", [P, TT, 6])
        mv = sb("mv", [P, TT, 2])
        sd = sb("sd", [P, TT])
        o_d = nc.dram_tensor("tail_scratch", (2, P, T), F32, kind="Internal").ap()
        ps_g = ctx.enter_context(nc.psum_tensor("ps_g", [P, 2, T], F32))
        ps_h = ctx.enter_context(nc.psum_tensor("ps_h", [P, 2, T], F32))
        ps_t = ctx.enter_context(nc.psum_tensor("ps_t", [P, KC, T], F32))
        ps_f = ctx.enter_context(nc.psum_tensor("ps_f", [P, TT, D], F32))

        ow_in = sem("ow_in"); rows_in = sem("rows_in")
        gh_hi_r = sem("gh_hi_r"); gh_lo_r = sem("gh_lo_r"); ow_hi_r = sem("ow_hi_r"); ow_lo_r = sem("ow_lo_r")
        ms2 = sem("f_ms2"); root2 = sem("f_root2"); rstd2_r = sem("f_rstd2_r"); rows_r = sem("rows_r")
        ow_w = sem("f_ow_w"); oc_in = sem("f_oc_in"); on_r = sem("f_on_r"); wo_full = sem("wo_full")
        wo_used = sem("wo_used"); x1_r = sem("f_x1_r"); sq2 = sem("f_sq2")
        xhat_r = sem("f_xhat_r"); tr_full = sem("tr_full"); y_r = sem("f_y_r"); n_r = sem("f_n_r")
        gh_full = sem("gh_full"); sil_r = sem("sil_r"); act_r = sem("act_r"); a_hi_r = sem("a_hi_r")
        a_lo_r = sem("a_lo_r"); out_used = sem("out_used")
        f_mul = sem("f_mul"); x2_r = sem("x2_r"); stat_r = sem("stat_r"); sd_r = sem("sd_r"); rs_r = sem("rs_r")
        bias_r = sem("bias_r"); x_pre = sem("x_pre"); shift_r = sem("shift_r"); z_r = sem("z_r"); stored = sem("stored")
        pool_waited = sem("f_pool_waited"); sp_waited = sem("f_sp_waited")

        block = ctx.enter_context(nc.Block())

        @block.sync
        def _(sp):
            ow_halves = dram["out_w"].rearrange("(h j p) n -> h p j n", h=2, p=P)
            sp.dma_start(ow_raw[0][:], ow_halves[0]).then_inc(ow_in, 16)
            sp.dma_start(o_d.rearrange("g p n -> p g n"), o_raw[:]).then_inc(ow_w, 16)
            sp.wait_ge(ow_w, 16)
            parts = o_d.rearrange("g (i k d) n -> k (g i) d n", i=HG, k=2)
            for k, dst in enumerate((o_c, d_c)):
                sp.dma_start(dst[:, 1, :], parts[k]).then_inc(oc_in, 16)
            sp.wait_ge(ow_in, 16)
            sp.dma_start(ow_raw[1], ow_halves[1]).then_inc(ow_in, 16)
            sp.wait_ge(gh_lo_r, JC)
            for i, name in ((0, "out_b"), (1, "l1_w"), (3, "l1_b")):
                sp.dma_start(rows[:, i, :], dram[name].partition_broadcast(P)).then_inc(rows_in, 16)

            def batch(b, par):
                sp.wait_ge(z_r, 2 * TT * (b + 1))
                sp.sem_inc(sp_waited, 1)
                sp.dma_start(dram["out"][bass.ds(b, 1)].rearrange("a p t n -> p (a t) n"), z[:, par]).then_inc(stored, 16)
                sp.wait_ge(stored, 16 * (b + 1))
                sp.sem_inc(sp_waited, 1)

            with sp.Fori(0, B // 2 - 1) as i:
                batch(2 * i, 0)
                batch(2 * i + 1, 1)
            batch(B - 2, 0)
            for w in range(2):
                sp.wait_ge(z_r, 2 * TT * B - 2 + 2 * w)
                sp.dma_start(dram["out"][B - 1][:, 2 * w:2 * w + 2, :], z[:, 1, 2 * w:2 * w + 2]).then_inc(stored, 16)
            sp.wait_ge(stored, 16 * (B + 1))

        @block.scalar
        def _(act):
            def gh_high(j):
                cols = slice(j * P, (j + 1) * P)
                act.activation(gh_hi[:, :, :, cols], gh_raw[:, :, :, cols], ACT.Copy).then_inc(gh_hi_r, 1)

            def ow_high(j):
                act.wait_ge(ow_in, 16 * (j // HJ + 1))
                act.activation(ow_hi[:, j, :], ow_raw[j // HJ][:, j % HJ, :], ACT.Copy).then_inc(ow_hi_r, 1)

            gh_high(0)
            gh_high(1)

            def y_copy(b):
                for k in range(KC):
                    act.wait_ge(tr_full, KC * (b - 1) + k + 1)
                    if not (isinstance(b, int) and b == 1):
                        act.wait_ge(n_r, 4 * (b - 1))
                    cf = coef[:, :, k:k + 1, bass.ds(b, 1)].rearrange("p i k b -> p i (k b)")
                    act.activation(y_n[:, k, :], ps_t[:, k, :], ACT.Identity, scale=cf[:, 2], bias=cf[:, 3])\
                       .then_inc(y_r, 1)

            def silu(n, j, fresh):
                act.wait_ge(gh_full, 2 * n + 1)
                if not fresh:
                    act.wait_ge(act_r, n - 1)
                act.activation(sil[:, j % 2, :], ps_g[:, j % 2, :], ACT.Silu).then_inc(sil_r, 1)

            def high(n, j, fresh):
                act.wait_ge(act_r, n + 1)
                if not fresh:
                    act.wait_ge(out_used, n - 3)
                act.activation(a_hi[:, j % 4, :], act_y[j % 2], ACT.Copy).then_inc(a_hi_r, 1)

            def squares(b, tiles):
                for t in tiles:
                    n = TT * (b - LB + 1) + t
                    if b == LB:
                        act.wait_ge(x1_r, t // 2 + 1)
                    if n > 0:
                        act.wait_ge(sq2, n)
                    act.activation(t_junk[:], x_all[:, b, t, :], ACT.Square, scale=1.0 / DH,
                                   accum_out=ss2[:, b, t:t + 1]).then_inc(sq2, 1)

            def deviation(b):
                act.wait_ge(stat_r, 9 * b + 9)
                act.activation(sd[:], sd[:], ACT.Sqrt).then_inc(sd_r, 1)

            def batch(b, first, last):
                for j in range(JC):
                    n = JC * b + j
                    silu(n, j, first and j < 2)
                    if j > 0:
                        high(n - 1, j - 1, first and j <= 4)
                    elif not first:
                        high(n - 1, JC - 1, False)
                    if first:
                        ow_high(j)
                        if j + 2 < JC:
                            gh_high(j + 2)
                    if j == 4 and not last:
                        y_copy(b + 1)
                    if first and j >= 6:
                        squares(LB - 1, (2 * j - 12, 2 * j - 11))
                    if isinstance(b, int) and b == 1 and j in (1, 2):
                        squares(LB, (2 * j - 2, 2 * j - 1))
                    if j == 5 and not first:
                        deviation(b - 1)
                        if isinstance(b, int) and b == 1:
                            act.wait_ge(ms2, 1)
                            act.activation(rstd2[:, RT:], rstd2[:, RT:], ACT.Sqrt).then_inc(root2, 1)

            batch(0, True, False)
            batch(1, False, False)
            with act.Fori(2, B - 1) as b:
                batch(b, False, False)
            batch(B - 1, False, True)
            high(JC * B - 1, JC - 1, False)
            deviation(B - 1)

        @block.vector
        def _(dve):
            def norm(b, fresh):
                if not fresh:
                    dve.wait_ge(tr_full, KC * (b - 1))
                for t in range(TT):
                    xs = x_all[:, bass.ds(b, 1), t, :].rearrange("p a n -> p (a n)")
                    dve.tensor_scalar(xhat[:, t, :], xs, rstd2[:, bass.ds(TT * b + t, 1)], None, ALU.mult)\
                       .then_inc(xhat_r, 1)

            def low_weights(j):
                cols = slice(j * P, (j + 1) * P)
                dve.wait_ge(gh_hi_r, j + 1)
                dve.tensor_tensor(gh_lo[:, :, :, cols], gh_raw[:, :, :, cols], gh_hi[:, :, :, cols].bitcast(F32),
                                  ALU.subtract).then_inc(gh_lo_r, 1)

            def ow_low(j):
                dve.wait_ge(ow_hi_r, j + 1)
                dve.tensor_tensor(ow_lo[:, j, :], ow_raw[j // HJ][:, j % HJ, :], ow_hi[:, j, :].bitcast(F32), ALU.subtract)\
                   .then_inc(ow_lo_r, 1)

            low_weights(0)
            low_weights(1)

            def split_n(b, par, fresh):
                for k in range(KC):
                    dve.wait_ge(y_r, KC * (b - 1) + k + 1)
                    if not fresh:
                        dve.wait_ge(gh_full, 2 * JC * (b - 1))
                    dve.tensor_copy(n_hi[par][:, k, :], y_n[:, k, :]).then_inc(n_r, 1)
                    dve.wait_ge(n_r, 4 * (b - 1) + 2 * k + 1)
                    dve.tensor_tensor(n_lo[par][:, k, :], y_n[:, k, :], n_hi[par][:, k, :].bitcast(F32), ALU.subtract)\
                       .then_inc(n_r, 1)

            def gate(n, j, fresh):
                dve.wait_ge(sil_r, n + 1)
                dve.wait_ge(gh_full, 2 * n + 2)
                if not fresh:
                    dve.wait_ge(a_lo_r, n - 1)
                dve.tensor_tensor(act_y[j % 2], ps_h[:, j % 2, :], sil[:, j % 2, :], ALU.mult).then_inc(act_r, 1)

            def low(n, j, fresh):
                dve.wait_ge(a_hi_r, n + 1)
                if not fresh:
                    dve.wait_ge(out_used, n - 3)
                dve.tensor_tensor(a_lo[:, j % 4, :], act_y[j % 2], a_hi[:, j % 4, :].bitcast(F32), ALU.subtract)\
                   .then_inc(a_lo_r, 1)

            def scale_half(b, w):
                dve.wait_ge(out_used, JC * (b + 1) if not (isinstance(b, int) and b == B - 1) else JC * B - 1 + w)
                al = tab[:, 1, bass.ds(b, 1), :].broadcast_to([P, 2, D])
                dve.tensor_tensor(f_t[:, 2 * w:2 * w + 2], ps_f[:, 2 * w:2 * w + 2], al, ALU.mult).then_inc(f_mul, 1)

            def scale_out(b, fresh):
                if not fresh:
                    dve.wait_ge(x2_r, 2 * b)
                for w in range(2):
                    scale_half(b, w)

            def x_tile(b, t):
                return x_all[:, bass.ds(b, 1), t, :].rearrange("p a n -> p (a n)")

            def new_x(b, w):
                dve.wait_ge(f_mul, 2 * b + w + 1)
                xs = x_all[:, bass.ds(b, 1), 2 * w:2 * w + 2, :].rearrange("p a t n -> p (a t) n")
                dve.tensor_tensor(xs, xs, f_t[:, 2 * w:2 * w + 2], ALU.add).then_inc(x2_r, 1)
                dve.wait_ge(x2_r, 2 * b + w + 1)
                for t in (2 * w, 2 * w + 1):
                    dve.bn_stats(st[:, t, :], x_tile(b, t)).then_inc(stat_r, 1)

            def stats(b):
                dve.wait_ge(x_pre, 2 * (b + 1))
                for w in range(2):
                    new_x(b, w)
                moments(b)

            def moments(b):
                for t in range(TT):
                    dve.wait_ge(stat_r, 9 * b + t + 1)
                    dve.bn_aggr(mv[:, t, :], st[:, t, :]).then_inc(stat_r, 1)
                dve.wait_ge(stat_r, 9 * b + 8)
                dve.tensor_scalar(sd[:], mv[:, :, 1], EPS_LN, None, ALU.add).then_inc(stat_r, 1)

            def centre(b, par, fresh):
                if not fresh:
                    dve.wait_ge(stored, 16 * (b - 1))
                for t in range(TT):
                    dve.scalar_tensor_tensor(out=z[:, par, t, :], in0=x_tile(b, t), scalar=mv[:, t, 0:1],
                                             in1=rows[:, 2, :], op0=ALU.subtract, op1=ALU.mult).then_inc(z_r, 1)

            def layer_norm(b, par):
                dve.wait_ge(sd_r, b + 1)
                dve.reciprocal(sd[:], sd[:]).then_inc(rs_r, 1)
                dve.wait_ge(rs_r, b + 1)
                if not (isinstance(b, int) and b > 0):
                    dve.wait_ge(shift_r, 3)
                shift = tab[:, 2, bass.ds(b, 1), :].rearrange("p a n -> p (a n)")
                for t in range(TT):
                    dve.wait_ge(z_r, 2 * TT * b + max(t + 1, TT))
                    dve.scalar_tensor_tensor(out=z[:, par, t, :], in0=z[:, par, t, :], scalar=sd[:, t:t + 1], in1=shift,
                                             op0=ALU.mult, op1=ALU.add).then_inc(z_r, 1)

            def attention_tail(j):
                for q in {1: (0, 1), 2: (2, 3)}.get(j, ()):
                    if q == 0:
                        dve.wait_ge(oc_in, 32)
                    part = d_c[:, 1, q * P:(q + 1) * P]
                    dve.reciprocal(part, part).then_inc(on_r, 1)
                if j == 3:
                    dve.wait_ge(on_r, 4)
                    dve.tensor_tensor(o_c[:, 1, :], o_c[:, 1, :], d_c[:, 1, :], ALU.mult).then_inc(on_r, 1)
                    dve.wait_ge(on_r, 5)
                    dve.tensor_copy(on_hi[:, 1, :], o_c[:, 1, :]).then_inc(on_r, 1)
                    dve.wait_ge(on_r, 6)
                    dve.tensor_tensor(on_lo[:, 1, :], o_c[:, 1, :], on_hi[:, 1, :].bitcast(F32), ALU.subtract)\
                       .then_inc(on_r, 1)
                if j in (6, 7):
                    w = j - 6
                    dve.wait_ge(wo_full, w + 1)
                    al = tab[:, 0, LB:LB + 1, :].broadcast_to([P, 2, D])
                    dve.tensor_tensor(wo_t[:, w], ps_t[:, w].rearrange("p (t n) -> p t n", t=2), al, ALU.mult)\
                       .then_inc(wo_used, 1)

            def first_pair():
                for b in (0, 1):
                    for j in range(JC):
                        n = JC * b + j
                        if j == 1 and b == 1:
                            dve.wait_ge(rows_in, 48)
                            dve.tensor_tensor(rows[:, 2, :], rows[:, 1, :], rows[:, 1, :], ALU.mult).then_inc(rows_r, 1)
                            dve.wait_ge(rows_r, 1)
                        if j == 2 and b == 1:
                            scale_out(0, True)
                        gate(n, j, n < 2)
                        if n > 0:
                            low(n - 1, (j - 1) % JC, n <= 4)
                        if j == 1:
                            norm(b + 1, b == 0)
                        if b == 0:
                            attention_tail(j)
                            ow_low(j)
                            if j + 2 < JC:
                                low_weights(j + 2)
                        if j == 4 and b == 1:
                            stats(0)
                            dve.wait_ge(sq2, 2 * TT)
                            dve.tensor_scalar(rstd2[:, RT:], ss2[:].rearrange("p b t -> p (b t)")[:, RT:], EPS_RMS,
                                              None, ALU.add).then_inc(ms2, 1)
                        if j == 5:
                            split_n(b + 1, 1 - b, b == 0)
                        if j == 5 and b == 1:
                            centre(0, 0, True)
                        if j == 6 and b == 1:
                            layer_norm(0, 0)
                            dve.wait_ge(root2, 1)
                            dve.reciprocal(rstd2[:, RT:], rstd2[:, RT:]).then_inc(rstd2_r, 1)
                            dve.wait_ge(rstd2_r, 1)

            def next_batch(b, par, fresh, last):
                for j in range(JC):
                    n = JC * b + j
                    if j == 2:
                        scale_out(b - 1, False)
                    gate(n, j, False)
                    low(n - 1, (j - 1) % JC, False)
                    if j == 1 and not last:
                        norm(b + 1, False)
                    if j == 4:
                        stats(b - 1)
                    if j == 5 and not last:
                        split_n(b + 1, 1 - par, False)
                    if j == 5:
                        centre(b - 1, 1 - par, fresh)
                    if j == 6:
                        layer_norm(b - 1, 1 - par)

            first_pair()
            with dve.Fori(1, 2) as i:
                next_batch(2 * i, 0, True, False)
                next_batch(2 * i + 1, 1, False, False)
            with dve.Fori(2, B // 2 - 1) as i:
                next_batch(2 * i, 0, False, False)
                next_batch(2 * i + 1, 1, False, False)
            next_batch(B - 2, 0, False, False)
            next_batch(B - 1, 1, False, True)
            low(JC * B - 1, JC - 1, False)
            dve.wait_ge(x2_r, 2 * (B - 1))
            dve.wait_ge(x_pre, 2 * B)
            for w in range(2):
                scale_half(B - 1, w)
                new_x(B - 1, w)
            moments(B - 1)
            centre(B - 1, 1, False)
            layer_norm(B - 1, 1)

        @block.gpsimd
        def _(pool):
            def add_bias(b):
                if not (isinstance(b, int) and b == 0):
                    pool.wait_ge(xhat_r, TT * b)
                    pool.sem_inc(pool_waited, 1)
                al = tab[:, 1, bass.ds(b, 1), :].rearrange("p a n -> p (a n)")
                pool.tensor_tensor(t_bias[:], al, rows[:, 0, :], ALU.mult).then_inc(bias_r, 1)
                pool.wait_ge(bias_r, b + 1)
                pool.sem_inc(pool_waited, 1)
                for w in range(2):
                    xs = x_all[:, bass.ds(b, 1), 2 * w:2 * w + 2, :].rearrange("p a t n -> p (a t) n")
                    pool.tensor_tensor(xs, xs, t_bias[:].unsqueeze(1).broadcast_to([P, 2, D]), ALU.add).then_inc(x_pre, 1)
                pool.wait_ge(x_pre, 2 * (b + 1))
                pool.sem_inc(pool_waited, 1)

            for w in range(2):
                pool.wait_ge(wo_used, w + 1)
                xs = x_all[:, LB, 2 * w:2 * w + 2, :]
                pool.tensor_tensor(xs, xs, wo_t[:, w], ALU.add).then_inc(x1_r, 1)
            pool.wait_ge(rows_in, 48)
            add_bias(0)
            shift = tab[:, 2]
            wrow, brow = (rows[:, i:i + 1, :].broadcast_to([P, B, D]) for i in (1, 3))
            for n, (row, op) in enumerate(((brow, ALU.add), (wrow, ALU.mult), (brow, ALU.add))):
                pool.tensor_tensor(shift, shift, row, op).then_inc(shift_r, 1)
                pool.wait_ge(shift_r, n + 1)

            with pool.Fori(1, B) as b:
                add_bias(b)

        @block.tensor
        def _(pe):
            GH, N, OW, A = (gh_hi, gh_lo), (n_hi, n_lo), (ow_hi, ow_lo), (a_hi, a_lo)
            PARTS = ((0, 0), (1, 0), (0, 1))

            def transposes(b, fresh):
                pe.wait_ge(xhat_r, TT * b)
                if isinstance(b, int) and b == 2:
                    pe.wait_ge(wo_used, 2)
                for k in range(KC):
                    if not fresh:
                        pe.wait_ge(y_r, KC * (b - 2) + k + 1)
                    for t in range(TT):
                        mm = pe.transpose(ps_t[:, k, t * P:(t + 1) * P], xhat[:, t, k * P:(k + 1) * P], ident[:])
                    mm.then_inc(tr_full, 1)

            def gate_hidden(n, par, j, b, fresh):
                if j == 0 and not fresh:
                    pe.wait_ge(n_r, 4 * b)
                for i, (ps, used) in enumerate(((ps_g, sil_r), (ps_h, act_r))):
                    if not fresh:
                        pe.wait_ge(used, n - 1)
                    m = 0
                    for k in range(KC):
                        for a, c in PARTS:
                            mm = pe.matmul(ps[:, j % 2, :], GH[a][:, k, i, j * P:(j + 1) * P], N[c][par][:, k, :],
                                           start=(m == 0), stop=(m == 5))
                            m += 1
                    mm.then_inc(gh_full, 1)

            def project_out(n, j, b, fresh):
                pe.wait_ge(a_hi_r, n + 1)
                pe.wait_ge(a_lo_r, n + 1)
                if j == 0 and not fresh:
                    pe.wait_ge(f_mul, 2 * b)
                out_products(j, range(TT)).then_inc(out_used, 1)

            def out_products(j, tiles):
                for t in tiles:
                    for m, (a, c) in enumerate(PARTS):
                        mm = pe.matmul(ps_f[:, t, :], A[a][:, j % 4, t * P:(t + 1) * P], OW[c][:, j, :],
                                       start=(j == 0 and m == 0 and t % 2 == 0), stop=(j == JC - 1 and m == 2),
                                       skip_group_check=True)
                return mm

            def project_o(w):
                pe.wait_ge(on_r, 7)
                pe.wait_ge(y_r, KC)
                for t in (2 * w, 2 * w + 1):
                    m = 0
                    for k in range(KC):
                        for a, c in PARTS:
                            mm = pe.matmul(ps_t[:, w, D * (t % 2):D * (t % 2 + 1)],
                                           (on_hi, on_lo)[a][:, k, t * P:(t + 1) * P], (wo_hi, wo_lo)[c][:, k, :],
                                           start=(m == 0), stop=(m == 5))
                            m += 1
                mm.then_inc(wo_full, 1)

            LAG = 2

            def batch(b, par, first, last):
                for j in range(JC):
                    n = JC * b + j
                    if first:
                        pe.wait_ge(gh_lo_r, j + 1)
                    gate_hidden(n, par, j, b, first and j < 2)
                    if j >= LAG:
                        if first:
                            pe.wait_ge(ow_lo_r, j - LAG + 1)
                        project_out(n - LAG, j - LAG, b, first)
                    elif not first:
                        project_out(n - LAG, j - LAG + JC, b - 1, False)
                    if j == 3 and not last:
                        transposes(b + 1, first)
                    if first and j in (5, 6):
                        project_o(j - 5)

            batch(0, 0, True, False)
            batch(1, 1, False, False)
            with pe.Fori(1, B // 2 - 1) as i:
                batch(2 * i, 0, False, False)
                batch(2 * i + 1, 1, False, False)
            batch(B - 2, 0, False, False)
            batch(B - 1, 1, False, True)
            pe.wait_ge(a_hi_r, JC * B)
            pe.wait_ge(a_lo_r, JC * B)
            for w in range(2):
                for j in (JC - 2, JC - 1):
                    mm = out_products(j, (2 * w, 2 * w + 1))
                mm.then_inc(out_used, 1)


def build(nc, dram):
    with ExitStack() as ctx:
        def sb(name, shape, dt=F32):
            return ctx.enter_context(nc.sbuf_tensor(name, shape, dt))

        tensors = {
            "x_all": sb("x_all", [P, B, TT, D]),
            "tab": sb("tab", [P, TAB, B, D]),
            "coef": sb("coef", [P, 4, KC, B]),
            "ident": sb("ident", [P, P]),
            "ss2": sb("ss2", [P, B, TT]),
            "rstd2": sb("rstd2", [P, B * TT]),
            "wo_hi": sb("wo_hi", [P, KC, D], F32R),
            "wo_lo": sb("wo_lo", [P, KC, D], F32R),
            "o_raw": sb("o_raw", [P, 2, T]),
            "o_c": sb("o_c", [P, 2, T]),
            "d_c": sb("d_c", [P, 2, T]),
            "on_hi": sb("on_hi", [P, 2, T], F32R),
            "on_lo": sb("on_lo", [P, 2, T], F32R),
            "wo_t": sb("wo_t", [P, 2, 2, D]),
            "n_hi": sb("n_hi", [P, KC, T], F32R),
            "n_lo": sb("n_lo", [P, KC, T], F32R),
            "raw": sb("raw", [P, KC * 2 * HID]),
        }
        attention_phase(nc, dram, tensors)
        ffn_phase(nc, dram, tensors)


_TRANSPOSED = {
    "gamma1": "L0_cond_attn_gamma_w", "beta1": "L0_cond_attn_beta_w", "gamma2": "L0_cond_ffn_gamma_w",
    "beta2": "L0_cond_ffn_beta_w", "alpha1": "L0_cond_attn_alpha_w", "alpha2": "L0_cond_ffn_alpha_w",
    "lin_w": "L1_cond_lin_w", "wq": "L0_cond_W_q", "wk": "L0_cond_W_k", "wv": "L0_cond_W_v", "wo": "L0_cond_W_o",
    "gate": "L0_cond_gate_w", "hidden": "L0_cond_hidden_w", "out_w": "L0_cond_out_w", "cond": "cond_256",
}
_PLAIN = {"lin_b": "L1_cond_lin_b", "l1_w": "L1_cond_weight", "l1_b": "L1_cond_bias", "out_b": "L0_cond_out_b"}


def kernel(**inputs):
    import numpy as _np
    import concourse.bacc as _bacc
    from concourse.bass_utils import run_bass_kernel_spmd as _run

    nc = _bacc.Bacc("TRN2", target_bir_lowering=False, num_devices=1)
    arrays = {"in_x": _np.ascontiguousarray(_np.asarray(inputs["x"])).reshape(B, P, TT, D)}
    for name, key in _TRANSPOSED.items():
        arrays["in_" + name] = _np.ascontiguousarray(_np.asarray(inputs[key]).T)
    for name, key in _PLAIN.items():
        arrays["in_" + name] = _np.ascontiguousarray(_np.asarray(inputs[key]))
    dram = {k[3:]: nc.dram_tensor(k, a.shape, mybir.dt.from_np(a.dtype), kind="ExternalInput").ap()
            for k, a in arrays.items()}
    dram["out"] = nc.dram_tensor("out_y", (B, P, TT, D), F32, kind="ExternalOutput").ap()
    build(nc, dram)
    r = _run(nc, [arrays], core_ids=[0])
    return r.results[0]["out_y"].reshape(B, P * TT, D)
```
